# Optimizing a Trainium2 kernel written in Bass

```python
import numpy as np
import jax
import jax.numpy as jnp

def _softmax(x, axis=-1):
    return jax.nn.softmax(x, axis=axis)

def _gelu(x):
    return jax.nn.gelu(x, approximate=True)

def _silu(x):
    return jax.nn.silu(x)

def _sigmoid(x):
    return jax.nn.sigmoid(x)

def _layernorm(x, axis=-1, eps=1e-05):
    m = jnp.mean(x, axis=axis, keepdims=True)
    v = jnp.var(x, axis=axis, keepdims=True)
    return (x - m) / jnp.sqrt(v + eps)

def _scatter_add(tgt, idx, src, axis=0):
    return tgt.at[idx].add(src)

def _segment_sum(src, seg, n):
    return jax.ops.segment_sum(src, seg, n)
kernel_name = 'mk_gnn_resnorm_d4_gnn_r8_16766a'

def setup_inputs(seed: int=0):
    np.random.seed(seed)
    _w = jnp.asarray

    def _rec_inputs():
        import jax
        import jax.numpy as jnp
        _gk = jax.random.key(seed)
        x = -0.000202 + 1 * jax.random.normal(jax.random.fold_in(_gk, 1), (12500, 64), jnp.float32)
        _s = jax.random.randint(jax.random.fold_in(_gk, 2), (100000,), 0, 12500, jnp.int32)
        _d = jax.random.randint(jax.random.fold_in(_gk, 3), (100000,), 0, 12500, jnp.int32)
        _loop = jnp.arange(12500, dtype=jnp.int32)
        src = jnp.concatenate([_s, _d, _loop])
        dst = jnp.concatenate([_d, _s, _loop])
        _o = jnp.argsort(dst, stable=True)
        src = src[_o]
        dst = dst[_o]
        edge_attr_64 = -4.21973e-05 + 0.999841 * jax.random.normal(jax.random.fold_in(_gk, 12), (212500, 64), jnp.float32)
        return (x, src, dst, edge_attr_64)
    x, src, dst, edge_attr_64 = _rec_inputs()

    def _L0_gnn_setup():
        import jax, jax.numpy as jnp
        import numpy as np
        N_NODES = 12500
        N_EDGES = 200000
        D = 64
        BN_EPS = 1e-05
        L2_EPS = 1e-12
        key = jax.random.key(seed)
        ks = jax.random.split(key, 6)
        h = jax.random.normal(ks[0], (N_NODES, D), dtype=jnp.float32)
        W = jax.random.normal(ks[1], (2 * D, D), dtype=jnp.float32) * (1.0 / np.sqrt(2 * D))
        b = jax.random.normal(ks[2], (D,), dtype=jnp.float32) * 0.01
        gamma = jnp.ones((D,), dtype=jnp.float32)
        beta = jnp.zeros((D,), dtype=jnp.float32)
        src = jax.random.randint(ks[3], (N_EDGES,), 0, N_NODES, dtype=jnp.int64 if jax.config.jax_enable_x64 else jnp.int32)
        dst = jax.random.randint(ks[4], (N_EDGES,), 0, N_NODES, dtype=jnp.int64 if jax.config.jax_enable_x64 else jnp.int32)
        return {'h': h, 'W': W, 'b': b, 'gamma': gamma, 'beta': beta, 'src': src, 'dst': dst}
    _L0_gnn_all = _L0_gnn_setup()
    _L0_gnn_in = {k: v for k, v in _L0_gnn_all.items() if k in ('W', 'b', 'gamma', 'beta')}
    del _L0_gnn_all

    def _L1_gnn_setup():
        import jax, jax.numpy as jnp
        import numpy as np
        N = 6250
        E = 100000
        D_IN = 64
        D_HID = 64
        D_OUT = 64

        def _sage_conv(x, src, dst, w_l, b_l, w_r, num_nodes):
            msg = x[src]
            agg = jax.ops.segment_sum(msg, dst, num_segments=num_nodes)
            cnt = jax.ops.segment_sum(jnp.ones((src.shape[0],), x.dtype), dst, num_segments=num_nodes)
            mean = agg / jnp.maximum(cnt, 1.0)[:, None]
            return mean @ w_l.T + b_l + x @ w_r.T
        key = jax.random.key(seed)
        ks = jax.random.split(key, 10)
        s = 1.0 / np.sqrt(D_IN)
        inp = {'x': jax.random.normal(ks[0], (N, D_IN), dtype=jnp.float32), 'edge_index': jax.random.randint(ks[1], (2, E), 0, N, dtype=jnp.int64), 'w1_l': jax.random.uniform(ks[2], (D_HID, D_IN), jnp.float32, -s, s), 'b1': jnp.zeros((D_HID,), jnp.float32), 'w1_r': jax.random.uniform(ks[3], (D_HID, D_IN), jnp.float32, -s, s), 'w2_l': jax.random.uniform(ks[4], (D_HID, D_HID), jnp.float32, -s, s), 'b2': jnp.zeros((D_HID,), jnp.float32), 'w2_r': jax.random.uniform(ks[5], (D_HID, D_HID), jnp.float32, -s, s), 'w_lin': jax.random.uniform(ks[6], (D_OUT, D_HID), jnp.float32, -s, s), 'b_lin': jnp.zeros((D_OUT,), jnp.float32)}
        return inp
    _L1_gnn_all = _L1_gnn_setup()
    _L1_gnn_in = {k: v for k, v in _L1_gnn_all.items() if k in ('w1_l', 'b1', 'w1_r', 'w2_l', 'b2', 'w2_r', 'w_lin', 'b_lin')}
    del _L1_gnn_all

    def _L2_gnn_setup():
        import jax, jax.numpy as jnp
        import numpy as np
        N = 6250
        E = 150000
        NODE_DIM = 64
        EDGE_DIM = 64
        key = jax.random.key(seed)
        ks = jax.random.split(key, 10)
        h = jax.random.normal(ks[0], (N, NODE_DIM), dtype=jnp.float32)
        e = jax.random.normal(ks[1], (E, EDGE_DIM), dtype=jnp.float32)
        edge_index = jax.random.randint(ks[2], (2, E), 0, N, dtype=jnp.int64)
        s1 = 1.0 / np.sqrt(NODE_DIM + EDGE_DIM)
        W1 = jax.random.uniform(ks[3], (NODE_DIM + EDGE_DIM, NODE_DIM), jnp.float32, -s1, s1)
        b1 = jax.random.uniform(ks[4], (NODE_DIM,), jnp.float32, -s1, s1)
        s2 = 1.0 / np.sqrt(NODE_DIM)
        W2 = jax.random.uniform(ks[5], (NODE_DIM, NODE_DIM), jnp.float32, -s2, s2)
        b2 = jax.random.uniform(ks[6], (NODE_DIM,), jnp.float32, -s2, s2)
        s3 = 1.0 / np.sqrt(2 * NODE_DIM)
        W3 = jax.random.uniform(ks[7], (2 * NODE_DIM, NODE_DIM), jnp.float32, -s3, s3)
        b3 = jax.random.uniform(ks[8], (NODE_DIM,), jnp.float32, -s3, s3)
        return {'h': h, 'e': e, 'W1': W1, 'b1': b1, 'W2': W2, 'b2': b2, 'W3': W3, 'b3': b3, 'edge_index': edge_index}
    _L2_gnn_all = _L2_gnn_setup()
    _L2_gnn_in = {k: v for k, v in _L2_gnn_all.items() if k in ('W1', 'b1', 'W2', 'b2', 'W3', 'b3')}
    del _L2_gnn_all

    def _L3_gnn_setup():
        import jax, jax.numpy as jnp
        import numpy as np
        N_NODES = 12500
        IN_FEATS = 64
        OUT_FEATS = 64

        def _mean_aggregate(feat, senders, receivers, num_nodes):
            summed = jax.ops.segment_sum(feat[senders], receivers, num_segments=num_nodes)
            deg = jax.ops.segment_sum(jnp.ones((senders.shape[0],), feat.dtype), receivers, num_segments=num_nodes)
            return summed / jnp.maximum(deg, 1.0)[:, None]
        key = jax.random.key(seed)
        k1, k2, k3, k4 = jax.random.split(key, 4)
        feat = jax.random.normal(k1, (N_NODES, IN_FEATS), dtype=jnp.float32)
        src = jax.random.randint(k2, (125000,), 0, N_NODES)
        dst = jax.random.randint(k3, (125000,), 0, N_NODES)
        W = jax.random.normal(k4, (OUT_FEATS, 2 * IN_FEATS), dtype=jnp.float32) / np.sqrt(2 * IN_FEATS)
        return {'feat': feat, 'src': src, 'dst': dst, 'W': W}
    _L3_gnn_all = _L3_gnn_setup()
    _L3_gnn_in = {k: v for k, v in _L3_gnn_all.items() if k in ('W',)}
    del _L3_gnn_all
    return {'x': x, 'src': src, 'dst': dst, 'edge_attr_64': edge_attr_64, 'L0_gnn_W': _L0_gnn_in['W'], 'L0_gnn_b': _L0_gnn_in['b'], 'L0_gnn_gamma': _L0_gnn_in['gamma'], 'L0_gnn_beta': _L0_gnn_in['beta'], 'L1_gnn_w1_l': _L1_gnn_in['w1_l'], 'L1_gnn_b1': _L1_gnn_in['b1'], 'L1_gnn_w1_r': _L1_gnn_in['w1_r'], 'L1_gnn_w2_l': _L1_gnn_in['w2_l'], 'L1_gnn_b2': _L1_gnn_in['b2'], 'L1_gnn_w2_r': _L1_gnn_in['w2_r'], 'L1_gnn_w_lin': _L1_gnn_in['w_lin'], 'L1_gnn_b_lin': _L1_gnn_in['b_lin'], 'L2_gnn_W1': _L2_gnn_in['W1'], 'L2_gnn_b1': _L2_gnn_in['b1'], 'L2_gnn_W2': _L2_gnn_in['W2'], 'L2_gnn_b2': _L2_gnn_in['b2'], 'L2_gnn_W3': _L2_gnn_in['W3'], 'L2_gnn_b3': _L2_gnn_in['b3'], 'L3_gnn_W': _L3_gnn_in['W']}

def reference(x, src, dst, edge_attr_64, L0_gnn_W, L0_gnn_b, L0_gnn_gamma, L0_gnn_beta, L1_gnn_w1_l, L1_gnn_b1, L1_gnn_w1_r, L1_gnn_w2_l, L1_gnn_b2, L1_gnn_w2_r, L1_gnn_w_lin, L1_gnn_b_lin, L2_gnn_W1, L2_gnn_b1, L2_gnn_W2, L2_gnn_b2, L2_gnn_W3, L2_gnn_b3, L3_gnn_W):
    import jax
    import jax.numpy as jnp

    def _L0_gnn_ref(h, W, b, gamma, beta, src, dst):
        import jax, jax.numpy as jnp
        import numpy as np
        N_NODES = 12500
        N_EDGES = 200000
        D = 64
        BN_EPS = 1e-05
        L2_EPS = 1e-12
        h_in = h
        m = h[src]
        c_sum = jax.ops.segment_sum(m, dst, num_segments=N_NODES)
        deg = jax.ops.segment_sum(jnp.ones((m.shape[0],), h.dtype), dst, num_segments=N_NODES)
        c = c_sum / jnp.maximum(deg, 1.0)[:, None]
        bundle = jnp.concatenate([h, c], axis=1) @ W + b
        norm = jnp.sqrt(jnp.sum(bundle * bundle, axis=1, keepdims=True))
        bundle = bundle / jnp.maximum(norm, L2_EPS)
        hn = jax.nn.relu(bundle)
        mu = jnp.mean(hn, axis=0)
        var = jnp.var(hn, axis=0)
        out = gamma * (hn - mu) * jax.lax.rsqrt(var + BN_EPS) + beta
        return h_in + out

    def _L1_gnn_ref(x, edge_index, w1_l, b1, w1_r, w2_l, b2, w2_r, w_lin, b_lin):
        import jax, jax.numpy as jnp
        import numpy as np
        N = 6250
        E = 100000
        D_IN = 64
        D_HID = 64
        D_OUT = 64

        def _sage_conv(x, src, dst, w_l, b_l, w_r, num_nodes):
            msg = x[src]
            agg = jax.ops.segment_sum(msg, dst, num_segments=num_nodes)
            cnt = jax.ops.segment_sum(jnp.ones((src.shape[0],), x.dtype), dst, num_segments=num_nodes)
            mean = agg / jnp.maximum(cnt, 1.0)[:, None]
            return mean @ w_l.T + b_l + x @ w_r.T
        src, dst = (edge_index[0], edge_index[1])
        n = x.shape[0]
        h = jax.nn.relu(_sage_conv(x, src, dst, w1_l, b1, w1_r, n))
        h = jax.nn.relu(_sage_conv(h, src, dst, w2_l, b2, w2_r, n))
        return h @ w_lin.T + b_lin

    def _L2_gnn_ref(h, e, W1, b1, W2, b2, W3, b3, edge_index):
        import jax, jax.numpy as jnp
        import numpy as np
        N = 6250
        E = 150000
        NODE_DIM = 64
        EDGE_DIM = 64
        src, dst = (edge_index[0], edge_index[1])
        msg_input = jnp.concatenate([h[src], e], axis=-1)
        hidden = jax.nn.relu(msg_input @ W1 + b1)
        messages = hidden @ W2 + b2
        agg = jax.ops.segment_sum(messages, dst, num_segments=h.shape[0])
        h_new = jax.nn.relu(jnp.concatenate([h, agg], axis=-1) @ W3 + b3)
        return h_new

    def _L3_gnn_ref(feat, src, dst, W):
        import jax, jax.numpy as jnp
        import numpy as np
        N_NODES = 12500
        IN_FEATS = 64
        OUT_FEATS = 64

        def _mean_aggregate(feat, senders, receivers, num_nodes):
            summed = jax.ops.segment_sum(feat[senders], receivers, num_segments=num_nodes)
            deg = jax.ops.segment_sum(jnp.ones((senders.shape[0],), feat.dtype), receivers, num_segments=num_nodes)
            return summed / jnp.maximum(deg, 1.0)[:, None]
        n = feat.shape[0]
        fwd_neigh = _mean_aggregate(feat, src, dst, n)
        bwd_neigh = _mean_aggregate(feat, dst, src, n)
        h = jnp.concatenate((fwd_neigh, bwd_neigh), axis=1)
        out = jnp.einsum('nd,od->no', h, W)
        return jax.nn.relu(out)
    edge_index = jnp.stack([src, dst])
    x = _layernorm(x + _L0_gnn_ref(x, L0_gnn_W, L0_gnn_b, L0_gnn_gamma, L0_gnn_beta, src, dst), axis=-1)
    x = _layernorm(x + _L1_gnn_ref(x, edge_index, L1_gnn_w1_l, L1_gnn_b1, L1_gnn_w1_r, L1_gnn_w2_l, L1_gnn_b2, L1_gnn_w2_r, L1_gnn_w_lin, L1_gnn_b_lin), axis=-1)
    x = _layernorm(x + _L2_gnn_ref(x, edge_attr_64, L2_gnn_W1, L2_gnn_b1, L2_gnn_W2, L2_gnn_b2, L2_gnn_W3, L2_gnn_b3, edge_index), axis=-1)
    x = _layernorm(x + _L3_gnn_ref(x, src, dst, L3_gnn_W), axis=-1)
    return x

_drawn_inputs = setup_inputs


def setup_inputs(seed=0):
    import zlib

    import numpy as np

    out = dict(_drawn_inputs(seed))
    spreads = {'L0_gnn_gamma': (1.0, 0.2),
     'L0_gnn_beta': (0.0, 0.1),
     'L1_gnn_b1': (0.0, 0.419),
     'L1_gnn_b2': (0.0, 0.1),
     'L1_gnn_b_lin': (0.0, 0.1)}
    factors = {'L0_gnn_b': 8.0, 'L1_gnn_w1_l': 2.766}
    for name, (base, spread) in spreads.items():
        noise = np.random.default_rng([zlib.crc32(name.encode()), seed]).standard_normal(out[name].shape)
        drawn = base * np.exp(spread * noise) if base else spread * noise
        out[name] = jnp.asarray(drawn.astype(out[name].dtype))
    for name, factor in factors.items():
        out[name] = (out[name] * factor).astype(out[name].dtype)
    return out
```

```python
from contextlib import ExitStack, contextmanager

import numpy as np

import concourse.bass as bass
from concourse import mybir

ALU = mybir.AluOpType
ACT = mybir.ActivationFunctionType
AX = mybir.AxisListType
F32 = mybir.dt.float32
BF16 = mybir.dt.bfloat16
I32 = mybir.dt.int32

P = 128
D = 64
N = 12500
NT = -(-N // P)
NP = NT * P
LAST = N - (NT - 1) * P
CT = 7
NCH = NT // CT
CW = CT * D
CF = CT * P
E = 212500
GROUP = 8
NG = -(-E // (P * GROUP))
EP = NG * GROUP * P
WINDOW = 128
RING = 4
ITERS = NG // RING
COPIES = 4
NS = NP + P
BN_EPS = 1e-5
LN_EPS = 1e-5
L2_EPS = 1e-12
assert NT % CT == 0 and NCH % 2 == 0 and NG % RING == 0 and CW <= 512

MATS = ["W0_self", "W0_agg", "W1_agg", "W1_self", "W2_agg", "W2_self", "Wlin", "We_node", "We_edge",
        "We_out", "Wn_self", "Wn_agg", "W3_fwd", "W3_bwd"]
ROWS = ["b0", "b1", "b2", "blin", "be", "be2", "bn", "gamma", "beta"]


class Kit:
    pass


def alloc(nc, ctx, ins):
    k = Kit()
    k.ins = ins

    def sb(name, shape, dt=F32):
        return ctx.enter_context(nc.sbuf_tensor(name, shape, dt))

    k.acc = sb("acc", [D, NP + WINDOW])
    k.x = sb("x_nm", [P, NT * D])
    k.h = sb("h_nm", [P, NT * D])
    k.y = sb("y_nm", [P, NT * D])
    k.w = sb("work_nm", [P, NT * D])
    k.gath = [sb(f"gath{b}", [P, GROUP, D]) for b in range(RING)]
    k.oneh = [sb(f"oneh{b}", [P, GROUP, WINDOW]) for b in range(2)]
    k.idx = [sb(f"idx{b}", [P, 2 * GROUP], I32) for b in range(RING)]
    k.first = [sb(f"first{b}", [P, 1], I32) for b in range(RING)]
    k.local = [sb(f"local{b}", [P, GROUP]) for b in range(RING)]
    k.hilo = [sb(f"hilo{b}", [P, 4, GROUP]) for b in range(2)]
    k.hilo_i = [sb(f"hilo_i{b}", [P, 4, GROUP], I32) for b in range(2)]
    k.xT = [sb(f"xT{b}", [D, CF]) for b in range(2)]
    k.mats = sb("mats", [P, len(MATS) * D])
    k.rows = sb("rows", [1, len(ROWS) * D])
    k.gamma = sb("gamma", [P, D])
    k.beta = sb("beta", [P, D])
    k.be2col = sb("be2col", [D, 1])
    k.be2w = sb("be2w", [P, D])
    k.iota = sb("iota", [P, P])
    k.ident = sb("ident", [P, P])
    k.lower = sb("lower", [P, P], BF16)
    k.ones = sb("ones", [P, P])
    k.mask = sb("mask", [P, 1])
    k.spare = sb("spare", [P, 1])
    k.flag = sb("flag", [1, 1], I32)
    k.deg = {s: sb(f"deg_{s}", [P, NT]) for s in ("src", "dst")}
    k.rdeg = {s: sb(f"rdeg_{s}", [P, NT]) for s in ("src", "dst")}
    k.small = [sb(f"small{j}", [P, P]) for j in range(3)]

    k.tab = {n: nc.dram_tensor(f"table_{n}", [NS, D], F32).ap() for n in ("x1", "h1", "pre", "x3", "t3")}
    k.part = [nc.dram_tensor(f"partial{c}", [NS, D], F32).ap() for c in range(COPIES)]
    return k


def mat(k, name, part=0):
    c = MATS.index(name) * D
    return k.mats[part:part + D, c:c + D]


def bias_row(k, name):
    c = ROWS.index(name) * D
    return k.rows[0:1, c:c + D].unsqueeze(1).to_broadcast([1, CT, D])


def nm3(t):
    return t[:, :].rearrange("p (t f) -> p t f", f=D)


def over_features(t, n=NT):
    return t.unsqueeze(2).to_broadcast([P, n, D])


def over_tiles(t, n=NT):
    return t.unsqueeze(1).to_broadcast([P, n, D])


def dram_nm(t, rows=NP):
    return t[0:rows, :].rearrange("(t p) f -> p t f", p=P)


def psum(nc, ctx, name, cols=512, parts=P):
    return ctx.enter_context(nc.psum_tensor(name, [parts, cols], F32, allow_name_mangling=True))


@contextmanager
def stage(nc):
    held = []

    def sem(name):
        held.append(nc.alloc_semaphore(f"{name}_{nc.next_id()}"))
        return held[-1]

    with ExitStack() as ctx:
        yield ctx, sem
    nc.gpsimd.dma_reset()
    for s in held:
        nc.gpsimd.sem_clear(s)
    nc.all_engine_barrier()
    for s in held:
        nc.release_semaphore(s)



def setup_stage(nc, k):
    ins = k.ins
    with stage(nc) as (ctx, sem):
        ps = psum(nc, ctx, "setup_ps")
        loaded, consts, step, zeroed, stored, summed, folded = (
            sem("setup_loaded"), sem("setup_consts"), sem("setup_step"), sem("setup_zeroed"),
            sem("setup_stored"), sem("setup_summed"), sem("setup_folded"))
        dst_all = k.h[:, 0:NG * GROUP].bitcast(I32)
        first_all = k.h[:, NG * GROUP:NG * GROUP + NG].bitcast(I32)
        dist = k.y[:, 0:NG * GROUP].rearrange("p (g t) -> p g t", t=GROUP)
        block = ctx.enter_context(nc.Block())
        n_loads = 9

        @block.sync
        def _(sp):
            sp.dma_start(dst_all, ins["dst_all"]).then_inc(loaded, 16)
            sp.dma_start(first_all, ins["first"].to_broadcast([P, NG])).then_inc(loaded, 16)
            sp.dma_start(k.mats[0:D, :], ins["mats"]).then_inc(loaded, 16)
            sp.dma_start(k.mats[D:P, :], ins["mats"]).then_inc(loaded, 16)
            sp.dma_start(k.rows[:, :], ins["rows"].rearrange("o r f -> o (r f)")).then_inc(loaded, 16)
            for name, tile in (("gamma", k.gamma), ("beta", k.beta)):
                r = ROWS.index(name)
                sp.dma_start(tile[:, :], ins["rows"][0, r:r + 1, :].to_broadcast([P, D])).then_inc(loaded, 16)
            sp.dma_start(k.be2col[:, :], ins["be2_col"]).then_inc(loaded, 16)
            sp.dma_start(nm3(k.x), dram_nm(ins["x"])).then_inc(loaded, 16)
            sp.wait_ge(zeroed, 1)
            for c in range(COPIES):
                sp.dma_start(dram_nm(k.part[c], NS), nm3(k.w)[:, 0:1, :].to_broadcast([P, NT + 1, D])
                             ).then_inc(stored, 16)
            for t in k.tab.values():
                sp.dma_start(t[NP:NS, :], k.w[:, 0:D]).then_inc(stored, 16)
            sp.wait_ge(stored, 16 * (COPIES + len(k.tab)))

        @block.gpsimd
        def _(pool):
            pool.iota(k.iota[:, :], [[1, P]], base=0, channel_multiplier=0,
                      allow_small_or_imprecise_dtypes=True).then_inc(consts, 1)
            pool.iota(k.spare[:, :], [[0, 1]], base=NP, channel_multiplier=1,
                      allow_small_or_imprecise_dtypes=True).then_inc(consts, 1)

        @block.vector
        def _(dve):
            n = [0]

            def link(ins_):
                n[0] += 1
                ins_.then_inc(step, 1)
                dve.wait_ge(step, n[0])

            dve.memset(k.w[:, :], 0.0).then_inc(zeroed, 1)
            dve.memset(k.ones[:, :], 1.0).then_inc(folded, 1)
            dve.wait_ge(consts, 2)
            link(dve.tensor_scalar(k.small[0][:, 0:1], k.spare[:, :], float(NP), None, ALU.subtract))
            dve.tensor_scalar(k.ident[:, :], k.iota[:, :], k.small[0][:, 0:1], None, ALU.is_equal)
            dve.tensor_scalar(k.lower[:, :], k.iota[:, :], k.small[0][:, 0:1], None, ALU.is_lt)
            dve.tensor_scalar(k.mask[:, :], k.small[0][:, 0:1], float(LAST), None, ALU.is_lt)
            dve.wait_ge(loaded, 16 * n_loads)
            link(dve.tensor_tensor(dist, dst_all.rearrange("p (g t) -> p g t", t=GROUP),
                                   first_all.unsqueeze(2).to_broadcast([P, NG, GROUP]), ALU.subtract))
            link(dve.tensor_reduce(k.small[0][:, 1:2], k.y[:, 0:NG * GROUP], AX.X, ALU.max))
            link(dve.tensor_reduce(k.small[0][:, 2:3], k.y[:, 0:NG * GROUP], AX.X, ALU.min))
            link(dve.tensor_scalar(k.small[0][:, 3:4], k.small[0][:, 1:2], float(WINDOW), None, ALU.is_lt))
            link(dve.tensor_scalar(k.small[0][:, 4:5], k.small[0][:, 2:3], 0.0, None, ALU.is_ge))
            dve.tensor_tensor(k.small[1][:, 0:1], k.small[0][:, 3:4], k.small[0][:, 4:5],
                              ALU.mult).then_inc(folded, 1)
            dve.tensor_copy(k.small[2][0:D, :], k.be2col[:, 0:1].to_broadcast([D, P])).then_inc(folded, 1)
            dve.wait_ge(summed, 2)
            dve.tensor_scalar(k.flag[:, :], ps[0:1, 0:1], float(P), None, ALU.is_ge)
            dve.tensor_copy(k.be2w[:, :], ps[:, D:2 * D])

        @block.tensor
        def _(pe):
            pe.wait_ge(folded, 3)
            pe.matmul(ps[0:1, 0:1], k.small[1][:, 0:1], k.ones[:, 0:1], start=True, stop=True).then_inc(summed, 1)
            pe.matmul(ps[:, D:2 * D], k.small[2][0:D, :], mat(k, "Wn_agg"), start=True,
                      stop=True).then_inc(summed, 1)



def degree_onehots(dve, k, b, sems, value):
    idx = k.idx[sems.ring(b)]
    hi_i, f = k.hilo_i[b % 2], k.hilo[b % 2]
    for s in range(2):
        col = idx[:, s * GROUP:(s + 1) * GROUP]
        dve.tensor_scalar(hi_i[:, s, :], col, P - 1, None, ALU.bitwise_and)
        last = dve.tensor_scalar(hi_i[:, 2 + s, :], col, 7, None, ALU.logical_shift_right)
    last.then_inc(sems.step, 1)
    dve.wait_ge(sems.step, value(1))
    dve.tensor_copy(f[:, :, :], hi_i[:, :, :]).then_inc(sems.step, 1)
    dve.wait_ge(sems.step, value(2))
    low, high = degree_views(k, b % 2)
    for s in range(2):
        dve.tensor_tensor(low[s], k.iota[:, :].unsqueeze(1).to_broadcast([P, GROUP, P]),
                          f[:, s, :].unsqueeze(2).to_broadcast([P, GROUP, P]), ALU.is_equal)
        last = dve.tensor_tensor(high[s], k.iota[:, 0:NT].unsqueeze(1).to_broadcast([P, GROUP, NT]),
                                 f[:, 2 + s, :].unsqueeze(2).to_broadcast([P, GROUP, NT]), ALU.is_equal)
    last.then_inc(sems.deg_ready[b % 2], 1)


def degree_views(k, b):
    words = k.w[:, :].bitcast(BF16)
    size = GROUP * (P + NT)
    low, high = [], []
    for s in range(2):
        at = (2 * b + s) * size
        low.append(words[:, at:at + GROUP * P].rearrange("p (t c) -> p t c", t=GROUP))
        high.append(words[:, at + GROUP * P:at + size].rearrange("p (t c) -> p t c", t=GROUP))
    return low, high


def degree_matmuls(pe, k, b, ps_deg, first, last):
    low, high = degree_views(k, b % 2)
    for t in range(GROUP):
        for s in range(2):
            ins_ = pe.matmul(ps_deg[s][:, 0:NT], low[s][:, t, :], high[s][:, t, :],
                             start=first and t == 0, stop=last and t == GROUP - 1)
    return ins_


class Names:
    pass


def finish_degrees(dve, k, ps_deg, done, base):
    for s, name in enumerate(("src", "dst")):
        dve.tensor_copy(k.deg[name][:, :], ps_deg[s][:, 0:NT])
        dve.tensor_scalar(k.rdeg[name][:, :], ps_deg[s][:, 0:NT], 1.0, None, ALU.max).then_inc(done, 1)
        dve.wait_ge(done, base + 2 * s + 1)
        dve.reciprocal(k.rdeg[name][:, :], k.rdeg[name][:, :]).then_inc(done, 1)
        dve.wait_ge(done, base + 2 * s + 2)


def degree_stage(nc, k):
    with stage(nc) as (ctx, sem):
        sems = Names()
        sems.ring = lambda b: b
        idx_ready = [sem(f"deg_idx_ready{b}") for b in range(2)]
        sems.step = sem("deg_step")
        sems.deg_ready = [sem(f"deg_onehot_ready{b}") for b in range(2)]
        counted = [sem(f"deg_counted{b}") for b in range(2)]
        done = sem("deg_done")
        ps_deg = [psum(nc, ctx, f"deg_ps{s}") for s in range(2)]
        block = ctx.enter_context(nc.Block())
        n = NG // 2

        @block.sync
        def _(sp):
            for b in range(2):
                sp.dma_start(k.idx[b][:, :], k.ins["cols"][b]).then_inc(idx_ready[b], 16)
            with sp.Fori(1, n) as i:
                for b in range(2):
                    sp.wait_ge(sems.deg_ready[b], i)
                    sp.dma_start(k.idx[b][:, :], group_cols(k, 2 * i + b)).then_inc(idx_ready[b], 16)

        @block.vector
        def _(dve):
            with dve.Fori(0, n) as i:
                for b in range(2):
                    dve.wait_ge(idx_ready[b], i * 16 + 16)
                    dve.wait_ge(counted[b], i + 1)
                    degree_onehots(dve, k, b, sems, lambda j: i * 4 + 2 * b + j)
            for b in range(2):
                dve.wait_ge(counted[b], n + 1)
            finish_degrees(dve, k, ps_deg, done, 0)

        @block.tensor
        def _(pe):
            for b in range(2):
                pe.sem_inc(counted[b])

            def count(b, i, first, last):
                pe.wait_ge(sems.deg_ready[b], i + 1)
                degree_matmuls(pe, k, b, ps_deg, first, last).then_inc(counted[b], 1)

            for b in range(2):
                count(b, 0, b == 0, False)
            with pe.Fori(1, n - 1) as i:
                for b in range(2):
                    count(b, i, False, False)
            for b in range(2):
                count(b, n - 1, False, b == 1)


def group_cols(k, g):
    return k.ins["cols"][bass.ds(g, 1)].rearrange("o p c -> (o p) c")


def group_first(k, g):
    return k.ins["first"][0:1, bass.ds(g, 1)].to_broadcast([P, 1])


halves = [t % 2 * (GROUP // 2) + t // 2 for t in range(GROUP)]


def attr_matmuls(pe, k, ps, attr):
    for t in range(GROUP):
        h, q = t % 2, t // 2
        mm = pe.matmul(ps[:, h * 512 + q * D:h * 512 + (q + 1) * D],
                       attr[h * D:(h + 1) * D, q * P:(q + 1) * P],
                       mat(k, "We_edge", h * D), start=True, stop=True)
    return mm


def attr_sum(dve, out, ps, rows):
    return dve.tensor_tensor(
        out.rearrange("p (h q f) -> p h q f", h=2, f=D),
        ps[:, :].rearrange("p (h q f) -> p h q f", h=2, f=D)[:, :, 0:GROUP // 2, :],
        rows[:, :, :].rearrange("p (q h) f -> p h q f", h=2), ALU.add)


def fast_pass(nc, k, table, degrees=False, edge_mlp=False):
    with stage(nc) as (ctx, sem):
        idx_ready = [sem(f"idx_ready{b}") for b in range(RING)]
        attr_ready = [sem(f"attr_ready{b}") for b in range(2)]
        gathered = [sem(f"gathered{b}") for b in range(RING)]
        onehot_ready = [sem(f"onehot_ready{b}") for b in range(RING)]
        attr_mm = [sem(f"attr_mm{b}") for b in range(2)]
        mlp_sum = [sem(f"mlp_sum{b}") for b in range(2)]
        message = [sem(f"message{b}") for b in range(2)]
        segmented = [sem(f"segmented{b}") for b in range(RING)]
        added = [sem(f"added{b}") for b in range(RING)]
        counted = [sem(f"counted{b}") for b in range(2)]
        local_ready, cleared, done, go = sem("local_ready"), sem("cleared"), sem("deg_done"), sem("pool_go")
        go_pe, go_sp = sem("pe_go"), sem("sp_go")
        sems = Names()
        sems.ring = lambda b: b
        sems.step = sem("deg_step")
        sems.deg_ready = [sem(f"deg_ready{b}") for b in range(2)]
        ps_seg = [psum(nc, ctx, f"ps_seg{b}", parts=D) for b in range(2)]
        if degrees:
            ps_deg = [psum(nc, ctx, f"ps_deg{s}") for s in range(2)]
        if edge_mlp:
            ps_attr = [psum(nc, ctx, f"ps_attr{b}", 1024) for b in range(2)]
            half = GROUP // 2
            attr = [k.w[:, b * half * P:(b + 1) * half * P] for b in range(2)]
            hid = [k.w[:, 2 * half * P + b * GROUP * D:2 * half * P + (b + 1) * GROUP * D] for b in range(2)]
            msg = [k.w[:, 2 * half * P + (2 + b) * GROUP * D:2 * half * P + (3 + b) * GROUP * D]
                   for b in range(2)]
        block = ctx.enter_context(nc.Block())

        def attr_of(g):
            c = g * (GROUP // 2 * P)
            return k.ins["attr"][:, bass.ds(c, GROUP // 2 * P)]

        @block.sync
        def _(sp):
            def load(b, g, i):
                if edge_mlp:
                    if not isinstance(i, int) or b >= 2:
                        sp.wait_ge(attr_mm[b % 2], i * 2 + b // 2)
                        sp.sem_inc(go_sp)
                    sp.dma_start(attr[b % 2], attr_of(g)).then_inc(attr_ready[b % 2], 16)
                sp.dma_start(k.idx[b][:, :], group_cols(k, g)).then_inc(idx_ready[b], 16)
                sp.dma_start(k.first[b][:, :], group_first(k, g)).then_inc(idx_ready[b], 16)

            for b in range(RING):
                load(b, b, 0)
            with sp.Fori(1, ITERS) as i:
                for b in range(RING):
                    sp.wait_ge(gathered[b], i * (16 * GROUP))
                    sp.wait_ge(added[b], i)
                    sp.sem_inc(go_sp)
                    load(b, i * RING + b, i)

        @block.gpsimd
        def _(pool):
            def gather(b, i):
                pool.wait_ge(idx_ready[b], i * 32 + 32)
                if not isinstance(i, int):
                    pool.wait_ge(segmented[b], i)
                pool.sem_inc(go)
                for t in range(GROUP):
                    pool.indirect_dma_start(
                        k.gath[b][:, t, :], None, table,
                        bass.IndirectOffsetOnAxis(ap=k.idx[b][:, t:t + 1], axis=0)).then_inc(gathered[b], 16)

            for b in range(RING):
                gather(b, 0)
            with pool.Fori(1, ITERS) as i:
                for b in range(RING):
                    gather(b, i)
            for b in range(RING):
                pool.wait_ge(gathered[b], ITERS * 16 * GROUP)

        @block.vector
        def _(dve):
            dve.memset(k.acc[:, :], 0.0).then_inc(cleared, 1)
            dve.wait_ge(cleared, 1)
            with dve.Fori(0, ITERS) as i:
                for b in range(RING):
                    dve.wait_ge(idx_ready[b], i * 32 + 32)
                    dve.tensor_tensor(k.local[b][:, :], k.idx[b][:, GROUP:2 * GROUP],
                                      k.first[b][:, 0:1].to_broadcast([P, GROUP]), ALU.subtract
                                      ).then_inc(local_ready, 1)
                    dve.wait_ge(local_ready, i * RING + b + 1)
                    dve.tensor_tensor(k.oneh[b % 2][:, :, :],
                                      k.iota[:, :].unsqueeze(1).to_broadcast([P, GROUP, WINDOW]),
                                      k.local[b][:, :].unsqueeze(2).to_broadcast([P, GROUP, WINDOW]),
                                      ALU.is_equal).then_inc(onehot_ready[b], 1)
                    if degrees:
                        dve.wait_ge(counted[b % 2], i * 2 + b // 2 + 1)
                        degree_onehots(dve, k, b, sems, lambda j: (i * RING + b) * 2 + j)
                    if edge_mlp:
                        dve.wait_ge(gathered[b], i * (16 * GROUP) + 16 * GROUP)
                        dve.wait_ge(attr_mm[b % 2], i * 2 + b // 2 + 1)
                        attr_sum(dve, hid[b % 2], ps_attr[b % 2], k.gath[b]).then_inc(mlp_sum[b % 2], 1)
                    at = dve.value_load(k.first[b][0:1, 0:1], min_val=0, max_val=NP)
                    dve.wait_ge(segmented[b], i + 1)
                    dve.tensor_tensor(k.acc[:, bass.ds(at, WINDOW)], k.acc[:, bass.ds(at, WINDOW)],
                                      ps_seg[b % 2][:, 0:WINDOW], ALU.add).then_inc(added[b], 1)
                    dve.wait_ge(added[b], i + 1)
            if degrees:
                for b in range(2):
                    dve.wait_ge(counted[b], 2 * ITERS + 1)
                finish_degrees(dve, k, ps_deg, done, 0)

        @block.scalar
        def _(act):
            if edge_mlp:
                with act.Fori(0, ITERS) as i:
                    for b in range(RING):
                        act.wait_ge(mlp_sum[b % 2], i * 2 + b // 2 + 1)
                        act.activation(msg[b % 2], hid[b % 2], ACT.Relu).then_inc(message[b % 2], 1)

        @block.tensor
        def _(pe):
            if degrees:
                for b in range(2):
                    pe.sem_inc(counted[b])

            def group(b, i, first=False, last=False):
                if edge_mlp:
                    pe.wait_ge(attr_ready[b % 2], i * 32 + (b // 2) * 16 + 16)
                    pe.sem_inc(go_pe)
                    attr_matmuls(pe, k, ps_attr[b % 2], attr[b % 2]).then_inc(attr_mm[b % 2], 1)
                    pe.wait_ge(message[b % 2], i * 2 + b // 2 + 1)
                    rows = msg[b % 2].rearrange("p (t f) -> p t f", f=D)
                    place = halves
                else:
                    pe.wait_ge(gathered[b], i * (16 * GROUP) + 16 * GROUP)
                    rows, place = k.gath[b], range(GROUP)
                pe.wait_ge(onehot_ready[b], i + 1)
                if b >= 2:
                    pe.wait_ge(added[b - 2], i + 1)
                for t in range(GROUP):
                    mm = pe.matmul(ps_seg[b % 2][:, 0:WINDOW], rows[:, place[t], :], k.oneh[b % 2][:, t, :],
                                   start=t == 0, stop=t == GROUP - 1)
                mm.then_inc(segmented[b], 1)
                if degrees:
                    pe.wait_ge(sems.deg_ready[b % 2], i * 2 + b // 2 + 1)
                    degree_matmuls(pe, k, b, ps_deg, first, last).then_inc(counted[b % 2], 1)

            for b in range(RING):
                group(b, 0, first=b == 0)
            with pe.Fori(1, ITERS - 1) as i:
                for b in range(RING):
                    group(b, i)
            for b in range(RING):
                group(b, ITERS - 1, last=b == RING - 1)


def equality(dve, k, eq, srow, col, low, cnt, sidx, link):
    link(dve.tensor_tensor(eq, srow, col.unsqueeze(2).to_broadcast([P, GROUP, P]), ALU.is_equal))
    link(dve.tensor_tensor(low, eq, k.lower[:, :].unsqueeze(1).to_broadcast([P, GROUP, P]), ALU.mult))
    link(dve.tensor_reduce(cnt[:, 0:GROUP], low, AX.X, ALU.add))
    link(dve.tensor_scalar(cnt[:, GROUP:2 * GROUP], cnt[:, 0:GROUP], 0.5, None, ALU.is_lt))
    link(dve.tensor_scalar(cnt[:, 2 * GROUP:3 * GROUP], col, k.spare[:, 0:1], None, ALU.subtract))
    link(dve.tensor_tensor(cnt[:, 3 * GROUP:4 * GROUP], cnt[:, 2 * GROUP:3 * GROUP],
                           cnt[:, GROUP:2 * GROUP], ALU.mult))
    return dve.tensor_scalar(sidx, cnt[:, 3 * GROUP:4 * GROUP], k.spare[:, 0:1], None, ALU.add)


EQ_STEPS = 6


def general_pass(nc, k, table, by, edge_mlp=False):
    gather_at, scatter_at = (0, GROUP) if by == "dst" else (GROUP, 0)
    row_of = 1 if by == "dst" else 0
    with stage(nc) as (ctx, sem):
        loaded, gathered, step, ready = sem("g_loaded"), sem("g_gathered"), sem("g_step"), sem("g_ready")
        attr_mm, mlp_sum, message = sem("g_attr_mm"), sem("g_mlp_sum"), sem("g_message")
        combined, copied, go = sem("g_combined"), sem("g_copied"), sem("g_go")
        scattered = [sem(f"g_scattered{c}") for c in range(COPIES)]
        go_pe, go_sp = sem("g_pe_go"), sem("g_sp_go")
        ps_c = psum(nc, ctx, "g_ps_c")
        ps_a = psum(nc, ctx, "g_ps_a", 1024)
        wcol = lambda a, n: k.w[:, a:a + n]
        eq = wcol(1024, 1024).rearrange("p (t c) -> p t c", c=P)
        low = wcol(2048, 1024).rearrange("p (t c) -> p t c", c=P)
        attr = wcol(3072, 512)
        hid, msg = wcol(3584, 512), wcol(4096, 512)
        cnt = wcol(4608, 64)
        sidx = wcol(4672, GROUP).bitcast(I32)
        comb = k.gath[1]
        per = (3 if edge_mlp else 2) * 16
        block = ctx.enter_context(nc.Block())
        each = 16 * GROUP // COPIES

        @block.sync
        def _(sp):
            def load(g):
                sp.dma_start(k.idx[0][:, :], group_cols(k, g)).then_inc(loaded, 16)
                sp.dma_start(wcol(0, GROUP * P).bitcast(I32),
                             k.ins["rows_of"][bass.ds(g, 1), row_of, :].to_broadcast([P, GROUP * P])
                             ).then_inc(loaded, 16)
                if edge_mlp:
                    sp.dma_start(attr, k.ins["attr"][:, bass.ds(g * (GROUP // 2 * P), GROUP // 2 * P)]
                                 ).then_inc(loaded, 16)

            load(0)
            with sp.Fori(1, NG) as g:
                for c in range(COPIES):
                    sp.wait_ge(scattered[c], g * each)
                sp.sem_inc(go_sp)
                load(g)
            for c in range(COPIES):
                sp.wait_ge(scattered[c], NG * each)

        @block.gpsimd
        def _(pool):
            with pool.Fori(0, NG) as g:
                pool.wait_ge(loaded, g * per + per)
                pool.sem_inc(go)
                for t in range(GROUP):
                    pool.indirect_dma_start(
                        k.gath[0][:, t, :], None, table,
                        bass.IndirectOffsetOnAxis(ap=k.idx[0][:, gather_at + t:gather_at + t + 1], axis=0)
                    ).then_inc(gathered, 16)
                pool.wait_ge(ready, g + 1)
                pool.wait_ge(copied, g + 1)
                pool.sem_inc(go)
                for t in range(GROUP):
                    c = t % COPIES
                    if t >= COPIES:
                        pool.wait_ge(scattered[c], g * each + 16 * (t // COPIES))
                        pool.sem_inc(go)
                    pool.indirect_dma_start(
                        k.part[c], bass.IndirectOffsetOnAxis(ap=sidx[:, t:t + 1], axis=0),
                        comb[:, t, :], None, compute_op=ALU.add).then_inc(scattered[c], 16)
            pool.wait_ge(gathered, NG * 16 * GROUP)
            for c in range(COPIES):
                pool.wait_ge(scattered[c], NG * each)

        @block.vector
        def _(dve):
            with dve.Fori(0, NG) as g:
                n = [0]

                def link(ins_):
                    n[0] += 1
                    ins_.then_inc(step, 1)
                    dve.wait_ge(step, g * EQ_STEPS + n[0])

                dve.wait_ge(loaded, g * per + per)
                equality(dve, k, eq, wcol(0, GROUP * P).bitcast(I32).rearrange("p (t c) -> p t c", c=P),
                         k.idx[0][:, scatter_at:scatter_at + GROUP], low, cnt, sidx, link).then_inc(ready, 1)
                assert n[0] == EQ_STEPS
                if edge_mlp:
                    dve.wait_ge(gathered, g * (16 * GROUP) + 16 * GROUP)
                    dve.wait_ge(attr_mm, g + 1)
                    attr_sum(dve, hid, ps_a, k.gath[0]).then_inc(mlp_sum, 1)

        @block.scalar
        def _(act):
            with act.Fori(0, NG) as g:
                if edge_mlp:
                    act.wait_ge(mlp_sum, g + 1)
                    act.activation(msg, hid, ACT.Relu).then_inc(message, 1)
                act.wait_ge(combined, g + 1)
                act.copy(comb[:, :, :].rearrange("p t f -> p (t f)"), ps_c[:, :]).then_inc(copied, 1)

        @block.tensor
        def _(pe):
            with pe.Fori(0, NG) as g:
                if edge_mlp:
                    pe.wait_ge(loaded, g * per + per)
                    pe.sem_inc(go_pe)
                    attr_matmuls(pe, k, ps_a, attr).then_inc(attr_mm, 1)
                    pe.wait_ge(message, g + 1)
                    rows = msg.rearrange("p (t f) -> p t f", f=D)
                    place = halves
                else:
                    pe.wait_ge(gathered, g * (16 * GROUP) + 16 * GROUP)
                    rows, place = k.gath[0], range(GROUP)
                pe.wait_ge(ready, g + 1)
                for t in range(GROUP):
                    mm = pe.matmul(ps_c[:, t * D:(t + 1) * D], eq[:, t, :], rows[:, place[t], :], start=True, stop=True)
                mm.then_inc(combined, 1)


def reverse_pass(nc, k, table):
    with stage(nc) as (ctx, sem):
        n_it = NG // 2
        idx_ready = [sem(f"r_idx_ready{b}") for b in range(2)]
        win_ready = [sem(f"r_win_ready{b}") for b in range(2)]
        ready = [sem(f"r_ready{b}") for b in range(2)]
        oh_ready = [sem(f"r_oh_ready{b}") for b in range(2)]
        mixed = [sem(f"r_mixed{b}") for b in range(2)]
        mix_copied = [sem(f"r_mix_copied{b}") for b in range(2)]
        combined = [sem(f"r_combined{b}") for b in range(2)]
        copied = [sem(f"r_copied{b}") for b in range(2)]
        scattered = [sem(f"r_scattered{c}") for c in range(COPIES)]
        free = [sem(f"r_free{b}") for b in range(2)]
        step, go = sem("r_step"), sem("r_go")
        ps_mix = [psum(nc, ctx, f"r_ps_mix{b}", 1024) for b in range(2)]
        ps_c = [psum(nc, ctx, f"r_ps_c{b}") for b in range(2)]
        area = NT * D // 2
        wcol = lambda b, a, n: k.w[:, b * area + a:b * area + a + n]
        hcol = lambda b, a, n: k.h[:, b * area + a:b * area + a + n]
        srow = [wcol(b, 0, 1024).bitcast(I32) for b in range(2)]
        eq = [wcol(b, 1024, 512).bitcast(BF16).rearrange("p (t c) -> p t c", c=P) for b in range(2)]
        low = [wcol(b, 1536, 512).bitcast(BF16).rearrange("p (t c) -> p t c", c=P) for b in range(2)]
        oh = [wcol(b, 2048, 512).bitcast(BF16).rearrange("p (t c) -> p t c", c=P) for b in range(2)]
        mix = [hcol(b, 0, 1024) for b in range(2)]
        win = [hcol(b, 1024, D) for b in range(2)]
        cnt = [hcol(b, 1100, 64) for b in range(2)]
        sidx = [hcol(b, 1164, GROUP).bitcast(I32) for b in range(2)]
        comb = k.gath
        each = 16 * GROUP // COPIES
        block = ctx.enter_context(nc.Block())

        @block.sync
        def _(sp):
            def load(b, g, i):
                sp.dma_start(k.idx[b][:, :], group_cols(k, g)).then_inc(idx_ready[b], 16)
                sp.dma_start(k.first[b][:, :], group_first(k, g)).then_inc(idx_ready[b], 16)
                sp.dma_start(srow[b], k.ins["rows_of"][bass.ds(g, 1), 0, :].to_broadcast([P, GROUP * P])
                             ).then_inc(idx_ready[b], 16)
                sp.wait_ge(idx_ready[b], i * 48 + 48)
                sp.sem_inc(go)
                at = sp.value_load(k.first[b][0:1, 0:1], min_val=0, max_val=NP)
                sp.dma_start(win[b], table[bass.ds(at, WINDOW), :]).then_inc(win_ready[b], 16)

            for b in range(2):
                load(b, b, 0)
            with sp.Fori(1, n_it) as i:
                for b in range(2):
                    sp.wait_ge(ready[b], i)
                    sp.wait_ge(oh_ready[b], i)
                    sp.wait_ge(combined[b], i)
                    load(b, i * 2 + b, i)
            for c in range(COPIES):
                sp.wait_ge(scattered[c], NG * each)

        @block.vector
        def _(dve):
            with dve.Fori(0, n_it) as i:
                for b in range(2):
                    n = [0]

                    def link(ins_):
                        n[0] += 1
                        ins_.then_inc(step, 1)
                        dve.wait_ge(step, (i * 2 + b) * (EQ_STEPS + 1) + n[0])

                    dve.wait_ge(idx_ready[b], i * 48 + 48)
                    dve.wait_ge(mixed[b], i + 1)
                    dve.wait_ge(free[b], i + 1)
                    link(dve.tensor_tensor(k.local[b][:, :], k.idx[b][:, GROUP:2 * GROUP],
                                           k.first[b][:, 0:1].to_broadcast([P, GROUP]), ALU.subtract))
                    dve.tensor_tensor(oh[b], k.iota[:, :].unsqueeze(1).to_broadcast([P, GROUP, P]),
                                      k.local[b][:, :].unsqueeze(2).to_broadcast([P, GROUP, P]),
                                      ALU.is_equal).then_inc(oh_ready[b], 1)
                    equality(dve, k, eq[b], srow[b].rearrange("p (t c) -> p t c", c=P),
                             k.idx[b][:, 0:GROUP], low[b], cnt[b], sidx[b], link).then_inc(ready[b], 1)

        @block.tensor
        def _(pe):
            for b in range(2):
                pe.sem_inc(mixed[b])
            with pe.Fori(0, n_it) as i:
                for b in range(2):
                    pe.wait_ge(oh_ready[b], i + 1)
                    pe.wait_ge(ready[b], i + 1)
                    pe.wait_ge(mix_copied[b], i + 1)
                    for t in range(GROUP):
                        mm = pe.matmul(ps_mix[b][:, t * P:(t + 1) * P], oh[b][:, t, :], eq[b][:, t, :],
                                       start=True, stop=True)
                    mm.then_inc(mixed[b], 1)
                    pe.wait_ge(mix_copied[b], i + 2)
                    pe.wait_ge(win_ready[b], i * 16 + 16)
                    pe.wait_ge(copied[b], i + 1)
                    for t in range(GROUP):
                        mm = pe.matmul(ps_c[b][:, t * D:(t + 1) * D], mix[b][:, t * P:(t + 1) * P], win[b],
                                       start=True, stop=True)
                    mm.then_inc(combined[b], 1)

        @block.scalar
        def _(act):
            for b in range(2):
                act.sem_inc(mix_copied[b])
                act.sem_inc(copied[b])
            with act.Fori(0, n_it) as i:
                for b in range(2):
                    act.wait_ge(mixed[b], i + 2)
                    act.copy(mix[b], ps_mix[b][:, :]).then_inc(mix_copied[b], 1)
                    act.wait_ge(combined[b], i + 1)
                    act.wait_ge(free[b], i + 1)
                    act.copy(comb[b][:, :, :].rearrange("p t f -> p (t f)"), ps_c[b][:, :]).then_inc(copied[b], 1)

        @block.gpsimd
        def _(pool):
            for b in range(2):
                pool.sem_inc(free[b])

            def scatter(b, i):
                pool.wait_ge(ready[b], i + 1)
                pool.wait_ge(copied[b], i + 2)
                for t in range(GROUP):
                    c = t % COPIES
                    if not isinstance(i, int) or b or t >= COPIES:
                        pool.wait_ge(scattered[c], (i * 2 + b) * each + 16 * (t // COPIES))
                        if t == COPIES - 1 and (not isinstance(i, int) or b):
                            pool.sem_inc(free[1 - b])
                    pool.sem_inc(go)
                    pool.indirect_dma_start(
                        k.part[c], bass.IndirectOffsetOnAxis(ap=sidx[b][:, t:t + 1], axis=0),
                        comb[b][:, t, :], None, compute_op=ALU.add).then_inc(scattered[c], 16)

            for b in range(2):
                scatter(b, 0)
            with pool.Fori(1, n_it) as i:
                for b in range(2):
                    scatter(b, i)
            for c in range(COPIES):
                pool.wait_ge(scattered[c], NG * each)


def gather_partials(nc, k, out, to_acc):
    with stage(nc) as (ctx, sem):
        loaded, step, zero_ready, zeroed = (sem("p_loaded"), sem("p_step"), sem("p_zero"), sem("p_zeroed"))
        turned, moved, staged, row_free = sem("p_turned"), sem("p_moved"), sem("p_staged"), sem("p_row_free")
        go = sem("p_go")
        rows = [k.gath[b][:, :, :].rearrange("p t f -> p (t f)")[:, 0:CW] for b in range(2)]
        ps = [psum(nc, ctx, f"p_ps{b}", 1024, parts=D) for b in range(2)]
        block = ctx.enter_context(nc.Block())

        @block.sync
        def _(sp):
            sp.dma_start(nm3(out), dram_nm(k.part[0])).then_inc(loaded, 16)
            for c in range(1, COPIES):
                if c > 1:
                    sp.wait_ge(step, c - 1)
                sp.dma_start(nm3(k.w), dram_nm(k.part[c])).then_inc(loaded, 16)
                sp.wait_ge(loaded, 16 * (c + 1))
            sp.wait_ge(zero_ready, 1)
            for c in range(COPIES):
                sp.dma_start(dram_nm(k.part[c], NS), nm3(k.w)[:, 0:1, :].to_broadcast([P, NT + 1, D])
                             ).then_inc(zeroed, 16)
            sp.wait_ge(zeroed, 16 * COPIES)

        @block.vector
        def _(dve):
            for c in range(1, COPIES):
                dve.wait_ge(loaded, 16 * (c + 1))
                dve.tensor_tensor(out[:, :], out[:, :], k.w[:, :], ALU.add).then_inc(step, 1)
                dve.wait_ge(step, c)
            dve.memset(k.w[:, 0:D], 0.0).then_inc(zero_ready, 1)

        @block.gpsimd
        def _(pool):
            if to_acc:
                pool.wait_ge(step, COPIES - 1)
                with pool.Fori(0, NCH // 2) as i:
                    for b in range(2):
                        pool.wait_ge(row_free, 2 * i + b + 1)
                        pool.tensor_copy(rows[b], out[:, bass.ds((2 * i + b) * CW, CW)]).then_inc(staged, 1)

        @block.tensor
        def _(pe):
            if to_acc:
                with pe.Fori(0, NCH // 2) as i:
                    for b in range(2):
                        pe.wait_ge(staged, 2 * i + b + 1)
                        pe.wait_ge(moved, 2 * i + b + 1)
                        pe.sem_inc(go)
                        for j in range(CT):
                            mm = pe.transpose(ps[b][:, j * P:(j + 1) * P],
                                              rows[b][:, j * D:(j + 1) * D], k.ident[:, :])
                        mm.then_inc(turned, 1)

        @block.scalar
        def _(act):
            if to_acc:
                act.sem_inc(moved, 2)
                act.sem_inc(row_free, 2)
                with act.Fori(0, NCH // 2) as i:
                    for b in range(2):
                        act.wait_ge(turned, 2 * i + b + 1)
                        act.sem_inc(row_free)
                        act.copy(k.acc[:, bass.ds((2 * i + b) * CF, CF)], ps[b][:, 0:CF]).then_inc(moved, 1)



def linear_stage(nc, k, out, src=None, w_self=None, bias=None, w_agg=None, w_first=None,
                 scale=None, plus=None, degree_row=False, relu=False):
    with stage(nc) as (ctx, sem):
        turned, moved, sums_mm, sums_moved = sem("l_turned"), sem("l_moved"), sem("l_sums"), sem("l_sums_moved")
        product, combined, finished, part = sem("l_product"), sem("l_combined"), sem("l_finished"), sem("l_part")
        staged, row_free, sums_staged, go = sem("l_staged"), sem("l_row_free"), sem("l_sums_staged"), sem("l_go")
        sums = [k.w[0:D, b * CF:(b + 1) * CF] for b in range(2)]
        rows = [k.gath[b][:, :, :].rearrange("p t f -> p (t f)")[:, 0:CW] for b in range(2)]
        ps_turn = psum(nc, ctx, "l_ps_turn", 1024, parts=D)
        ps_first = psum(nc, ctx, "l_ps_first", 1024, parts=D)
        ps_self = [psum(nc, ctx, f"l_ps_self{b}") for b in range(2)]
        ps_agg = [psum(nc, ctx, f"l_ps_agg{b}") for b in range(2)]
        two_steps = scale is not None or degree_row
        separate = scale is not None
        temp = [k.oneh[b][:, :, :].rearrange("p t c -> p (t c)")[:, 0:CW] for b in range(2)]
        block = ctx.enter_context(nc.Block())

        def chunk(t, c, w):
            return t[:, bass.ds(c * w, w)]

        @block.tensor
        def _(pe):
            with pe.Fori(0, NCH // 2) as i:
                for b in range(2):
                    c = 2 * i + b
                    if src is not None:
                        pe.wait_ge(staged, c + 1)
                        pe.wait_ge(moved, c + 1)
                        pe.sem_inc(go)
                        for j in range(CT):
                            mm = pe.transpose(ps_turn[:, j * P:(j + 1) * P],
                                              rows[b][:, j * D:(j + 1) * D], k.ident[:, :])
                        mm.then_inc(turned, 1)
                    if w_first is not None:
                        pe.wait_ge(sums_staged, c + 1)
                        pe.wait_ge(sums_moved, c + 1)
                        pe.sem_inc(go)
                        for j in range(2):
                            mm = pe.matmul(ps_first[:, j * 512:j * 512 + CF // 2], mat(k, w_first),
                                           sums[b][:, j * (CF // 2):(j + 1) * (CF // 2)],
                                           start=True, stop=True)
                        mm.then_inc(sums_mm, 1)
                    pe.wait_ge(combined, c + 1)
                    if src is not None:
                        pe.matmul(ps_self[b][:, 0:CW].rearrange("p (t f) -> p t f", f=D), k.ones[0:1, :],
                                  bias_row(k, bias), start=True, stop=False, skip_group_check=True)
                        pe.wait_ge(moved, c + 2)
                        for j in range(CT):
                            mm = pe.matmul(ps_self[b][:, j * D:(j + 1) * D], k.xT[b][:, j * P:(j + 1) * P],
                                           mat(k, w_self), start=False, stop=w_agg is None or separate,
                                           skip_group_check=True)
                    if w_agg is not None:
                        pe.wait_ge(sums_moved, c + 2)
                        for j in range(CT):
                            target = ps_agg[b] if separate else ps_self[b]
                            mm = pe.matmul(target[:, j * D:(j + 1) * D], k.sT[b][:, j * P:(j + 1) * P], mat(k, w_agg),
                                           start=separate, stop=True, skip_group_check=True)
                    mm.then_inc(product, 1)

        @block.scalar
        def _(act):
            act.sem_inc(moved, 1)
            act.sem_inc(sums_moved, 1)
            act.sem_inc(row_free, 2)
            with act.Fori(0, NCH // 2) as i:
                for b in range(2):
                    c = 2 * i + b
                    if src is not None:
                        act.wait_ge(turned, c + 1)
                        act.wait_ge(combined, c + 1)
                        act.sem_inc(row_free)
                        act.copy(k.xT[b][:, :], ps_turn[:, 0:CF]).then_inc(moved, 1)
                    if w_first is not None:
                        act.wait_ge(combined, c + 1)
                        act.copy(sums[b], chunk(k.acc, c, CF)).then_inc(sums_staged, 1)
                        act.wait_ge(sums_mm, c + 1)
                        act.copy(k.sT[b][:, :].rearrange("p (a c) -> p a c", a=2),
                                 ps_first[:, :].rearrange("p (a c) -> p a c", a=2)[:, :, 0:CF // 2]
                                 ).then_inc(sums_moved, 1)
                    elif w_agg is not None:
                        act.wait_ge(combined, c + 1)
                        act.copy(k.sT[b][:, :], chunk(k.acc, c, CF)).then_inc(sums_moved, 1)

        @block.gpsimd
        def _(pool):
            if src is not None:
                with pool.Fori(0, NCH // 2) as i:
                    for b in range(2):
                        c = 2 * i + b
                        pool.wait_ge(row_free, c + 1)
                        pool.tensor_copy(rows[b], chunk(src, c, CW)).then_inc(staged, 1)

        @block.vector
        def _(dve):
            dve.sem_inc(combined, 2)
            with dve.Fori(0, NCH // 2) as i:
                for b in range(2):
                    c = 2 * i + b
                    dve.wait_ge(product, c + 1)
                    o = chunk(out, c, CW)
                    o3 = o.rearrange("p (t f) -> p t f", f=D)
                    t3 = temp[b].rearrange("p (t f) -> p t f", f=D)
                    if two_steps:
                        if degree_row:
                            dve.tensor_tensor(t3, over_features(k.deg["dst"][:, bass.ds(c * CT, CT)], CT),
                                              over_tiles(k.be2w[:, :], CT), ALU.mult).then_inc(part, 1)
                        else:
                            dve.tensor_tensor(t3, ps_agg[b][:, 0:CW].rearrange("p (t f) -> p t f", f=D),
                                              over_features(scale[:, bass.ds(c * CT, CT)], CT),
                                              ALU.mult).then_inc(part, 1)
                        dve.wait_ge(part, c + 1)
                        other = ps_self[b][:, 0:CW] if src is not None else chunk(plus, c, CW)
                        dve.tensor_tensor(o, temp[b], other, ALU.add).then_inc(combined, 1)
                        if relu:
                            dve.wait_ge(combined, c + 3)
                            dve.tensor_scalar(o, o, 0.0, None, ALU.max)
                    elif relu:
                        dve.tensor_scalar(o, ps_self[b][:, 0:CW], 0.0, None, ALU.max).then_inc(combined, 1)
                    else:
                        dve.tensor_copy(o, ps_self[b][:, 0:CW]).then_inc(combined, 1)


def norm_stage(nc, k, src, twice=False, batch=False, tables=(), out=None):
    with stage(nc) as (ctx, sem):
        step, act_done, pe_done, stored = sem("n_step"), sem("n_act"), sem("n_pe"), sem("n_stored")
        ps = psum(nc, ctx, "n_ps")
        s0, s1, s2 = k.small
        block = ctx.enter_context(nc.Block())
        marks = {}
        w, y = k.w, k.y

        @block.vector
        def _(dve):
            n, na, npe = [0], [0], [0]

            def link(ins_, name=None):
                n[0] += 1
                ins_.then_inc(step, 1)
                dve.wait_ge(step, n[0])
                if name:
                    marks[name] = n[0]

            def wait_act():
                na[0] += 1
                dve.wait_ge(act_done, na[0])

            def wait_pe():
                npe[0] += 1
                dve.wait_ge(pe_done, npe[0])

            if batch:
                link(dve.tensor_tensor(w[:, :], src[:, :], src[:, :], ALU.mult))
                link(dve.tensor_reduce(s0[:, 0:NT], nm3(w), AX.X, ALU.add), "sumsq")
                wait_act()
                link(dve.tensor_scalar(s0[:, 0:NT], s1[:, 0:NT], L2_EPS, None, ALU.max))
                link(dve.reciprocal(s1[:, 0:NT], s0[:, 0:NT]))
                link(dve.tensor_tensor(nm3(src), nm3(src), over_features(s1[:, 0:NT]), ALU.mult))
                link(dve.tensor_scalar(src[:, :], src[:, :], 0.0, None, ALU.max))
                last = src[:, (NT - 1) * D:NT * D]
                link(dve.tensor_scalar(last, last, k.mask[:, 0:1], None, ALU.mult), "rows")
                wait_pe()
                per_feature = ps[:, 0:CW].rearrange("p (t f) -> p f t", f=D)
                link(dve.tensor_reduce(s0[:, 0:D], per_feature, AX.X, ALU.add))
                link(dve.tensor_scalar(s0[:, 0:D], s0[:, 0:D], 1.0 / N, None, ALU.mult))
                link(dve.tensor_tensor(nm3(src), nm3(src), over_tiles(s0[:, 0:D]), ALU.subtract))
                link(dve.tensor_scalar(last, last, k.mask[:, 0:1], None, ALU.mult))
                link(dve.tensor_tensor(w[:, :], src[:, :], src[:, :], ALU.mult), "squares")
                wait_pe()
                link(dve.tensor_reduce(s0[:, 0:D], per_feature, AX.X, ALU.add))
                link(dve.tensor_scalar(s0[:, 0:D], s0[:, 0:D], 1.0 / N, BN_EPS, ALU.mult, ALU.add), "var")
                wait_act()
                link(dve.reciprocal(s2[:, 0:D], s1[:, 0:D]))
                link(dve.tensor_tensor(s2[:, 0:D], s2[:, 0:D], k.gamma[:, :], ALU.mult))
                link(dve.tensor_tensor(nm3(src), nm3(src), over_tiles(s2[:, 0:D]), ALU.mult))
                link(dve.tensor_tensor(nm3(src), nm3(src), over_tiles(k.beta[:, :]), ALU.add))
                link(dve.tensor_tensor(src[:, :], src[:, :], k.x[:, :], ALU.add))
            link(dve.tensor_tensor(y[:, :], src[:, :], k.x[:, :], ALU.add))
            link(dve.tensor_reduce(s0[:, 0:NT], nm3(y), AX.X, ALU.add))
            link(dve.tensor_scalar(s0[:, 0:NT], s0[:, 0:NT], 1.0 / D, None, ALU.mult))
            link(dve.tensor_tensor(nm3(y), nm3(y), over_features(s0[:, 0:NT]), ALU.subtract))
            link(dve.tensor_tensor(w[:, :], y[:, :], y[:, :], ALU.mult))
            link(dve.tensor_reduce(s0[:, 0:NT], nm3(w), AX.X, ALU.add))
            link(dve.tensor_scalar(s0[:, 0:NT], s0[:, 0:NT], 1.0 / D, LN_EPS, ALU.mult, ALU.add), "lnvar")
            wait_act()
            link(dve.reciprocal(s2[:, 0:NT], s1[:, 0:NT]))
            link(dve.tensor_tensor(nm3(k.x), nm3(y), over_features(s2[:, 0:NT]), ALU.mult), "x")

        @block.scalar
        def _(act):
            if batch:
                act.wait_ge(step, marks["sumsq"])
                act.activation(s1[:, 0:NT], s0[:, 0:NT], ACT.Sqrt).then_inc(act_done, 1)
                act.wait_ge(step, marks["var"])
                act.activation(s1[:, 0:D], s0[:, 0:D], ACT.Sqrt).then_inc(act_done, 1)
            act.wait_ge(step, marks["lnvar"])
            act.activation(s1[:, 0:NT], s0[:, 0:NT], ACT.Sqrt).then_inc(act_done, 1)

        @block.tensor
        def _(pe):
            if batch:
                for name, rows in (("rows", src), ("squares", w)):
                    pe.wait_ge(step, marks[name])
                    for c in range(NCH):
                        mm = pe.matmul(ps[:, 0:CW], k.ones[:, :], rows[:, c * CW:(c + 1) * CW],
                                       start=c == 0, stop=c == NCH - 1)
                    mm.then_inc(pe_done, 1)

        @block.sync
        def _(sp):
            sp.wait_ge(step, marks["x"])
            count = 0
            for t in tables:
                sp.dma_start(dram_nm(t), nm3(k.x)).then_inc(stored, 16)
                count += 16
            if out is not None:
                full = (NT - 1) * P
                sp.dma_start(out[0:full, :].rearrange("(t p) f -> p t f", p=P),
                             nm3(k.x)[:, 0:NT - 1, :]).then_inc(stored, 16)
                sp.dma_start(out[full:N, :], k.x[0:LAST, (NT - 1) * D:NT * D]).then_inc(stored, 16)
                count += 32
            if count:
                sp.wait_ge(stored, count)


def store_stage(nc, k, table, rows):
    with stage(nc) as (ctx, sem):
        stored = sem("t_stored")
        block = ctx.enter_context(nc.Block())

        @block.sync
        def _(sp):
            sp.dma_start(dram_nm(table), nm3(rows)).then_inc(stored, 16)
            sp.wait_ge(stored, 16)


def scale_stage(nc, k, rows, factor):
    with stage(nc) as (ctx, sem):
        block = ctx.enter_context(nc.Block())

        @block.vector
        def _(dve):
            dve.tensor_tensor(nm3(rows), nm3(rows), over_features(factor[:, :]), ALU.mult)


def segment_sums(nc, k, fast, table, degrees=False, edge_mlp=False):
    with nc.If(fast):
        fast_pass(nc, k, table, degrees, edge_mlp)
    with nc.Else():
        if degrees:
            degree_stage(nc, k)
        general_pass(nc, k, table, "dst", edge_mlp)
        gather_partials(nc, k, k.y, True)


def build(nc, ins, out):
    with ExitStack() as ctx:
        k = alloc(nc, ctx, ins)
        k.sT = [ctx.enter_context(nc.sbuf_tensor(f"sT{b}", [D, CF], F32)) for b in range(2)]
        setup_stage(nc, k)
        fast = nc.values_load(k.flag[0:1, 0:1], min_val=0, max_val=1,
                              skip_runtime_bounds_check_because="it is the result of a comparison")
        segment_sums(nc, k, fast, ins["x"], degrees=True)
        linear_stage(nc, k, k.h, src=k.x, w_self="W0_self", bias="b0", w_agg="W0_agg", scale=k.rdeg["dst"])
        norm_stage(nc, k, k.h, batch=True, tables=[k.tab["x1"]])
        segment_sums(nc, k, fast, k.tab["x1"])
        linear_stage(nc, k, k.h, src=k.x, w_self="W1_self", bias="b1", w_agg="W1_agg",
                     scale=k.rdeg["dst"], relu=True)
        store_stage(nc, k, k.tab["h1"], k.h)
        segment_sums(nc, k, fast, k.tab["h1"])
        linear_stage(nc, k, k.y, src=k.h, w_self="W2_self", bias="b2", w_agg="W2_agg",
                     scale=k.rdeg["dst"], relu=True)
        linear_stage(nc, k, k.h, src=k.y, w_self="Wlin", bias="blin")
        norm_stage(nc, k, k.h)
        linear_stage(nc, k, k.h, src=k.x, w_self="We_node", bias="be")
        store_stage(nc, k, k.tab["pre"], k.h)
        segment_sums(nc, k, fast, k.tab["pre"], edge_mlp=True)
        linear_stage(nc, k, k.h, src=k.x, w_self="Wn_self", bias="bn", w_agg="Wn_agg", w_first="We_out",
                     degree_row=True, relu=True)
        norm_stage(nc, k, k.h, tables=[k.tab["x3"]])
        linear_stage(nc, k, k.h, src=k.x, w_self="W3_bwd", bias="zero")
        store_stage(nc, k, k.tab["t3"], k.h)
        segment_sums(nc, k, fast, k.tab["x3"])
        with nc.If(fast):
            reverse_pass(nc, k, k.tab["t3"])
        with nc.Else():
            general_pass(nc, k, k.tab["t3"], "src")
        gather_partials(nc, k, k.h, False)
        scale_stage(nc, k, k.h, k.rdeg["src"])
        linear_stage(nc, k, k.y, w_agg="W3_fwd", scale=k.rdeg["dst"], plus=k.h, relu=True)
        norm_stage(nc, k, k.y, out=out)


ROWS.append("zero")


def kernel(x, src, dst, edge_attr_64, L0_gnn_W, L0_gnn_b, L0_gnn_gamma, L0_gnn_beta, L1_gnn_w1_l, L1_gnn_b1,
           L1_gnn_w1_r, L1_gnn_w2_l, L1_gnn_b2, L1_gnn_w2_r, L1_gnn_w_lin, L1_gnn_b_lin, L2_gnn_W1, L2_gnn_b1,
           L2_gnn_W2, L2_gnn_b2, L2_gnn_W3, L2_gnn_b3, L3_gnn_W):
    import concourse.bacc as bacc
    from concourse.bass_utils import run_bass_kernel_spmd

    def padded(a, rows, fill=0):
        return np.concatenate([a, np.full((rows - a.shape[0],) + a.shape[1:], fill, a.dtype)])

    def pieces(a):
        return np.asarray(a)

    src, dst = padded(pieces(src), EP, N), padded(pieces(dst), EP, N)
    s3, d3 = src.reshape(NG, GROUP, P), dst.reshape(NG, GROUP, P)
    attr = padded(pieces(edge_attr_64), EP).reshape(EP // (2 * P), 2, P, D)
    l0, l3, e1, e3 = (pieces(a) for a in (L0_gnn_W, L3_gnn_W, L2_gnn_W1, L2_gnn_W3))
    t = lambda a: pieces(a).T
    mats = {"W0_self": l0[:D], "W0_agg": l0[D:], "W1_agg": t(L1_gnn_w1_l), "W1_self": t(L1_gnn_w1_r),
            "W2_agg": t(L1_gnn_w2_l), "W2_self": t(L1_gnn_w2_r), "Wlin": t(L1_gnn_w_lin),
            "We_node": e1[:D], "We_edge": e1[D:], "We_out": pieces(L2_gnn_W2), "Wn_self": e3[:D],
            "Wn_agg": e3[D:], "W3_fwd": t(l3[:, :D]), "W3_bwd": t(l3[:, D:])}
    rows = {"b0": L0_gnn_b, "b1": L1_gnn_b1, "b2": L1_gnn_b2, "blin": L1_gnn_b_lin, "be": L2_gnn_b1,
            "be2": L2_gnn_b2, "bn": L2_gnn_b3, "gamma": L0_gnn_gamma, "beta": L0_gnn_beta,
            "zero": np.zeros(D, np.float32)}
    arrays = {
        "x": padded(pieces(x), NP),
        "cols": np.concatenate([s3.transpose(0, 2, 1), d3.transpose(0, 2, 1)], axis=2),
        "dst_all": d3.transpose(2, 0, 1).reshape(P, NG * GROUP),
        "first": d3[:, 0, 0].reshape(1, NG),
        "rows_of": np.stack([src.reshape(NG, GROUP * P), dst.reshape(NG, GROUP * P)], axis=1),
        "attr": attr.transpose(1, 3, 0, 2).reshape(P, EP // 2),
        "mats": np.concatenate([mats[m] for m in MATS], axis=1),
        "rows": np.stack([pieces(rows[r]) for r in ROWS])[None],
        "be2_col": pieces(L2_gnn_b2).reshape(D, 1),
    }
    nc = bacc.Bacc("TRN2", target_bir_lowering=False, num_devices=1)
    ins, feed = {}, {}
    for name, a in arrays.items():
        feed[f"in_{name}"] = np.ascontiguousarray(a)
        ins[name] = nc.dram_tensor(f"in_{name}", a.shape, mybir.dt.from_np(a.dtype), kind="ExternalInput").ap()
    out = nc.dram_tensor("out", (N, D), F32, kind="ExternalOutput").ap()
    build(nc, ins, out)
    return run_bass_kernel_spmd(nc, [feed], core_ids=[0]).results[0]["out"]
```

```python
from contextlib import ExitStack, contextmanager

import numpy as np

import concourse.bass as bass
from concourse import mybir

ALU = mybir.AluOpType
ACT = mybir.ActivationFunctionType
AX = mybir.AxisListType
F32 = mybir.dt.float32
BF16 = mybir.dt.bfloat16
I32 = mybir.dt.int32

P = 128
D = 64
N = 12500
NT = -(-N // P)
NP = NT * P
LAST = N - (NT - 1) * P
CT = 7
NCH = NT // CT
CW = CT * D
CF = CT * P
E = 212500
GROUP = 8
NG = -(-E // (P * GROUP))
EP = NG * GROUP * P
WINDOW = 128
RING = 4
SLOTS = 16
BODIES = NG // SLOTS
COPIES = 4
ZERO_DMAS = COPIES + 1
NS = NP + P
BN_EPS = 1e-5
LN_EPS = 1e-5
L2_EPS = 1e-12
assert NT % CT == 0 and NG % SLOTS == 0 and SLOTS % RING == 0 and CW <= 512 and BODIES == NCH - 1

MATS = ["W0_self", "W0_agg", "W1_agg", "W1_self", "W2_agg", "W2_self", "Wlin", "We_node", "We_edge",
        "We_out", "Wn_self", "Wn_agg", "W3_fwd", "W3_bwd"]
ROWS = ["b0", "b1", "b2", "blin", "be", "be2", "bn", "gamma", "beta"]


class Kit:
    pass


def alloc(nc, ctx, ins):
    k = Kit()
    k.ins = ins

    def sb(name, shape, dt=F32):
        return ctx.enter_context(nc.sbuf_tensor(name, shape, dt))

    k.acc = sb("acc", [D + 1, NP + WINDOW])
    k.x = sb("x_nm", [P, NT * D])
    k.h = sb("h_nm", [P, NT * D])
    k.y = sb("y_nm", [P, NT * D])
    k.w = sb("work_nm", [P, NT * D])
    k.gath = [sb(f"gath{b}", [P, GROUP, D + 1]) for b in range(RING)]
    k.oneh = [sb(f"oneh{b}", [P, GROUP, WINDOW]) for b in range(2)]
    k.idx = [sb(f"idx{b}", [P, 2 * GROUP], I32) for b in range(RING)]
    k.first = [sb(f"first{b}", [P, 1], I32) for b in range(RING)]
    k.local = [sb(f"local{b}", [P, GROUP]) for b in range(RING)]
    k.hilo = [sb(f"hilo{b}", [P, 4, GROUP]) for b in range(2)]
    k.hilo_i = [sb(f"hilo_i{b}", [P, 4, GROUP], I32) for b in range(2)]
    k.xT = [sb(f"xT{b}", [D + 1, CF]) for b in range(2)]
    k.sT = [sb("sT", [D, CF])]
    k.agg_count = sb("agg_count", [D + 1, D + 1])
    k.chunk = [sb(f"chunk{j}", [P, CW]) for j in range(4)]
    k.sums = sb("sums", [P, CW])
    k.parts = k.h[:, 0:COPIES * CW].rearrange("p (n c) -> p n c", n=COPIES)
    k.stat = [sb(f"stat{j}", [P, CT]) for j in range(4)]
    k.zero = sb("zero", [P, D])
    k.mats = sb("mats", [P, len(MATS) * D])
    k.rows = sb("rows", [1, len(ROWS) * D])
    k.gamma = sb("gamma", [P, D])
    k.beta = sb("beta", [P, D])
    k.be2col = sb("be2col", [D, 1])
    k.be2w = sb("be2w", [P, D])
    k.iota = sb("iota", [P, P])
    k.ident = sb("ident", [P, P])
    k.lower = sb("lower", [P, P], BF16)
    k.ones = sb("ones", [P, P])
    k.mask = sb("mask", [P, 1])
    k.spare = sb("spare", [P, 1])
    k.flag = sb("flag", [1, 1], I32)
    k.deg = {s: sb(f"deg_{s}", [P, NT]) for s in ("src", "dst")}
    k.rdeg = {s: sb(f"rdeg_{s}", [P, NT]) for s in ("src", "dst")}
    k.small = [sb(f"small{j}", [P, P]) for j in range(3)]

    k.tab = {n: nc.dram_tensor(f"table_{n}", [NS if n == "x3" else NP, D], F32).ap()
             for n in ("x1", "h1", "pre", "x3")}
    k.part = [nc.dram_tensor(f"partial{c}", [NS, D], F32).ap() for c in range(COPIES)]
    return k


def mat(k, name, part=0):
    c = MATS.index(name) * D
    return k.mats[part:part + D, c:c + D]


def bias_row(k, name):
    c = ROWS.index(name) * D
    return k.rows[0:1, c:c + D].unsqueeze(1).to_broadcast([1, CT, D])


def nm3(t):
    return t[:, :].rearrange("p (t f) -> p t f", f=D)


def over_features(t, n=NT):
    return t.unsqueeze(2).to_broadcast([P, n, D])


def over_tiles(t, n=NT):
    return t.unsqueeze(1).to_broadcast([P, n, D])


def dram_nm(t, rows=NP):
    return t[0:rows, :].rearrange("(t p) f -> p t f", p=P)


def psum(nc, ctx, name, cols=512, parts=P):
    return ctx.enter_context(nc.psum_tensor(name, [parts, cols], F32, allow_name_mangling=True))


@contextmanager
def stage(nc):
    held = []

    def sem(name):
        held.append(nc.alloc_semaphore(f"{name}_{nc.next_id()}"))
        return held[-1]

    with ExitStack() as ctx:
        yield ctx, sem
    nc.gpsimd.dma_reset()
    for s in held:
        nc.gpsimd.sem_clear(s)
    nc.all_engine_barrier()
    for s in held:
        nc.release_semaphore(s)



def setup_stage(nc, k):
    ins = k.ins
    with stage(nc) as (ctx, sem):
        ps = psum(nc, ctx, "setup_ps")
        loaded, consts, step, summed, folded = (
            sem("setup_loaded"), sem("setup_consts"), sem("setup_step"), sem("setup_summed"), sem("setup_folded"))
        dst_all = k.h[:, 0:NG * GROUP].bitcast(I32)
        first_all = k.h[:, NG * GROUP:NG * GROUP + NG].bitcast(I32)
        past = k.w[:, 0:NG].rearrange("p (j u) -> p j u", u=SLOTS)
        dist = k.y[:, 0:NG * GROUP].rearrange("p (g t) -> p g t", t=GROUP)
        block = ctx.enter_context(nc.Block())
        n_loads = 8

        @block.sync
        def _(sp):
            sp.dma_start(dst_all, ins["dst_all"]).then_inc(loaded, 16)
            sp.dma_start(first_all, ins["first"].to_broadcast([P, NG])).then_inc(loaded, 16)
            sp.dma_start(k.mats[0:D, :], ins["mats"]).then_inc(loaded, 16)
            sp.dma_start(k.mats[D:P, :], ins["mats"]).then_inc(loaded, 16)
            sp.dma_start(k.rows[:, :], ins["rows"].rearrange("o r f -> o (r f)")).then_inc(loaded, 16)
            for name, tile in (("gamma", k.gamma), ("beta", k.beta)):
                r = ROWS.index(name)
                sp.dma_start(tile[:, :], ins["rows"][0, r:r + 1, :].to_broadcast([P, D])).then_inc(loaded, 16)
            sp.dma_start(k.be2col[:, :], ins["be2_col"]).then_inc(loaded, 16)

        @block.gpsimd
        def _(pool):
            pool.iota(k.iota[:, :], [[1, P]], base=0, channel_multiplier=0,
                      allow_small_or_imprecise_dtypes=True).then_inc(consts, 1)
            pool.iota(past[:, 0:BODIES - 1, :], [[CF, BODIES - 1], [0, SLOTS]], base=0, channel_multiplier=0,
                      allow_small_or_imprecise_dtypes=True).then_inc(consts, 1)
            pool.iota(past[:, BODIES - 1, :].rearrange("p (h u) -> p h u", h=2), [[CF, 2], [0, SLOTS // 2]],
                      base=CF * (BODIES - 1), channel_multiplier=0,
                      allow_small_or_imprecise_dtypes=True).then_inc(consts, 1)
            pool.iota(k.spare[:, :], [[0, 1]], base=NP, channel_multiplier=1,
                      allow_small_or_imprecise_dtypes=True).then_inc(consts, 1)

        @block.vector
        def _(dve):
            n = [0]

            def link(ins_):
                n[0] += 1
                ins_.then_inc(step, 1)
                dve.wait_ge(step, n[0])

            dve.memset(k.zero[:, :], 0.0)
            for b in range(RING):
                dve.memset(k.gath[b][:, :, D:D + 1], 1.0)
            link(dve.memset(k.agg_count[:, :], 0.0))
            dve.memset(k.agg_count[D:D + 1, D:D + 1], 1.0)
            dve.memset(k.ones[:, :], 1.0).then_inc(folded, 1)
            dve.wait_ge(consts, 4)
            link(dve.tensor_scalar(k.small[0][:, 0:1], k.spare[:, :], float(NP), None, ALU.subtract))
            dve.tensor_scalar(k.ident[:, :], k.iota[:, :], k.small[0][:, 0:1], None, ALU.is_equal)
            dve.tensor_scalar(k.lower[:, :], k.iota[:, :], k.small[0][:, 0:1], None, ALU.is_lt)
            dve.tensor_scalar(k.mask[:, :], k.small[0][:, 0:1], float(LAST), None, ALU.is_lt)
            dve.wait_ge(loaded, 16 * n_loads)
            dve.tensor_copy(k.agg_count[0:D, 0:D], mat(k, "W0_agg"))
            link(dve.tensor_tensor(dist, dst_all.rearrange("p (g t) -> p g t", t=GROUP),
                                   first_all.unsqueeze(2).to_broadcast([P, NG, GROUP]), ALU.subtract))
            link(dve.tensor_reduce(k.small[0][:, 1:2], k.y[:, 0:NG * GROUP], AX.X, ALU.max))
            link(dve.tensor_reduce(k.small[0][:, 2:3], k.y[:, 0:NG * GROUP], AX.X, ALU.min))
            link(dve.tensor_scalar(k.small[0][:, 3:4], k.small[0][:, 1:2], float(WINDOW), None, ALU.is_lt))
            link(dve.tensor_scalar(k.small[0][:, 4:5], k.small[0][:, 2:3], 0.0, None, ALU.is_ge))
            link(dve.tensor_tensor(k.small[0][:, 5:6], k.small[0][:, 3:4], k.small[0][:, 4:5], ALU.mult))
            link(dve.tensor_tensor(k.w[:, NG:2 * NG], first_all, k.w[:, 0:NG], ALU.subtract))
            link(dve.tensor_reduce(k.small[0][:, 6:7], k.w[:, NG:2 * NG], AX.X, ALU.min))
            link(dve.tensor_scalar(k.small[0][:, 7:8], k.small[0][:, 6:7], 0.0, None, ALU.is_ge))
            dve.tensor_tensor(k.small[1][:, 0:1], k.small[0][:, 5:6], k.small[0][:, 7:8],
                              ALU.mult).then_inc(folded, 1)
            dve.tensor_copy(k.small[2][0:D, :], k.be2col[:, 0:1].to_broadcast([D, P])).then_inc(folded, 1)
            dve.wait_ge(summed, 2)
            dve.tensor_scalar(k.flag[:, :], ps[0:1, 0:1], float(P), None, ALU.is_ge)
            dve.tensor_copy(k.be2w[:, :], ps[:, D:2 * D])

        @block.tensor
        def _(pe):
            pe.wait_ge(folded, 3)
            pe.matmul(ps[0:1, 0:1], k.small[1][:, 0:1], k.ones[:, 0:1], start=True, stop=True).then_inc(summed, 1)
            pe.matmul(ps[:, D:2 * D], k.small[2][0:D, :], mat(k, "Wn_agg"), start=True,
                      stop=True).then_inc(summed, 1)



def degree_onehots(dve, k, b, ring, sems, value, sides):
    idx = k.idx[ring]
    hi_i, f = k.hilo_i[b % 2], k.hilo[b % 2]
    for s in range(sides):
        col = idx[:, s * GROUP:(s + 1) * GROUP]
        dve.tensor_scalar(hi_i[:, s, :], col, P - 1, None, ALU.bitwise_and)
        last = dve.tensor_scalar(hi_i[:, 2 + s, :], col, 7, None, ALU.logical_shift_right)
    last.then_inc(sems.step, 1)
    dve.wait_ge(sems.step, value(1))
    for s in range(sides):
        last = dve.tensor_copy(f[:, s::2, :], hi_i[:, s::2, :])
    last.then_inc(sems.step, 1)
    dve.wait_ge(sems.step, value(2))
    low, high = degree_views(k, b % 2)
    for s in range(sides):
        dve.tensor_tensor(low[s], k.iota[:, :].unsqueeze(1).to_broadcast([P, GROUP, P]),
                          f[:, s, :].unsqueeze(2).to_broadcast([P, GROUP, P]), ALU.is_equal)
        last = dve.tensor_tensor(high[s], k.iota[:, 0:NT].unsqueeze(1).to_broadcast([P, GROUP, NT]),
                                 f[:, 2 + s, :].unsqueeze(2).to_broadcast([P, GROUP, NT]), ALU.is_equal)
    last.then_inc(sems.deg_ready[b % 2], 1)


def degree_views(k, b):
    words = k.w[:, :].bitcast(BF16)
    size = GROUP * (P + NT)
    low, high = [], []
    for s in range(2):
        at = (2 * b + s) * size
        low.append(words[:, at:at + GROUP * P].rearrange("p (t c) -> p t c", t=GROUP))
        high.append(words[:, at + GROUP * P:at + size].rearrange("p (t c) -> p t c", t=GROUP))
    return low, high


def degree_zero(pe, k, ps_deg, first):
    for s in range(len(ps_deg)):
        ins_ = pe.matmul(ps_deg[s][:, 0:NT], k.zero[:, :].bitcast(BF16), k.lower[:, 0:NT], start=first,
                         stop=not first)
    return ins_


def degree_matmuls(pe, k, b, ps_deg):
    low, high = degree_views(k, b % 2)
    for t in range(GROUP):
        for s in range(len(ps_deg)):
            ins_ = pe.matmul(ps_deg[s][:, 0:NT], low[s][:, t, :], high[s][:, t, :],
                             start=False, stop=False)
    return ins_


class Names:
    pass


def finish_degrees(dve, k, ps_deg, done, base):
    for s, name in enumerate(("src", "dst")[:len(ps_deg)]):
        dve.tensor_copy(k.deg[name][:, :], ps_deg[s][:, 0:NT])
        dve.tensor_scalar(k.rdeg[name][:, :], ps_deg[s][:, 0:NT], 1.0, None, ALU.max).then_inc(done, 1)
        dve.wait_ge(done, base + 2 * s + 1)
        dve.reciprocal(k.rdeg[name][:, :], k.rdeg[name][:, :]).then_inc(done, 1)
        dve.wait_ge(done, base + 2 * s + 2)


def degree_stage(nc, k):
    with stage(nc) as (ctx, sem):
        sems = Names()
        idx_ready = [sem(f"deg_idx_ready{b}") for b in range(2)]
        sems.step = sem("deg_step")
        sems.deg_ready = [sem(f"deg_onehot_ready{b}") for b in range(2)]
        counted = [sem(f"deg_counted{b}") for b in range(2)]
        done = sem("deg_done")
        ps_deg = [psum(nc, ctx, f"deg_ps{s}") for s in range(2)]
        block = ctx.enter_context(nc.Block())
        n = NG // 2

        @block.sync
        def _(sp):
            for b in range(2):
                sp.dma_start(k.idx[b][:, :], k.ins["cols"][b]).then_inc(idx_ready[b], 16)
            with sp.Fori(1, n) as i:
                for b in range(2):
                    sp.wait_ge(sems.deg_ready[b], i)
                    sp.dma_start(k.idx[b][:, :], group_cols(k, 2 * i + b)).then_inc(idx_ready[b], 16)

        @block.vector
        def _(dve):
            with dve.Fori(0, n) as i:
                for b in range(2):
                    dve.wait_ge(idx_ready[b], i * 16 + 16)
                    dve.wait_ge(counted[b], i + 1)
                    degree_onehots(dve, k, b, b, sems, lambda j: i * 4 + 2 * b + j, 2)
            for b in range(2):
                dve.wait_ge(counted[b], n + 1 + b)
            finish_degrees(dve, k, ps_deg, done, 0)

        @block.tensor
        def _(pe):
            for b in range(2):
                pe.sem_inc(counted[b])
            degree_zero(pe, k, ps_deg, True)
            with pe.Fori(0, n) as i:
                for b in range(2):
                    pe.wait_ge(sems.deg_ready[b], i + 1)
                    degree_matmuls(pe, k, b, ps_deg).then_inc(counted[b], 1)
            degree_zero(pe, k, ps_deg, False).then_inc(counted[1], 1)


def zero_partials(eng, k, zeroed):
    for c in range(COPIES):
        eng.dma_start(dram_nm(k.part[c], NS), k.zero[:, :].unsqueeze(1).to_broadcast([P, NT + 1, D])
                      ).then_inc(zeroed, 16)
    eng.dma_start(k.tab["x3"][NP:NS, :], k.zero[:, :]).then_inc(zeroed, 16)


def zero_stage(nc, k):
    with stage(nc) as (ctx, sem):
        zeroed, x_loaded = sem("z_zeroed"), sem("z_x_loaded")
        block = ctx.enter_context(nc.Block())

        @block.sync
        def _(sp):
            sp.dma_start(nm3(k.x), dram_nm(k.ins["x"])).then_inc(x_loaded, 16)
            sp.wait_ge(x_loaded, 16)

        @block.scalar
        def _(act):
            zero_partials(act, k, zeroed)
            act.wait_ge(zeroed, 16 * ZERO_DMAS)


def group_cols(k, g):
    return k.ins["cols"][bass.ds(g, 1)].rearrange("o p c -> (o p) c")


def group_first(k, g):
    return k.ins["first"][0:1, bass.ds(g, 1)].to_broadcast([P, 1])


halves = [t % 2 * (GROUP // 2) + t // 2 for t in range(GROUP)]


def attr_matmuls(pe, k, ps, attr):
    for t in range(GROUP):
        h, q = t % 2, t // 2
        mm = pe.matmul(ps[:, h * 512 + q * D:h * 512 + (q + 1) * D],
                       attr[h * D:(h + 1) * D, q * P:(q + 1) * P],
                       mat(k, "We_edge", h * D), start=True, stop=True)
    return mm


def attr_sum(dve, out, ps, rows):
    return dve.tensor_tensor(
        out.rearrange("p (h q f) -> p h q f", h=2, f=D),
        ps[:, :].rearrange("p (h q f) -> p h q f", h=2, f=D)[:, :, 0:GROUP // 2, :],
        rows[:, :, 0:D].rearrange("p (q h) f -> p h q f", h=2), ALU.add)


def after(eng, sem, value):
    if not isinstance(value, int) or value > 0:
        eng.wait_ge(sem, value)


def fast_pass(nc, k, table, layer):
    degrees, edge_mlp = layer == "mean", layer == "edge"
    with stage(nc) as (ctx, sem):
        idx_ready = [sem(f"idx_ready{b}") for b in range(RING)]
        gathered = [sem(f"gathered{b}") for b in range(RING)]
        onehot_ready = [sem(f"onehot_ready{b}") for b in range(RING)]
        segmented = [sem(f"segmented{b}") for b in range(RING)]
        added = [sem(f"added{b}") for b in range(RING)]
        attr_ready = [sem(f"attr_ready{b}") for b in range(2)]
        attr_mm, mlp_sum = sem("attr_mm"), sem("mlp_sum")
        message = [sem(f"message{b}") for b in range(2)]
        counted = [sem(f"counted{b}") for b in range(2)]
        local_ready, cleared, done, x_loaded = sem("local_ready"), sem("cleared"), sem("deg_done"), sem("x_loaded")
        go, go_pe, go_sp = sem("pool_go"), sem("pe_go"), sem("sp_go")
        sems = Names()
        sems.step = sem("deg_step")
        sems.deg_ready = [sem(f"deg_ready{b}") for b in range(2)]
        wide = D + degrees
        ps_seg = [psum(nc, ctx, f"ps_seg{b}", parts=D + 1) for b in range(2)]
        work = NodeWork(nc, k, ctx, sem, layer, counting=degrees)
        if degrees:
            ps_deg = [psum(nc, ctx, "ps_deg")]
        if edge_mlp:
            ps_attr = psum(nc, ctx, "ps_attr", 1024)
            half = GROUP // 2
            attr = [k.w[:, b * half * P:(b + 1) * half * P] for b in range(2)]
            hid, msg = [[k.w[:, (2 * n + b) * GROUP * D:(2 * n + b + 1) * GROUP * D] for b in range(2)]
                        for n in (1, 2)]
        block = ctx.enter_context(nc.Block())

        def uses(j, u, n):
            return j * (SLOTS // n) + u // n

        def no_chunk(u):
            return ()

        def one_chunk(c):
            return lambda u: ((c, u),)

        def two_chunks(u):
            c, half_slot = BODIES - 2 + 2 * u // SLOTS, u % (SLOTS // 2)
            return ((c, 2 * half_slot), (c, 2 * half_slot + 1))

        @block.sync
        def _(sp):
            def body(j):
                for u in range(SLOTS):
                    b, n, g = u % RING, uses(j, u, RING), j * SLOTS + u
                    after(sp, gathered[b], n * (16 * GROUP))
                    after(sp, added[b], n)
                    sp.sem_inc(go_sp)
                    if edge_mlp:
                        after(sp, attr_mm, g - 1 if isinstance(j, int) else j * SLOTS + (u - 1))
                        sp.sem_inc(go_sp)
                        sp.dma_start(attr[u % 2], k.ins["attr"][:, bass.ds(g * (GROUP // 2 * P), GROUP // 2 * P)]
                                     ).then_inc(attr_ready[u % 2], 16)
                    sp.dma_start(k.idx[b][:, :], group_cols(k, g)).then_inc(idx_ready[b], 16)
                    sp.dma_start(k.first[b][:, :], group_first(k, g)).then_inc(idx_ready[b], 16)

            body(0)
            if degrees:
                sp.dma_start(nm3(k.x), dram_nm(k.ins["x"])).then_inc(x_loaded, 16)
            with sp.Fori(1, BODIES) as j:
                body(j)

        @block.gpsimd
        def _(pool):
            def body(j):
                for u in range(SLOTS):
                    b, n = u % RING, uses(j, u, RING)
                    pool.wait_ge(idx_ready[b], n * 32 + 32)
                    after(pool, segmented[b], n)
                    pool.sem_inc(go)
                    for t in range(GROUP):
                        pool.indirect_dma_start(
                            k.gath[b][:, t, 0:D], None, table[0:NP, :],
                            bass.IndirectOffsetOnAxis(ap=k.idx[b][:, t:t + 1], axis=0)
                        ).then_inc(gathered[b], 16)

            body(0)
            with pool.Fori(1, BODIES) as j:
                body(j)
            for b in range(RING):
                pool.wait_ge(gathered[b], NG // RING * 16 * GROUP)

        @block.vector
        def _(dve):
            def body(j, steps=no_chunk):
                for u in range(SLOTS):
                    b, n = u % RING, uses(j, u, RING)
                    dve.wait_ge(idx_ready[b], n * 32 + 32)
                    dve.tensor_tensor(k.local[b][:, :], k.idx[b][:, GROUP:2 * GROUP],
                                      k.first[b][:, 0:1].to_broadcast([P, GROUP]), ALU.subtract
                                      ).then_inc(local_ready, 1)
                    dve.wait_ge(local_ready, j * SLOTS + u + 1)
                    dve.tensor_tensor(k.oneh[u % 2][:, :, :],
                                      k.iota[:, :].unsqueeze(1).to_broadcast([P, GROUP, WINDOW]),
                                      k.local[b][:, :].unsqueeze(2).to_broadcast([P, GROUP, WINDOW]),
                                      ALU.is_equal).then_inc(onehot_ready[b], 1)
                    if degrees:
                        after(dve, counted[u % 2], uses(j, u, 2))
                        degree_onehots(dve, k, u, b, sems, lambda m: (j * SLOTS + u) * 2 + m, 1)
                    if edge_mlp:
                        dve.wait_ge(gathered[b], n * (16 * GROUP) + 16 * GROUP)
                        dve.wait_ge(attr_mm, j * SLOTS + u + 1)
                        attr_sum(dve, hid[u % 2], ps_attr, k.gath[b]).then_inc(mlp_sum, 1)
                    if u > 0:
                        add(u - 1, uses(j, u - 1, RING) + 1)
                    elif not isinstance(j, int) or j > 0:
                        add(SLOTS - 1, j * (SLOTS // RING))
                    for c, step in steps(u):
                        work.vector(dve, c, step)

            def add(u, count):
                b = u % RING
                at = dve.value_load(k.first[b][0:1, 0:1], min_val=0, max_val=NP)
                dve.wait_ge(segmented[b], count)
                window = k.acc[0:wide, bass.ds(at, WINDOW)]
                dve.tensor_tensor(window, window, ps_seg[u % 2][0:wide, 0:WINDOW], ALU.add).then_inc(added[b], 1)
                dve.wait_ge(added[b], count)

            dve.memset(k.acc[:, :], 0.0).then_inc(cleared, 1)
            dve.wait_ge(cleared, 1)
            work.vector_start(dve)
            body(0)
            if degrees:
                dve.wait_ge(x_loaded, 16)
            with dve.Fori(0, BODIES - 2) as c:
                body(c + 1, one_chunk(c))
            body(BODIES - 1, two_chunks)
            add(SLOTS - 1, NG // RING)
            for u in range(SLOTS):
                work.vector(dve, NCH - 1, u)
            if degrees:
                for b in range(2):
                    dve.wait_ge(counted[b], NG // 2 + b)
                finish_degrees(dve, k, ps_deg, done, 0)

        @block.scalar
        def _(act):
            def body(j, steps=no_chunk):
                for u in range(SLOTS):
                    if edge_mlp:
                        act.wait_ge(mlp_sum, j * SLOTS + u + 1)
                        act.activation(msg[u % 2], hid[u % 2], ACT.Relu).then_inc(message[u % 2], 1)
                    for c, step in steps(u):
                        if step == 0:
                            act.wait_ge(added[RING - 1], uses(j, u, RING))
                        work.scalar(act, c, step)

            work.scalar_start(act)
            if edge_mlp:
                body(0)
            if degrees:
                act.wait_ge(x_loaded, 16)
            with act.Fori(0, BODIES - 2) as c:
                body(c + 1, one_chunk(c))
            body(BODIES - 1, two_chunks)
            act.wait_ge(added[RING - 1], NG // RING)
            for u in range(SLOTS):
                work.scalar(act, NCH - 1, u)
            work.scalar_end(act)

        @block.tensor
        def _(pe):
            def body(j, steps=no_chunk):
                for u in range(SLOTS):
                    b, n = u % RING, uses(j, u, RING)
                    if edge_mlp:
                        pe.wait_ge(attr_ready[u % 2], uses(j, u, 2) * 16 + 16)
                        after(pe, mlp_sum, j * SLOTS + u)
                        pe.sem_inc(go_pe)
                        attr_matmuls(pe, k, ps_attr, attr[u % 2]).then_inc(attr_mm, 1)
                        pe.wait_ge(message[u % 2], uses(j, u, 2) + 1)
                        rows, place = msg[u % 2].rearrange("p (t f) -> p t f", f=D), halves
                    else:
                        pe.wait_ge(gathered[b], n * (16 * GROUP) + 16 * GROUP)
                        rows, place = k.gath[b], range(GROUP)
                    pe.wait_ge(onehot_ready[b], n + 1)
                    after(pe, added[(u - 2) % RING], n + 1 if u % RING >= 2 else n)
                    for t in range(GROUP):
                        mm = pe.matmul(ps_seg[u % 2][0:wide, 0:WINDOW], rows[:, place[t], 0:wide], k.oneh[u % 2][:, t, :],
                                       start=t == 0, stop=t == GROUP - 1)
                    mm.then_inc(segmented[b], 1)
                    if degrees:
                        pe.wait_ge(sems.deg_ready[u % 2], uses(j, u, 2) + 1)
                        degree_matmuls(pe, k, u, ps_deg).then_inc(counted[u % 2], 1)
                    for c, step in steps(u):
                        work.tensor(pe, c, step)

            work.tensor_start(pe)
            if degrees:
                degree_zero(pe, k, ps_deg, True)
            body(0)
            with pe.Fori(0, BODIES - 2) as c:
                body(c + 1, one_chunk(c))
            body(BODIES - 1, two_chunks)
            if degrees:
                degree_zero(pe, k, ps_deg, False).then_inc(counted[1], 1)
            for u in range(SLOTS):
                work.tensor(pe, NCH - 1, u)


def equality(dve, k, eq, srow, col, low, cnt, sidx, link):
    link(dve.tensor_tensor(eq, srow, col.unsqueeze(2).to_broadcast([P, GROUP, P]), ALU.is_equal))
    link(dve.tensor_tensor(low, eq, k.lower[:, :].unsqueeze(1).to_broadcast([P, GROUP, P]), ALU.mult))
    link(dve.tensor_reduce(cnt[:, 0:GROUP], low, AX.X, ALU.add))
    link(dve.tensor_scalar(cnt[:, GROUP:2 * GROUP], cnt[:, 0:GROUP], 0.5, None, ALU.is_lt))
    link(dve.tensor_scalar(cnt[:, 2 * GROUP:3 * GROUP], col, k.spare[:, 0:1], None, ALU.subtract))
    link(dve.tensor_tensor(cnt[:, 3 * GROUP:4 * GROUP], cnt[:, 2 * GROUP:3 * GROUP],
                           cnt[:, GROUP:2 * GROUP], ALU.mult))
    return dve.tensor_scalar(sidx, cnt[:, 3 * GROUP:4 * GROUP], k.spare[:, 0:1], None, ALU.add)


EQ_STEPS = 6


def general_pass(nc, k, table, by, edge_mlp=False):
    gather_at, scatter_at = (0, GROUP) if by == "dst" else (GROUP, 0)
    row_of = 1 if by == "dst" else 0
    with stage(nc) as (ctx, sem):
        loaded, gathered, step, ready = sem("g_loaded"), sem("g_gathered"), sem("g_step"), sem("g_ready")
        attr_mm, mlp_sum, message = sem("g_attr_mm"), sem("g_mlp_sum"), sem("g_message")
        combined, copied, go = sem("g_combined"), sem("g_copied"), sem("g_go")
        scattered = [sem(f"g_scattered{c}") for c in range(COPIES)]
        go_pe, go_sp = sem("g_pe_go"), sem("g_sp_go")
        ps_c = psum(nc, ctx, "g_ps_c")
        ps_a = psum(nc, ctx, "g_ps_a", 1024)
        wcol = lambda a, n: k.w[:, a:a + n]
        eq = wcol(1024, 1024).rearrange("p (t c) -> p t c", c=P)
        low = wcol(2048, 1024).rearrange("p (t c) -> p t c", c=P)
        attr = wcol(3072, 512)
        hid, msg = wcol(3584, 512), wcol(4096, 512)
        cnt = wcol(4608, 64)
        sidx = wcol(4672, GROUP).bitcast(I32)
        comb = k.gath[1]
        per = (3 if edge_mlp else 2) * 16
        block = ctx.enter_context(nc.Block())
        each = 16 * GROUP // COPIES

        @block.sync
        def _(sp):
            def load(g):
                sp.dma_start(k.idx[0][:, :], group_cols(k, g)).then_inc(loaded, 16)
                sp.dma_start(wcol(0, GROUP * P).bitcast(I32),
                             k.ins["rows_of"][bass.ds(g, 1), row_of, :].to_broadcast([P, GROUP * P])
                             ).then_inc(loaded, 16)
                if edge_mlp:
                    sp.dma_start(attr, k.ins["attr"][:, bass.ds(g * (GROUP // 2 * P), GROUP // 2 * P)]
                                 ).then_inc(loaded, 16)

            load(0)
            with sp.Fori(1, NG) as g:
                for c in range(COPIES):
                    sp.wait_ge(scattered[c], g * each)
                sp.sem_inc(go_sp)
                load(g)
            for c in range(COPIES):
                sp.wait_ge(scattered[c], NG * each)

        @block.gpsimd
        def _(pool):
            with pool.Fori(0, NG) as g:
                pool.wait_ge(loaded, g * per + per)
                pool.sem_inc(go)
                for t in range(GROUP):
                    pool.indirect_dma_start(
                        k.gath[0][:, t, 0:D], None, table[0:NP, :],
                        bass.IndirectOffsetOnAxis(ap=k.idx[0][:, gather_at + t:gather_at + t + 1], axis=0)
                    ).then_inc(gathered, 16)
                pool.wait_ge(ready, g + 1)
                pool.wait_ge(copied, g + 1)
                pool.sem_inc(go)
                for t in range(GROUP):
                    c = t % COPIES
                    if t >= COPIES:
                        pool.wait_ge(scattered[c], g * each + 16 * (t // COPIES))
                        pool.sem_inc(go)
                    pool.indirect_dma_start(
                        k.part[c], bass.IndirectOffsetOnAxis(ap=sidx[:, t:t + 1], axis=0),
                        comb[:, t, 0:D], None, compute_op=ALU.add).then_inc(scattered[c], 16)
            pool.wait_ge(gathered, NG * 16 * GROUP)
            for c in range(COPIES):
                pool.wait_ge(scattered[c], NG * each)

        @block.vector
        def _(dve):
            with dve.Fori(0, NG) as g:
                n = [0]

                def link(ins_):
                    n[0] += 1
                    ins_.then_inc(step, 1)
                    dve.wait_ge(step, g * EQ_STEPS + n[0])

                dve.wait_ge(loaded, g * per + per)
                equality(dve, k, eq, wcol(0, GROUP * P).bitcast(I32).rearrange("p (t c) -> p t c", c=P),
                         k.idx[0][:, scatter_at:scatter_at + GROUP], low, cnt, sidx, link).then_inc(ready, 1)
                assert n[0] == EQ_STEPS
                if edge_mlp:
                    dve.wait_ge(gathered, g * (16 * GROUP) + 16 * GROUP)
                    dve.wait_ge(attr_mm, g + 1)
                    attr_sum(dve, hid, ps_a, k.gath[0]).then_inc(mlp_sum, 1)

        @block.scalar
        def _(act):
            with act.Fori(0, NG) as g:
                if edge_mlp:
                    act.wait_ge(mlp_sum, g + 1)
                    act.activation(msg, hid, ACT.Relu).then_inc(message, 1)
                act.wait_ge(combined, g + 1)
                act.copy(comb[:, :, 0:D], ps_c[:, :].rearrange("p (t f) -> p t f", f=D)).then_inc(copied, 1)

        @block.tensor
        def _(pe):
            with pe.Fori(0, NG) as g:
                if edge_mlp:
                    pe.wait_ge(loaded, g * per + per)
                    pe.sem_inc(go_pe)
                    attr_matmuls(pe, k, ps_a, attr).then_inc(attr_mm, 1)
                    pe.wait_ge(message, g + 1)
                    rows = msg.rearrange("p (t f) -> p t f", f=D)
                    place = halves
                else:
                    pe.wait_ge(gathered, g * (16 * GROUP) + 16 * GROUP)
                    rows, place = k.gath[0], range(GROUP)
                pe.wait_ge(ready, g + 1)
                for t in range(GROUP):
                    mm = pe.matmul(ps_c[:, t * D:(t + 1) * D], eq[:, t, :], rows[:, place[t], 0:D], start=True, stop=True)
                mm.then_inc(combined, 1)


def reverse_pass(nc, k, table):
    with stage(nc) as (ctx, sem):
        idx_ready = [sem(f"r_idx_ready{b}") for b in range(RING)]
        win_ready = [sem(f"r_win_ready{b}") for b in range(RING)]
        ready = [sem(f"r_ready{b}") for b in range(RING)]
        oh_ready = [sem(f"r_oh_ready{b}") for b in range(RING)]
        mixed, mix_copied, combined, copied, free = (
            sem("r_mixed"), sem("r_mix_copied"), sem("r_combined"), sem("r_copied"), sem("r_free"))
        scattered = [sem(f"r_scattered{c}") for c in range(COPIES)]
        step, go = sem("r_step"), sem("r_go")
        ps_mix = [psum(nc, ctx, f"r_ps_mix{b}", 1024) for b in range(2)]
        ps_c = [psum(nc, ctx, f"r_ps_c{b}") for b in range(2)]
        words, half = GROUP * P, GROUP * P // 2
        area = 3 * half
        onehots = lambda b, n: k.w[:, b * area + n * half:b * area + (n + 1) * half].bitcast(BF16).rearrange(
            "p (t c) -> p t c", c=P)
        eq, low, oh = ([onehots(b, n) for b in range(RING)] for n in range(3))
        srow = [k.y[:, b * words:(b + 1) * words].bitcast(I32) for b in range(RING)]
        mix = [k.h[:, b * words:(b + 1) * words] for b in range(RING)]
        win = [k.h[:, RING * words + b * D:RING * words + (b + 1) * D] for b in range(RING)]
        rest = lambda b, at, n: k.y[:, RING * words + b * 64 + at:RING * words + b * 64 + at + n]
        cnt = [rest(b, 0, 4 * GROUP) for b in range(RING)]
        sidx = [rest(b, 4 * GROUP, GROUP).bitcast(I32) for b in range(RING)]
        comb = k.gath
        each = 16 * GROUP // COPIES
        assert RING * area <= NT * D and RING * (words + D) <= NT * D
        block = ctx.enter_context(nc.Block())

        @block.sync
        def _(sp):
            def load(b, g, i):
                sp.dma_start(k.idx[b][:, :], group_cols(k, g)).then_inc(idx_ready[b], 16)
                sp.dma_start(k.first[b][:, :], group_first(k, g)).then_inc(idx_ready[b], 16)
                sp.dma_start(srow[b], k.ins["rows_of"][bass.ds(g, 1), 0, :].to_broadcast([P, words])
                             ).then_inc(idx_ready[b], 16)
                sp.wait_ge(idx_ready[b], i * 48 + 48)
                sp.sem_inc(go)
                at = sp.value_load(k.first[b][0:1, 0:1], min_val=0, max_val=NP)
                sp.dma_start(win[b], table[bass.ds(at, WINDOW), :]).then_inc(win_ready[b], 16)

            for b in range(RING):
                load(b, b, 0)
            with sp.Fori(1, NG // RING) as i:
                for b in range(RING):
                    sp.wait_ge(combined, (i - 1) * RING + b + 1)
                    sp.wait_ge(oh_ready[b], i)
                    sp.wait_ge(ready[b], i)
                    sp.sem_inc(go)
                    load(b, i * RING + b, i)
            for c in range(COPIES):
                sp.wait_ge(scattered[c], NG * each)

        @block.vector
        def _(dve):
            with dve.Fori(0, NG // RING) as i:
                for b in range(RING):
                    n = [0]

                    def link(ins_):
                        n[0] += 1
                        ins_.then_inc(step, 1)
                        dve.wait_ge(step, (i * RING + b) * (EQ_STEPS + 1) + n[0])

                    dve.wait_ge(idx_ready[b], i * 48 + 48)
                    dve.wait_ge(mixed, i * RING + b + 1)
                    dve.wait_ge(free, i * RING + b + 1)
                    link(dve.tensor_tensor(k.local[b][:, :], k.idx[b][:, GROUP:2 * GROUP],
                                           k.first[b][:, 0:1].to_broadcast([P, GROUP]), ALU.subtract))
                    dve.tensor_tensor(oh[b], k.iota[:, :].unsqueeze(1).to_broadcast([P, GROUP, P]),
                                      k.local[b][:, :].unsqueeze(2).to_broadcast([P, GROUP, P]),
                                      ALU.is_equal).then_inc(oh_ready[b], 1)
                    equality(dve, k, eq[b], srow[b].rearrange("p (t c) -> p t c", c=P),
                             k.idx[b][:, 0:GROUP], low[b], cnt[b], sidx[b], link).then_inc(ready[b], 1)

        @block.tensor
        def _(pe):
            pe.sem_inc(mixed, RING)

            def mix_of(b, i):
                pe.wait_ge(oh_ready[b], i + 1)
                pe.wait_ge(ready[b], i + 1)
                pe.wait_ge(mix_copied, i * RING + b + RING - 1)
                for t in range(GROUP):
                    mm = pe.matmul(ps_mix[b % 2][:, t * P:(t + 1) * P], oh[b][:, t, :], eq[b][:, t, :],
                                   start=True, stop=True)
                mm.then_inc(mixed, 1)

            def rows_of(b, i):
                pe.wait_ge(mix_copied, i * RING + b + RING + 1)
                pe.wait_ge(win_ready[b], i * 16 + 16)
                pe.wait_ge(copied, i * RING + b + RING - 1)
                for t in range(GROUP):
                    mm = pe.matmul(ps_c[b % 2][:, t * D:(t + 1) * D], mix[b][:, t * P:(t + 1) * P], win[b],
                                   start=True, stop=True)
                mm.then_inc(combined, 1)

            with pe.Fori(0, NG // RING) as i:
                for b in range(RING):
                    mix_of(b, i)
                    rows_of(b, i)

        @block.scalar
        def _(act):
            act.sem_inc(mix_copied, RING)
            act.sem_inc(copied, RING)
            with act.Fori(0, NG // RING) as i:
                for b in range(RING):
                    act.wait_ge(mixed, i * RING + b + RING + 1)
                    act.copy(mix[b], ps_mix[b % 2][:, :]).then_inc(mix_copied, 1)
                    act.wait_ge(combined, i * RING + b + 1)
                    act.wait_ge(free, i * RING + b + 1)
                    act.copy(comb[b][:, :, 0:D], ps_c[b % 2][:, :].rearrange("p (t f) -> p t f", f=D)
                             ).then_inc(copied, 1)

        @block.gpsimd
        def _(pool):
            pool.sem_inc(free, RING)

            def scatter(b, i):
                peeled = isinstance(i, int) and b == 0
                pool.wait_ge(ready[b], i + 1)
                pool.wait_ge(copied, i * RING + b + RING + 1)
                for t in range(GROUP):
                    c = t % COPIES
                    if not peeled or t >= COPIES:
                        pool.wait_ge(scattered[c], (i * RING + b) * each + 16 * (t // COPIES))
                        if t == COPIES - 1 and not peeled:
                            pool.sem_inc(free)
                    pool.sem_inc(go)
                    pool.indirect_dma_start(
                        k.part[c], bass.IndirectOffsetOnAxis(ap=sidx[b][:, t:t + 1], axis=0),
                        comb[b][:, t, 0:D], None, compute_op=ALU.add).then_inc(scattered[c], 16)

            for b in range(RING):
                scatter(b, 0)
            with pool.Fori(1, NG // RING) as i:
                for b in range(RING):
                    scatter(b, i)
            for c in range(COPIES):
                pool.wait_ge(scattered[c], NG * each)


def gather_partials(nc, k):
    out = k.y
    with stage(nc) as (ctx, sem):
        loaded, step, zeroed = sem("p_loaded"), sem("p_step"), sem("p_zeroed")
        turned, moved, staged, row_free = sem("p_turned"), sem("p_moved"), sem("p_staged"), sem("p_row_free")
        go = sem("p_go")
        rows = [k.chunk[b][:, :] for b in range(2)]
        ps = [psum(nc, ctx, f"p_ps{b}", 1024, parts=D) for b in range(2)]
        block = ctx.enter_context(nc.Block())

        @block.sync
        def _(sp):
            sp.dma_start(nm3(out), dram_nm(k.part[0])).then_inc(loaded, 16)
            for c in range(1, COPIES):
                if c > 1:
                    sp.wait_ge(step, c - 1)
                sp.dma_start(nm3(k.w), dram_nm(k.part[c])).then_inc(loaded, 16)
                sp.wait_ge(loaded, 16 * (c + 1))
            zero_partials(sp, k, zeroed)
            sp.wait_ge(zeroed, 16 * ZERO_DMAS)

        @block.vector
        def _(dve):
            for c in range(1, COPIES):
                dve.wait_ge(loaded, 16 * (c + 1))
                dve.tensor_tensor(out[:, :], out[:, :], k.w[:, :], ALU.add).then_inc(step, 1)
                dve.wait_ge(step, c)

        @block.gpsimd
        def _(pool):
            pool.wait_ge(step, COPIES - 1)
            with pool.Fori(0, NCH // 2) as i:
                for b in range(2):
                    pool.wait_ge(row_free, 2 * i + b + 1)
                    pool.tensor_copy(rows[b], out[:, bass.ds((2 * i + b) * CW, CW)]).then_inc(staged, 1)

        @block.tensor
        def _(pe):
            with pe.Fori(0, NCH // 2) as i:
                for b in range(2):
                    pe.wait_ge(staged, 2 * i + b + 1)
                    pe.wait_ge(moved, 2 * i + b + 1)
                    pe.sem_inc(go)
                    for j in range(CT):
                        mm = pe.transpose(ps[b][:, j * P:(j + 1) * P], rows[b][:, j * D:(j + 1) * D],
                                          k.ident[:, :])
                    mm.then_inc(turned, 1)

        @block.scalar
        def _(act):
            act.sem_inc(moved, 2)
            act.sem_inc(row_free, 2)
            with act.Fori(0, NCH // 2) as i:
                for b in range(2):
                    act.wait_ge(turned, 2 * i + b + 1)
                    act.sem_inc(row_free)
                    act.copy(k.acc[0:D, bass.ds((2 * i + b) * CF, CF)], ps[b][:, 0:CF]).then_inc(moved, 1)



LAYERS = {
    "mean": dict(source="x", self=("W0_self", "b0"), agg="W0_agg"),
    "sage1": dict(source="x", self=("W1_self", "b1"), agg="W1_agg"),
    "sage2": dict(source="h", self=("W2_self", "b2"), agg="W2_agg", then=(("Wlin", "blin"), ("We_node", "be"))),
    "edge": dict(source="x", self=("Wn_self", "bn"), agg="Wn_agg"),
    "both": dict(source="partials", self=("W3_bwd", "zero"), agg="W3_fwd"),
}
LINKS = {"mean": 14, "sage1": 2, "sage2": 11, "edge": 11, "both": 14}


class NodeWork:

    def __init__(self, nc, k, ctx, sem, layer, counting=False):
        self.k, self.layer, self.spec = k, layer, LAYERS[layer]
        self.units = 1 + len(self.spec.get("then", ()))
        self.rows_ready, self.turned, self.moved = sem("w_rows_ready"), sem("w_turned"), sem("w_moved")
        self.product, self.consumed, self.step = sem("w_product"), sem("w_consumed"), sem("w_step")
        self.loaded, self.stored, self.go = sem("w_loaded"), sem("w_stored"), sem("w_go")
        self.first_mm, self.first_moved = sem("w_first_mm"), sem("w_first_moved")
        self.var_ready, self.std_ready, self.result = sem("w_var_ready"), sem("w_std_ready"), sem("w_result")
        self.copied, self.parts_free = sem("w_copied"), sem("w_parts_free")
        self.ps_turn = psum(nc, ctx, "w_ps_turn", 1024, parts=D)
        self.ps_self, self.ps_agg = psum(nc, ctx, "w_ps_self"), psum(nc, ctx, "w_ps_agg")
        self.xT, self.sT, self.s2T = k.xT[0][0:D, :], k.xT[1], k.sT[0]
        self.rows, self.t, self.y, self.q = k.chunk
        self.n_links = 0
        self.wide = D + counting
        self.counting = counting

    def count(self, c, unit=0):
        return c * self.units + unit + 1

    def of(self, buffer, c):
        return buffer[:, bass.ds(c * CW, CW)] if not isinstance(c, int) else buffer[:, c * CW:(c + 1) * CW]

    def of_nodes(self, values, c):
        return over_features(self.part(values, c), CT)

    def part(self, values, c):
        return values[:, bass.ds(c * CT, CT)] if not isinstance(c, int) else values[:, c * CT:(c + 1) * CT]

    def dram(self, table, c):
        part = table[bass.ds(c * CF, CF), :] if not isinstance(c, int) else table[c * CF:(c + 1) * CF, :]
        return part.rearrange("(t p) f -> p t f", p=P)

    def link(self, dve, c, ins):
        self.n_links += 1
        ins.then_inc(self.step, 1)
        dve.wait_ge(self.step, c * LINKS[self.layer] + self.n_links)

    def turn(self, pe, c, unit):
        pe.wait_ge(self.rows_ready, self.count(c, unit))
        pe.sem_inc(self.go)
        for j in range(CT):
            mm = pe.transpose(self.ps_turn[:, j * P:(j + 1) * P], self.rows[:, j * D:(j + 1) * D],
                              self.k.ident[:, :])
        mm.then_inc(self.turned, 1)

    def multiply(self, pe, c, unit, matrix, bias, agg=None, first=False):
        k = self.k
        pe.wait_ge(self.consumed, self.count(c, unit))
        pe.matmul(self.ps_self[:, 0:CW].rearrange("p (t f) -> p t f", f=D), k.ones[0:1, :],
                  bias_row(k, bias), start=True, stop=False, skip_group_check=True)
        pe.wait_ge(self.moved, self.count(c, unit))
        pe.sem_inc(self.go)
        for j in range(CT):
            mm = pe.matmul(self.ps_self[:, j * D:(j + 1) * D], self.xT[:, j * P:(j + 1) * P],
                           mat(k, matrix), start=False, stop=not first, skip_group_check=True)
        if first:
            for h in range(2):
                mm = pe.matmul(self.ps_turn[:, h * 512:h * 512 + CF // 2], mat(k, "We_out"),
                               self.sT[0:D, h * (CF // 2):(h + 1) * (CF // 2)], start=True, stop=True)
            mm.then_inc(self.first_mm, 1)
            return
        if agg is not None:
            for j in range(CT):
                mm = pe.matmul(self.ps_agg[:, j * self.wide:(j + 1) * self.wide],
                               self.sT[0:self.wide, j * P:(j + 1) * P],
                               k.agg_count[:, :] if self.counting else mat(k, agg),
                               start=True, stop=True, skip_group_check=True)
        mm.then_inc(self.product, 1)

    def tensor(self, pe, c, slot):
        k, layer = self.k, self.layer
        late = layer == "both"
        if slot == 1 + late:
            self.turn(pe, c, 0)
        if slot == 3 + late:
            self.multiply(pe, c, 0, *self.spec["self"], self.spec["agg"], layer == "edge")
        if layer == "edge" and slot == 5:
            pe.wait_ge(self.first_moved, self.count(c))
            for j in range(CT):
                mm = pe.matmul(self.ps_self[:, j * D:(j + 1) * D], self.s2T[:, j * P:(j + 1) * P],
                               mat(k, "Wn_agg"), start=False, stop=True, skip_group_check=True)
            mm.then_inc(self.product, 1)
        if layer == "sage2":
            for unit, at in ((1, 5), (2, 11)):
                if slot == at:
                    self.turn(pe, c, unit)
                if slot == at + 2:
                    self.multiply(pe, c, unit, *self.spec["then"][unit - 1])

    def move(self, act, c, unit, sums):
        act.wait_ge(self.turned, self.count(c, unit))
        act.wait_ge(self.product, self.count(c, unit))
        if sums:
            at = bass.ds(c * CF, CF) if not isinstance(c, int) else slice(c * CF, (c + 1) * CF)
            act.copy(self.sT[0:self.wide, :], self.k.acc[0:self.wide, at])
        act.copy(self.xT[:, :], self.ps_turn[:, 0:CF]).then_inc(self.moved, 1)

    def sqrt(self, act, c, width=CT):
        act.wait_ge(self.var_ready, c + 1)
        act.activation(self.k.stat[1][:, 0:width], self.k.stat[0][:, 0:width], ACT.Sqrt
                       ).then_inc(self.std_ready, 1)

    def store(self, act, c, table, rows):
        act.dma_start(self.dram(table, c), rows.rearrange("p (t f) -> p t f", f=D)).then_inc(self.stored, 16)

    def scalar(self, act, c, slot):
        k, layer = self.k, self.layer
        late = layer == "both"
        if slot == 0:
            if late:
                act.wait_ge(self.parts_free, c + 1)
                act.sem_inc(self.go)
                for n in range(COPIES):
                    act.dma_start(k.parts[:, n, :].rearrange("p (t f) -> p t f", f=D),
                                  self.dram(k.part[n], c)).then_inc(self.loaded, 16)
            else:
                act.copy(self.rows[:, :], self.of(k.x if self.spec["source"] == "x" else k.h, c)
                         ).then_inc(self.rows_ready, 1)
        if slot == 2 + late:
            self.move(act, c, 0, True)
        if layer == "mean" and slot == 6:
            self.sqrt(act, c)
        if self.counting and slot in (8, 10, 12, 14):
            act.dma_start(self.dram(k.part[(slot - 8) // 2], c), k.zero[:, :].unsqueeze(1).to_broadcast([P, CT, D])
                          ).then_inc(self.stored, 16)
        if self.counting and isinstance(c, int) and c == NCH - 1 and slot == 15:
            for t in [k.tab["x3"]] + k.part:
                act.dma_start(t[NP:NS, :], k.zero[:, :]).then_inc(self.stored, 16)
        if layer == "sage1" and slot == 5:
            act.wait_ge(self.result, c + 1)
            act.sem_inc(self.go)
            self.store(act, c, k.tab["h1"], self.of(k.h, c))
        if layer == "sage2":
            if slot in (6, 12):
                self.move(act, c, slot // 6, False)
            if slot == 9:
                self.sqrt(act, c)
            if slot == 14:
                act.wait_ge(self.product, self.count(c, 2) + 1)
                act.wait_ge(self.stored, c * 16 + 16)
                act.copy(self.q[:, :], self.ps_self[:, 0:CW]).then_inc(self.copied, 1)
                act.sem_inc(self.consumed)
            if slot == 15:
                act.wait_ge(self.copied, c + 1)
                act.sem_inc(self.go)
                self.store(act, c, k.tab["pre"], self.q[:, :])
        if layer == "edge":
            if slot == 4:
                act.wait_ge(self.first_mm, self.count(c))
                act.copy(self.s2T[:, :].rearrange("p (a c) -> p a c", a=2),
                         self.ps_turn[:, :].rearrange("p (a c) -> p a c", a=2)[:, :, 0:CF // 2]
                         ).then_inc(self.first_moved, 1)
            if slot == 7:
                self.sqrt(act, c)
            if slot == 9:
                act.wait_ge(self.result, c + 1)
                act.sem_inc(self.go)
                self.store(act, c, k.tab["x3"], self.of(k.x, c))
        if late:
            if slot == 7:
                self.sqrt(act, c)
            if slot == 9:
                act.wait_ge(self.result, c + 1)
                act.sem_inc(self.go)
                if isinstance(c, int) and c == NCH - 1:
                    full = (CT - 1) * P
                    act.dma_start(k.out[c * CF:c * CF + full, :].rearrange("(t p) f -> p t f", p=P),
                                  self.of(k.x, c).rearrange("p (t f) -> p t f", f=D)[:, 0:CT - 1, :]
                                  ).then_inc(self.stored, 16)
                    act.dma_start(k.out[c * CF + full:N, :], k.x[0:LAST, (NT - 1) * D:NT * D]
                                  ).then_inc(self.stored, 16)
                else:
                    self.store(act, c, k.out, self.of(k.x, c))

    def scalar_end(self, act):
        if self.counting:
            act.wait_ge(self.stored, 16 + 16 * (COPIES * NCH + 1 + COPIES))
        elif self.layer != "mean":
            act.wait_ge(self.stored, 16 + 16 * (NCH + (self.layer == "both")))

    def tensor_start(self, pe):
        pe.sem_inc(self.product)

    def scalar_start(self, act):
        act.sem_inc(self.stored, 16)

    def vector_start(self, dve):
        dve.sem_inc(self.consumed)
        dve.sem_inc(self.parts_free)
        if self.layer == "mean":
            dve.memset(self.k.sums[:, :], 0.0)

    def combine(self, dve, c, out, relu):
        k, link = self.k, self.link
        dve.wait_ge(self.product, self.count(c) + 1)
        o3 = lambda t: t.rearrange("p (t f) -> p t f", f=D)
        if self.layer == "edge":
            link(dve, c, dve.tensor_tensor(o3(self.t[:, :]), self.of_nodes(k.deg["dst"], c),
                                           over_tiles(k.be2w[:, :], CT), ALU.mult))
        else:
            products = self.ps_agg[:, 0:CT * self.wide].rearrange("p (t f) -> p t f", f=self.wide)
            if self.counting:
                degree = products[:, :, D:D + 1].rearrange("p t o -> p (t o)")
                dve.tensor_copy(self.part(k.deg["dst"], c), degree)
                link(dve, c, dve.tensor_scalar(k.stat[2][:, 0:CT], degree, 1.0, None, ALU.max))
                link(dve, c, dve.reciprocal(self.part(k.rdeg["dst"], c), k.stat[2][:, 0:CT]))
            link(dve, c, dve.tensor_tensor(o3(self.t[:, :]), products[:, :, 0:D],
                                           self.of_nodes(k.rdeg["dst"], c), ALU.mult))
        if not relu:
            return dve.tensor_tensor(out, self.t[:, :], self.ps_self[:, 0:CW], ALU.add)
        link(dve, c, dve.tensor_tensor(self.t[:, :], self.t[:, :], self.ps_self[:, 0:CW], ALU.add))
        return dve.tensor_scalar(out, self.t[:, :], 0.0, None, ALU.max)

    def norm_begin(self, dve, c):
        k, link, y3 = self.k, self.link, self.y[:, :].rearrange("p (t f) -> p t f", f=D)
        s = k.stat[2]
        link(dve, c, dve.tensor_reduce(s[:, 0:CT], y3, AX.X, ALU.add))
        link(dve, c, dve.tensor_scalar(s[:, 0:CT], s[:, 0:CT], 1.0 / D, None, ALU.mult))
        link(dve, c, dve.tensor_tensor(y3, y3, over_features(s[:, 0:CT], CT), ALU.subtract))
        link(dve, c, dve.tensor_tensor(self.t[:, :], self.y[:, :], self.y[:, :], ALU.mult))
        link(dve, c, dve.tensor_reduce(s[:, 0:CT], self.t[:, :].rearrange("p (t f) -> p t f", f=D),
                                       AX.X, ALU.add))
        dve.tensor_scalar(k.stat[0][:, 0:CT], s[:, 0:CT], 1.0 / D, LN_EPS, ALU.mult, ALU.add
                          ).then_inc(self.var_ready, 1)

    def norm_end(self, dve, c):
        k, y3 = self.k, self.y[:, :].rearrange("p (t f) -> p t f", f=D)
        dve.wait_ge(self.std_ready, c + 1)
        self.link(dve, c, dve.reciprocal(k.stat[3][:, 0:CT], k.stat[1][:, 0:CT]))
        scale = over_features(k.stat[3][:, 0:CT], CT)
        if self.layer == "sage2":
            dve.tensor_tensor(self.rows[:, :].rearrange("p (t f) -> p t f", f=D), y3, scale,
                              ALU.mult).then_inc(self.rows_ready, 1)
        dve.tensor_tensor(self.of(k.x, c).rearrange("p (t f) -> p t f", f=D), y3, scale,
                          ALU.mult).then_inc(self.result, 1)

    def vector(self, dve, c, slot):
        k, layer, link = self.k, self.layer, self.link
        if slot == 0:
            self.n_links = 0
        if layer == "mean":
            if slot == 4:
                link(dve, c, self.combine(dve, c, self.y[:, :], False))
                dve.sem_inc(self.consumed)
                link(dve, c, dve.tensor_tensor(self.t[:, :], self.y[:, :], self.y[:, :], ALU.mult))
                dve.tensor_reduce(k.stat[0][:, 0:CT], self.t[:, :].rearrange("p (t f) -> p t f", f=D),
                                  AX.X, ALU.add).then_inc(self.var_ready, 1)
            if slot == 7:
                dve.wait_ge(self.std_ready, c + 1)
                link(dve, c, dve.tensor_scalar(k.stat[2][:, 0:CT], k.stat[1][:, 0:CT], L2_EPS, None, ALU.max))
                link(dve, c, dve.reciprocal(k.stat[3][:, 0:CT], k.stat[2][:, 0:CT]))
                link(dve, c, dve.tensor_tensor(
                    self.t[:, :].rearrange("p (t f) -> p t f", f=D),
                    self.y[:, :].rearrange("p (t f) -> p t f", f=D),
                    over_features(k.stat[3][:, 0:CT], CT), ALU.mult))
                h = self.of(k.h, c)
                link(dve, c, dve.tensor_scalar(h, self.t[:, :], 0.0, None, ALU.max))
                if isinstance(c, int) and c == NCH - 1:
                    last = k.h[:, (NT - 1) * D:NT * D]
                    link(dve, c, dve.tensor_scalar(last, last, k.mask[:, 0:1], None, ALU.mult))
                link(dve, c, dve.tensor_tensor(k.sums[:, :], k.sums[:, :], h, ALU.add))
            if slot == 9:
                link(dve, c, dve.tensor_scalar(self.t[:, :], self.of(k.x, c), 2.0, None, ALU.mult))
                link(dve, c, dve.tensor_tensor(self.of(k.y, c).rearrange("p (t f) -> p t f", f=D),
                                               self.t[:, :].rearrange("p (t f) -> p t f", f=D),
                                               over_tiles(k.beta[:, :], CT), ALU.add))
        if layer == "sage1" and slot == 4:
            self.combine(dve, c, self.of(k.h, c), True).then_inc(self.result, 1)
            dve.sem_inc(self.consumed)
        if layer == "sage2":
            if slot == 4:
                self.combine(dve, c, self.rows[:, :], True).then_inc(self.rows_ready, 1)
                dve.sem_inc(self.consumed)
            if slot == 8:
                dve.wait_ge(self.product, self.count(c, 1) + 1)
                link(dve, c, dve.tensor_tensor(self.y[:, :], self.ps_self[:, 0:CW], self.of(k.x, c), ALU.add))
                dve.sem_inc(self.consumed)
                self.norm_begin(dve, c)
            if slot == 10:
                self.norm_end(dve, c)
        if layer == "edge":
            if slot == 6:
                link(dve, c, self.combine(dve, c, self.y[:, :], True))
                dve.sem_inc(self.consumed)
                link(dve, c, dve.tensor_tensor(self.y[:, :], self.y[:, :], self.of(k.x, c), ALU.add))
                self.norm_begin(dve, c)
            if slot == 8:
                self.norm_end(dve, c)
        if layer == "both":
            if slot == 1:
                dve.wait_ge(self.loaded, c * (16 * COPIES) + 16 * COPIES)
                for n in (1, 2, 3):
                    link(dve, c, dve.tensor_tensor(k.parts[:, 0, :], k.parts[:, 0, :], k.parts[:, n, :], ALU.add))
                dve.tensor_tensor(self.rows[:, :].rearrange("p (t f) -> p t f", f=D),
                                  k.parts[:, 0, :].rearrange("p (t f) -> p t f", f=D),
                                  self.of_nodes(k.rdeg["src"], c), ALU.mult).then_inc(self.rows_ready, 1)
                dve.sem_inc(self.parts_free)
            if slot == 6:
                link(dve, c, self.combine(dve, c, self.y[:, :], True))
                dve.sem_inc(self.consumed)
                link(dve, c, dve.tensor_tensor(self.y[:, :], self.y[:, :], self.of(k.x, c), ALU.add))
                self.norm_begin(dve, c)
            if slot == 8:
                self.norm_end(dve, c)
        if slot == SLOTS - 1:
            assert self.n_links <= LINKS[layer]
            if self.n_links < LINKS[layer]:
                dve.sem_inc(self.step, LINKS[layer] - self.n_links)


def node_stage(nc, k, layer):
    with stage(nc) as (ctx, sem):
        work = NodeWork(nc, k, ctx, sem, layer)
        block = ctx.enter_context(nc.Block())

        @block.tensor
        def _(pe):
            work.tensor_start(pe)
            with pe.Fori(0, NCH - 1) as c:
                for u in range(SLOTS):
                    work.tensor(pe, c, u)
            for u in range(SLOTS):
                work.tensor(pe, NCH - 1, u)

        @block.scalar
        def _(act):
            work.scalar_start(act)
            with act.Fori(0, NCH - 1) as c:
                for u in range(SLOTS):
                    work.scalar(act, c, u)
            for u in range(SLOTS):
                work.scalar(act, NCH - 1, u)
            work.scalar_end(act)

        @block.vector
        def _(dve):
            work.vector_start(dve)
            with dve.Fori(0, NCH - 1) as c:
                for u in range(SLOTS):
                    work.vector(dve, c, u)
            for u in range(SLOTS):
                work.vector(dve, NCH - 1, u)


def batch_norm_stage(nc, k):
    with stage(nc) as (ctx, sem):
        step, act_done, pe_done, stored = sem("n_step"), sem("n_act"), sem("n_pe"), sem("n_stored")
        ps = psum(nc, ctx, "n_ps")
        s0, s1, s2 = k.small
        h, y, w = k.h, k.y, k.w
        last = h[:, (NT - 1) * D:NT * D]
        block = ctx.enter_context(nc.Block())
        marks = {}

        @block.vector
        def _(dve):
            n = [0]

            def link(ins_, name=None):
                n[0] += 1
                ins_.then_inc(step, 1)
                dve.wait_ge(step, n[0])
                if name:
                    marks[name] = n[0]

            link(dve.tensor_reduce(s0[:, 0:D], k.sums[:, :].rearrange("p (t f) -> p f t", f=D),
                                   AX.X, ALU.add), "sums")
            dve.wait_ge(pe_done, 1)
            link(dve.tensor_scalar(s0[:, 0:D], ps[:, 0:D], 1.0 / N, None, ALU.mult))
            link(dve.tensor_tensor(nm3(h), nm3(h), over_tiles(s0[:, 0:D]), ALU.subtract))
            link(dve.tensor_scalar(last, last, k.mask[:, 0:1], None, ALU.mult), "centred")
            dve.wait_ge(act_done, 1)
            link(dve.tensor_reduce(s2[:, 0:D], w[:, :].rearrange("p (t f) -> p f t", f=D), AX.X, ALU.add),
                 "squares")
            dve.wait_ge(pe_done, 2)
            link(dve.tensor_scalar(s0[:, 0:D], ps[:, D:2 * D], 1.0 / N, BN_EPS, ALU.mult, ALU.add), "var")
            dve.wait_ge(act_done, 2)
            link(dve.reciprocal(s2[:, 0:D], s1[:, 0:D]))
            link(dve.tensor_tensor(s2[:, 0:D], s2[:, 0:D], k.gamma[:, :], ALU.mult))
            link(dve.tensor_tensor(nm3(h), nm3(h), over_tiles(s2[:, 0:D]), ALU.mult))
            link(dve.tensor_tensor(y[:, :], h[:, :], y[:, :], ALU.add))
            link(dve.tensor_reduce(s0[:, 0:NT], nm3(y), AX.X, ALU.add))
            link(dve.tensor_scalar(s0[:, 0:NT], s0[:, 0:NT], 1.0 / D, None, ALU.mult))
            link(dve.tensor_tensor(nm3(y), nm3(y), over_features(s0[:, 0:NT]), ALU.subtract), "y")
            dve.wait_ge(act_done, 3)
            link(dve.tensor_reduce(s0[:, 0:NT], nm3(w), AX.X, ALU.add))
            link(dve.tensor_scalar(s0[:, 0:NT], s0[:, 0:NT], 1.0 / D, LN_EPS, ALU.mult, ALU.add), "lnvar")
            dve.wait_ge(act_done, 4)
            link(dve.reciprocal(s2[:, 0:NT], s1[:, 0:NT]))
            link(dve.tensor_tensor(nm3(k.x), nm3(y), over_features(s2[:, 0:NT]), ALU.mult), "x")

        @block.scalar
        def _(act):
            act.wait_ge(step, marks["centred"])
            act.activation(w[:, :], h[:, :], ACT.Square).then_inc(act_done, 1)
            act.wait_ge(step, marks["var"])
            act.activation(s1[:, 0:D], s0[:, 0:D], ACT.Sqrt).then_inc(act_done, 1)
            act.wait_ge(step, marks["y"])
            act.activation(w[:, :], y[:, :], ACT.Square).then_inc(act_done, 1)
            act.wait_ge(step, marks["lnvar"])
            act.activation(s1[:, 0:NT], s0[:, 0:NT], ACT.Sqrt).then_inc(act_done, 1)

        @block.tensor
        def _(pe):
            pe.wait_ge(step, marks["sums"])
            pe.matmul(ps[:, 0:D], k.ones[:, :], s0[:, 0:D], start=True, stop=True).then_inc(pe_done, 1)
            pe.wait_ge(step, marks["squares"])
            pe.matmul(ps[:, D:2 * D], k.ones[:, :], s2[:, 0:D], start=True, stop=True).then_inc(pe_done, 1)

        @block.sync
        def _(sp):
            sp.wait_ge(step, marks["x"])
            sp.dma_start(dram_nm(k.tab["x1"]), nm3(k.x)).then_inc(stored, 16)
            sp.wait_ge(stored, 16)


def layer_of(nc, k, fast, table, layer):
    with nc.If(fast):
        fast_pass(nc, k, table, layer)
    with nc.Else():
        if layer == "mean":
            zero_stage(nc, k)
            degree_stage(nc, k)
        general_pass(nc, k, table, "dst", layer == "edge")
        gather_partials(nc, k)
        node_stage(nc, k, layer)


def build(nc, ins, out):
    with ExitStack() as ctx:
        k = alloc(nc, ctx, ins)
        k.out = out
        setup_stage(nc, k)
        fast = nc.values_load(k.flag[0:1, 0:1], min_val=0, max_val=1,
                              skip_runtime_bounds_check_because="it is the result of a comparison")
        layer_of(nc, k, fast, ins["x"], "mean")
        batch_norm_stage(nc, k)
        layer_of(nc, k, fast, k.tab["x1"], "sage1")
        layer_of(nc, k, fast, k.tab["h1"], "sage2")
        layer_of(nc, k, fast, k.tab["pre"], "edge")
        with nc.If(fast):
            reverse_pass(nc, k, k.tab["x3"])
            fast_pass(nc, k, k.tab["x3"], "both")
        with nc.Else():
            general_pass(nc, k, k.tab["x3"], "dst")
            gather_partials(nc, k)
            general_pass(nc, k, k.tab["x3"], "src")
            node_stage(nc, k, "both")


ROWS.append("zero")


def kernel(x, src, dst, edge_attr_64, L0_gnn_W, L0_gnn_b, L0_gnn_gamma, L0_gnn_beta, L1_gnn_w1_l, L1_gnn_b1,
           L1_gnn_w1_r, L1_gnn_w2_l, L1_gnn_b2, L1_gnn_w2_r, L1_gnn_w_lin, L1_gnn_b_lin, L2_gnn_W1, L2_gnn_b1,
           L2_gnn_W2, L2_gnn_b2, L2_gnn_W3, L2_gnn_b3, L3_gnn_W):
    import concourse.bacc as bacc
    from concourse.bass_utils import run_bass_kernel_spmd

    def padded(a, rows, fill=0):
        return np.concatenate([a, np.full((rows - a.shape[0],) + a.shape[1:], fill, a.dtype)])

    def pieces(a):
        return np.asarray(a)

    src, dst = padded(pieces(src), EP, N), padded(pieces(dst), EP, N)
    s3, d3 = src.reshape(NG, GROUP, P), dst.reshape(NG, GROUP, P)
    attr = padded(pieces(edge_attr_64), EP).reshape(EP // (2 * P), 2, P, D)
    l0, l3, e1, e3 = (pieces(a) for a in (L0_gnn_W, L3_gnn_W, L2_gnn_W1, L2_gnn_W3))
    t = lambda a: pieces(a).T
    mats = {"W0_self": l0[:D], "W0_agg": l0[D:], "W1_agg": t(L1_gnn_w1_l), "W1_self": t(L1_gnn_w1_r),
            "W2_agg": t(L1_gnn_w2_l), "W2_self": t(L1_gnn_w2_r), "Wlin": t(L1_gnn_w_lin),
            "We_node": e1[:D], "We_edge": e1[D:], "We_out": pieces(L2_gnn_W2), "Wn_self": e3[:D],
            "Wn_agg": e3[D:], "W3_fwd": t(l3[:, :D]), "W3_bwd": t(l3[:, D:])}
    rows = {"b0": L0_gnn_b, "b1": L1_gnn_b1, "b2": L1_gnn_b2, "blin": L1_gnn_b_lin, "be": L2_gnn_b1,
            "be2": L2_gnn_b2, "bn": L2_gnn_b3, "gamma": L0_gnn_gamma, "beta": L0_gnn_beta,
            "zero": np.zeros(D, np.float32)}
    arrays = {
        "x": padded(pieces(x), NP),
        "cols": np.concatenate([s3.transpose(0, 2, 1), d3.transpose(0, 2, 1)], axis=2),
        "dst_all": d3.transpose(2, 0, 1).reshape(P, NG * GROUP),
        "first": d3[:, 0, 0].reshape(1, NG),
        "rows_of": np.stack([src.reshape(NG, GROUP * P), dst.reshape(NG, GROUP * P)], axis=1),
        "attr": attr.transpose(1, 3, 0, 2).reshape(P, EP // 2),
        "mats": np.concatenate([mats[m] for m in MATS], axis=1),
        "rows": np.stack([pieces(rows[r]) for r in ROWS])[None],
        "be2_col": pieces(L2_gnn_b2).reshape(D, 1),
    }
    nc = bacc.Bacc("TRN2", target_bir_lowering=False, num_devices=1)
    ins, feed = {}, {}
    for name, a in arrays.items():
        feed[f"in_{name}"] = np.ascontiguousarray(a)
        ins[name] = nc.dram_tensor(f"in_{name}", a.shape, mybir.dt.from_np(a.dtype), kind="ExternalInput").ap()
    out = nc.dram_tensor("out", (N, D), F32, kind="ExternalOutput").ap()
    build(nc, ins, out)
    return run_bass_kernel_spmd(nc, [feed], core_ids=[0]).results[0]["out"]
```

```python
from contextlib import ExitStack, contextmanager

import numpy as np

import concourse.bass as bass
from concourse import mybir

ALU = mybir.AluOpType
ACT = mybir.ActivationFunctionType
AX = mybir.AxisListType
F32 = mybir.dt.float32
BF16 = mybir.dt.bfloat16
I32 = mybir.dt.int32

P = 128
D = 64
N = 12500
NT = -(-N // P)
NP = NT * P
LAST = N - (NT - 1) * P
CT = 7
NCH = NT // CT
ROUND = NCH // 2
CW = CT * D
CF = CT * P
E = 212500
GROUP = 8
NG = -(-E // (P * GROUP))
EP = NG * GROUP * P
WINDOW = 128
LAST_TILES = -(-E // P) - (NG - 1) * GROUP
RING = 4
SLOTS = 16
BODIES = NG // SLOTS
COPIES = 8
ZERO_DMAS = COPIES + 1
NS = NP + P
BN_EPS = 1e-5
LN_EPS = 1e-5
L2_EPS = 1e-12
assert NT % CT == 0 and NG % SLOTS == 0 and SLOTS % RING == 0 and CW <= 512
assert BODIES == NCH - 1 and COPIES == GROUP

MATS = ["W0_self", "W0_agg", "W1_agg", "W1_self", "W2_agg", "W2_self", "Wlin", "We_node", "We_edge",
        "We_out", "Wn_self", "Wn_agg", "W3_fwd", "W3_bwd"]
ROWS = ["b0", "b1", "b2", "blin", "be", "be2", "bn", "gamma", "beta", "zero"]


class Kit:
    pass


def alloc(nc, ctx, ins):
    k = Kit()
    k.ins = ins

    def sb(name, shape, dt=F32):
        return ctx.enter_context(nc.sbuf_tensor(name, shape, dt))

    k.acc = sb("acc", [D + 1, NP + WINDOW])
    k.x = sb("x_nm", [P, NT * D])
    k.h = sb("h_nm", [P, NT * D])
    k.y = sb("y_nm", [P, NT * D])
    k.w = sb("work_nm", [P, NT * D])
    k.gath = [sb(f"gath{b}", [P, GROUP, D + 1]) for b in range(RING)]
    k.oneh = [sb(f"oneh{b}", [P, GROUP, WINDOW]) for b in range(2)]
    k.idx = [sb(f"idx{b}", [P, 2 * GROUP], I32) for b in range(RING)]
    k.first = [sb(f"first{b}", [P, 1], I32) for b in range(RING)]
    k.local = [sb(f"local{b}", [P, GROUP]) for b in range(RING)]
    k.hilo = [sb(f"hilo{b}", [P, 4, GROUP]) for b in range(2)]
    k.hilo_i = [sb(f"hilo_i{b}", [P, 4, GROUP], I32) for b in range(2)]
    k.xT = [sb(f"xT{b}", [D + 1, CF]) for b in range(2)]
    k.sT = [sb("sT", [D, CF])]
    k.agg_count = sb("agg_count", [D + 1, D + 1])
    k.chunk = [sb(f"chunk{j}", [P, CW]) for j in range(4)]
    k.sums = sb("sums", [P, CW])
    k.base, k.squares = k.h[:, 0:CW], k.h[:, CW:2 * CW]
    k.is_first = sb("is_first", [P, 1])
    k.lane_n = sb("lane_n", [P, 2])
    k.centre = sb("centre", [D, D])
    k.parts = k.h[:, 0:COPIES * CW].rearrange("p (n c) -> p n c", n=COPIES)
    k.stat = [sb(f"stat{j}", [P, CT]) for j in range(4)]
    k.zero = sb("zero", [P, D])
    k.mats = sb("mats", [P, len(MATS) * D])
    k.rows = sb("rows", [1, len(ROWS) * D])
    k.gamma = sb("gamma", [P, D])
    k.beta = sb("beta", [P, D])
    k.be2col = sb("be2col", [D, 1])
    k.be2w = sb("be2w", [P, D])
    k.iota = sb("iota", [P, P])
    k.ident = sb("ident", [P, P])
    k.lower = sb("lower", [P, P], BF16)
    k.ones = sb("ones", [P, P])
    k.mask = sb("mask", [P, 1])
    k.spare = sb("spare", [P, 1])
    k.flag = sb("flag", [1, 1], I32)
    k.deg = {s: sb(f"deg_{s}", [P, NT]) for s in ("src", "dst")}
    k.rdeg = {s: sb(f"rdeg_{s}", [P, NT]) for s in ("src", "dst")}
    k.small = [sb(f"small{j}", [P, P]) for j in range(3)]

    k.tab = {n: nc.dram_tensor(f"table_{n}", [NS if n == "x3" else NP, D], F32).ap()
             for n in ("x1", "h1", "pre", "x3")}
    k.part = [nc.dram_tensor(f"partial{c}", [NS, D], F32).ap() for c in range(COPIES)]
    return k


def mat(k, name, part=0):
    c = MATS.index(name) * D
    return k.mats[part:part + D, c:c + D]


def bias_row(k, name):
    c = ROWS.index(name) * D
    return k.rows[0:1, c:c + D].unsqueeze(1).to_broadcast([1, CT, D])


def nm3(t):
    return t[:, :].rearrange("p (t f) -> p t f", f=D)


def over_features(t, n=NT):
    return t.unsqueeze(2).to_broadcast([P, n, D])


def over_tiles(t, n=NT):
    return t.unsqueeze(1).to_broadcast([P, n, D])


def dram_nm(t, rows=NP):
    return t[0:rows, :].rearrange("(t p) f -> p t f", p=P)


def psum(nc, ctx, name, cols=512, parts=P):
    return ctx.enter_context(nc.psum_tensor(name, [parts, cols], F32, allow_name_mangling=True))


@contextmanager
def stage(nc):
    held = []

    def sem(name):
        held.append(nc.alloc_semaphore(f"{name}_{nc.next_id()}"))
        return held[-1]

    with ExitStack() as ctx:
        yield ctx, sem
    nc.gpsimd.dma_reset()
    engines = [nc.gpsimd, nc.sync, nc.scalar, nc.vector, nc.tensor]
    for n, s in enumerate(held):
        engines[n % len(engines)].sem_clear(s)
    nc.all_engine_barrier()
    for s in held:
        nc.release_semaphore(s)



def setup_stage(nc, k):
    ins = k.ins
    with stage(nc) as (ctx, sem):
        ps = psum(nc, ctx, "setup_ps")
        loaded, consts, step, summed, folded = (
            sem("setup_loaded"), sem("setup_consts"), sem("setup_step"), sem("setup_summed"), sem("setup_folded"))
        dst_all = k.h[:, 0:NG * GROUP].bitcast(I32)
        first_all = k.h[:, NG * GROUP:NG * GROUP + NG].bitcast(I32)
        past = k.w[:, 0:NG].rearrange("p (j u) -> p j u", u=SLOTS)
        dist = k.y[:, 0:NG * GROUP].rearrange("p (g t) -> p g t", t=GROUP)
        block = ctx.enter_context(nc.Block())
        n_loads = 8

        @block.sync
        def _(sp):
            sp.dma_start(dst_all, ins["dst_all"]).then_inc(loaded, 16)
            sp.dma_start(first_all, ins["first"].to_broadcast([P, NG])).then_inc(loaded, 16)
            sp.dma_start(k.mats[0:D, :], ins["mats"]).then_inc(loaded, 16)
            sp.dma_start(k.mats[D:P, :], ins["mats"]).then_inc(loaded, 16)
            sp.dma_start(k.rows[:, :], ins["rows"].rearrange("o r f -> o (r f)")).then_inc(loaded, 16)
            for name, tile in (("gamma", k.gamma), ("beta", k.beta)):
                r = ROWS.index(name)
                sp.dma_start(tile[:, :], ins["rows"][0, r:r + 1, :].to_broadcast([P, D])).then_inc(loaded, 16)
            sp.dma_start(k.be2col[:, :], ins["be2_col"]).then_inc(loaded, 16)

        @block.gpsimd
        def _(pool):
            pool.iota(k.iota[:, :], [[1, P]], base=0, channel_multiplier=0,
                      allow_small_or_imprecise_dtypes=True).then_inc(consts, 1)
            pool.iota(past[:, 0:BODIES - 1, :], [[CF, BODIES - 1], [0, SLOTS]], base=0, channel_multiplier=0,
                      allow_small_or_imprecise_dtypes=True).then_inc(consts, 1)
            pool.iota(past[:, BODIES - 1, :].rearrange("p (h u) -> p h u", h=2), [[CF, 2], [0, SLOTS // 2]],
                      base=CF * (BODIES - 1), channel_multiplier=0,
                      allow_small_or_imprecise_dtypes=True).then_inc(consts, 1)
            pool.iota(k.spare[:, :], [[0, 1]], base=NP, channel_multiplier=1,
                      allow_small_or_imprecise_dtypes=True).then_inc(consts, 1)

        @block.vector
        def _(dve):
            n = [0]

            def link(ins_):
                n[0] += 1
                ins_.then_inc(step, 1)
                dve.wait_ge(step, n[0])

            dve.memset(k.zero[:, :], 0.0)
            for b in range(RING):
                dve.memset(k.gath[b][:, :, D:D + 1], 1.0)
            link(dve.memset(k.agg_count[:, :], 0.0))
            dve.memset(k.agg_count[D:D + 1, D:D + 1], 1.0)
            dve.memset(k.ones[:, :], 1.0).then_inc(folded, 1)
            dve.wait_ge(consts, 4)
            link(dve.tensor_scalar(k.small[0][:, 0:1], k.spare[:, :], float(NP), None, ALU.subtract))
            dve.tensor_scalar(k.ident[:, :], k.iota[:, :], k.small[0][:, 0:1], None, ALU.is_equal)
            dve.tensor_scalar(k.lower[:, :], k.iota[:, :], k.small[0][:, 0:1], None, ALU.is_lt)
            dve.tensor_scalar(k.mask[:, :], k.small[0][:, 0:1], float(LAST), None, ALU.is_lt)
            dve.tensor_scalar(k.lane_n[:, 0:1], k.small[0][:, 0:1], float(LAST), None, ALU.is_lt)
            link(dve.tensor_scalar(k.centre[:, :], k.iota[0:D, 0:D], k.small[0][0:D, 0:1], None, ALU.is_equal))
            dve.tensor_scalar(k.centre[:, :], k.centre[:, :], 1.0 / D, None, ALU.subtract)
            link(dve.tensor_scalar(k.lane_n[:, 0:1], k.lane_n[:, 0:1], NCH - 1.0, None, ALU.add))
            dve.reciprocal(k.lane_n[:, 1:2], k.lane_n[:, 0:1])
            dve.wait_ge(loaded, 16 * n_loads)
            dve.tensor_copy(k.agg_count[0:D, 0:D], mat(k, "W0_agg"))
            link(dve.tensor_tensor(dist, dst_all.rearrange("p (g t) -> p g t", t=GROUP),
                                   first_all.unsqueeze(2).to_broadcast([P, NG, GROUP]), ALU.subtract))
            link(dve.tensor_reduce(k.small[0][:, 1:2], k.y[:, 0:NG * GROUP], AX.X, ALU.max))
            link(dve.tensor_reduce(k.small[0][:, 2:3], k.y[:, 0:NG * GROUP], AX.X, ALU.min))
            link(dve.tensor_scalar(k.small[0][:, 3:4], k.small[0][:, 1:2], float(WINDOW), None, ALU.is_lt))
            link(dve.tensor_scalar(k.small[0][:, 4:5], k.small[0][:, 2:3], 0.0, None, ALU.is_ge))
            link(dve.tensor_tensor(k.small[0][:, 5:6], k.small[0][:, 3:4], k.small[0][:, 4:5], ALU.mult))
            link(dve.tensor_tensor(k.w[:, NG:2 * NG], first_all, k.w[:, 0:NG], ALU.subtract))
            link(dve.tensor_reduce(k.small[0][:, 6:7], k.w[:, NG:2 * NG], AX.X, ALU.min))
            link(dve.tensor_scalar(k.small[0][:, 7:8], k.small[0][:, 6:7], 0.0, None, ALU.is_ge))
            dve.tensor_tensor(k.small[1][:, 0:1], k.small[0][:, 5:6], k.small[0][:, 7:8],
                              ALU.mult).then_inc(folded, 1)
            dve.tensor_copy(k.small[2][0:D, :], k.be2col[:, 0:1].to_broadcast([D, P])).then_inc(folded, 1)
            dve.wait_ge(summed, 2)
            dve.tensor_scalar(k.flag[:, :], ps[0:1, 0:1], float(P), None, ALU.is_ge)
            dve.tensor_copy(k.be2w[:, :], ps[:, D:2 * D])

        @block.tensor
        def _(pe):
            pe.wait_ge(folded, 3)
            pe.matmul(ps[0:1, 0:1], k.small[1][:, 0:1], k.ones[:, 0:1], start=True, stop=True).then_inc(summed, 1)
            pe.matmul(ps[:, D:2 * D], k.small[2][0:D, :], mat(k, "Wn_agg"), start=True,
                      stop=True).then_inc(summed, 1)



def degree_onehots(dve, k, b, ring, deg_step, deg_ready, value, sides):
    idx = k.idx[ring]
    hi_i, f = k.hilo_i[b % 2], k.hilo[b % 2]
    for s in range(sides):
        col = idx[:, s * GROUP:(s + 1) * GROUP]
        dve.tensor_scalar(hi_i[:, s, :], col, P - 1, None, ALU.bitwise_and)
        last = dve.tensor_scalar(hi_i[:, 2 + s, :], col, 7, None, ALU.logical_shift_right)
    last.then_inc(deg_step, 1)
    dve.wait_ge(deg_step, value(1))
    for s in range(sides):
        last = dve.tensor_copy(f[:, s::2, :], hi_i[:, s::2, :])
    last.then_inc(deg_step, 1)
    dve.wait_ge(deg_step, value(2))
    low, high = degree_views(k, b % 2)
    for s in range(sides):
        dve.tensor_tensor(low[s], k.iota[:, :].unsqueeze(1).to_broadcast([P, GROUP, P]),
                          f[:, s, :].unsqueeze(2).to_broadcast([P, GROUP, P]), ALU.is_equal)
        last = dve.tensor_tensor(high[s], k.iota[:, 0:NT].unsqueeze(1).to_broadcast([P, GROUP, NT]),
                                 f[:, 2 + s, :].unsqueeze(2).to_broadcast([P, GROUP, NT]), ALU.is_equal)
    last.then_inc(deg_ready[b % 2], 1)


def degree_views(k, b):
    words = k.w[:, :].bitcast(BF16)
    size = GROUP * (P + NT)
    low, high = [], []
    for s in range(2):
        at = (2 * b + s) * size
        low.append(words[:, at:at + GROUP * P].rearrange("p (t c) -> p t c", t=GROUP))
        high.append(words[:, at + GROUP * P:at + size].rearrange("p (t c) -> p t c", t=GROUP))
    return low, high


def degree_zero(pe, k, ps_deg, first):
    for s in range(len(ps_deg)):
        ins_ = pe.matmul(ps_deg[s][:, 0:NT], k.zero[:, :].bitcast(BF16), k.lower[:, 0:NT], start=first,
                         stop=not first)
    return ins_


def degree_matmuls(pe, k, b, ps_deg):
    low, high = degree_views(k, b % 2)
    for t in range(GROUP):
        for s in range(len(ps_deg)):
            ins_ = pe.matmul(ps_deg[s][:, 0:NT], low[s][:, t, :], high[s][:, t, :],
                             start=False, stop=False)
    return ins_


def finish_degrees(dve, k, ps_deg, done):
    for s, name in enumerate(("src", "dst")[:len(ps_deg)]):
        dve.tensor_copy(k.deg[name][:, :], ps_deg[s][:, 0:NT])
        dve.tensor_scalar(k.rdeg[name][:, :], ps_deg[s][:, 0:NT], 1.0, None, ALU.max).then_inc(done, 1)
        dve.wait_ge(done, 2 * s + 1)
        dve.reciprocal(k.rdeg[name][:, :], k.rdeg[name][:, :]).then_inc(done, 1)
        dve.wait_ge(done, 2 * s + 2)


def degree_stage(nc, k):
    with stage(nc) as (ctx, sem):
        idx_ready = [sem(f"deg_idx_ready{b}") for b in range(2)]
        deg_step = sem("deg_step")
        deg_ready = [sem(f"deg_onehot_ready{b}") for b in range(2)]
        counted = [sem(f"deg_counted{b}") for b in range(2)]
        done = sem("deg_done")
        ps_deg = [psum(nc, ctx, f"deg_ps{s}") for s in range(2)]
        block = ctx.enter_context(nc.Block())
        n = NG // 2

        @block.sync
        def _(sp):
            for b in range(2):
                sp.dma_start(k.idx[b][:, :], k.ins["cols"][b]).then_inc(idx_ready[b], 16)
            with sp.Fori(1, n) as i:
                for b in range(2):
                    sp.wait_ge(deg_ready[b], i)
                    sp.dma_start(k.idx[b][:, :], group_cols(k, 2 * i + b)).then_inc(idx_ready[b], 16)

        @block.vector
        def _(dve):
            with dve.Fori(0, n) as i:
                for b in range(2):
                    dve.wait_ge(idx_ready[b], i * 16 + 16)
                    dve.wait_ge(counted[b], i + 1)
                    degree_onehots(dve, k, b, b, deg_step, deg_ready, lambda j: i * 4 + 2 * b + j, 2)
            for b in range(2):
                dve.wait_ge(counted[b], n + 1 + b)
            finish_degrees(dve, k, ps_deg, done)

        @block.tensor
        def _(pe):
            for b in range(2):
                pe.sem_inc(counted[b])
            degree_zero(pe, k, ps_deg, True)
            with pe.Fori(0, n) as i:
                for b in range(2):
                    pe.wait_ge(deg_ready[b], i + 1)
                    degree_matmuls(pe, k, b, ps_deg).then_inc(counted[b], 1)
            degree_zero(pe, k, ps_deg, False).then_inc(counted[1], 1)


def zero_partials(eng, k, zeroed):
    for c in range(COPIES):
        eng.dma_start(dram_nm(k.part[c], NS), k.zero[:, :].unsqueeze(1).to_broadcast([P, NT + 1, D])
                      ).then_inc(zeroed, 16)
    eng.dma_start(k.tab["x3"][NP:NS, :], k.zero[:, :]).then_inc(zeroed, 16)


def zero_stage(nc, k):
    with stage(nc) as (ctx, sem):
        zeroed, x_loaded = sem("z_zeroed"), sem("z_x_loaded")
        block = ctx.enter_context(nc.Block())

        @block.sync
        def _(sp):
            sp.dma_start(nm3(k.x), dram_nm(k.ins["x"])).then_inc(x_loaded, 16)
            sp.wait_ge(x_loaded, 16)

        @block.scalar
        def _(act):
            zero_partials(act, k, zeroed)
            act.wait_ge(zeroed, 16 * ZERO_DMAS)


def group_cols(k, g):
    return k.ins["cols"][bass.ds(g, 1)].rearrange("o p c -> (o p) c")


def group_first(k, g):
    return k.ins["first"][0:1, bass.ds(g, 1)].to_broadcast([P, 1])


halves = [t % 2 * (GROUP // 2) + t // 2 for t in range(GROUP)]


def attr_matmuls(pe, k, ps, attr):
    for t in range(GROUP):
        h, q = t % 2, t // 2
        mm = pe.matmul(ps[:, h * 512 + q * D:h * 512 + (q + 1) * D],
                       attr[h * D:(h + 1) * D, q * P:(q + 1) * P],
                       mat(k, "We_edge", h * D), start=True, stop=True)
    return mm


def attr_sum(dve, out, ps, rows):
    return dve.tensor_tensor(
        out.rearrange("p (h q f) -> p h q f", h=2, f=D),
        ps[:, :].rearrange("p (h q f) -> p h q f", h=2, f=D)[:, :, 0:GROUP // 2, :],
        rows[:, :, 0:D].rearrange("p (q h) f -> p h q f", h=2), ALU.add)


def after(eng, sem, value):
    if not isinstance(value, int) or value > 0:
        eng.wait_ge(sem, value)


def fast_pass(nc, k, table, layer):
    degrees, edge_mlp = layer == "mean", layer == "edge"
    with stage(nc) as (ctx, sem):
        idx_ready = [sem(f"idx_ready{b}") for b in range(RING)]
        gathered = [sem(f"gathered{b}") for b in range(RING)]
        onehot_ready = [sem(f"onehot_ready{b}") for b in range(RING)]
        segmented = [sem(f"segmented{b}") for b in range(RING)]
        added = [sem(f"added{b}") for b in range(RING)]
        attr_ready = [sem(f"attr_ready{b}") for b in range(2)]
        attr_mm, mlp_sum = sem("attr_mm"), sem("mlp_sum")
        message = [sem(f"message{b}") for b in range(2)]
        counted = [sem(f"counted{b}") for b in range(2)]
        local_ready, cleared, done, x_loaded = sem("local_ready"), sem("cleared"), sem("deg_done"), sem("x_loaded")
        go, go_pe, go_sp = sem("pool_go"), sem("pe_go"), sem("sp_go")
        deg_step = sem("deg_step")
        deg_ready = [sem(f"deg_ready{b}") for b in range(2)]
        wide = D + degrees
        ps_seg = [psum(nc, ctx, f"ps_seg{b}", parts=D + 1) for b in range(2)]
        zeroes = {"mean": range(0, COPIES // 2), "sage1": range(COPIES // 2, COPIES)}.get(layer, ())
        work = NodeWork(nc, k, ctx, sem, layer, degrees, zeroes)
        if degrees:
            ps_deg = [psum(nc, ctx, "ps_deg")]
        if edge_mlp:
            ps_attr = psum(nc, ctx, "ps_attr", 1024)
            half = GROUP // 2
            attr = [k.w[:, b * half * P:(b + 1) * half * P] for b in range(2)]
            hid, msg = [[k.w[:, (2 * n + b) * GROUP * D:(2 * n + b + 1) * GROUP * D] for b in range(2)]
                        for n in (1, 2)]
        block = ctx.enter_context(nc.Block())

        def uses(j, u, n):
            return j * (SLOTS // n) + u // n

        def tiles_of(j, u):
            return LAST_TILES if isinstance(j, int) and j * SLOTS + u == NG - 1 else GROUP

        def landed(j, u):
            return uses(j, u, RING) * (16 * GROUP) + 16 * tiles_of(j, u)

        def no_chunk(u):
            return ()

        def one_chunk(c):
            return lambda u: ((c, u),)

        def two_chunks(u):
            c, first_step = BODIES - 2 + 2 * u // SLOTS, 3 * (u % (SLOTS // 2))
            if u == SLOTS - 2:
                return tuple((NCH - 1, step) for step in range(work.sums_at))
            return tuple((c, step) for step in range(first_step, min(first_step + 3, SLOTS)))

        @block.sync
        def _(sp):
            def body(j):
                for u in range(SLOTS):
                    b, n, g = u % RING, uses(j, u, RING), j * SLOTS + u
                    after(sp, gathered[b], n * (16 * GROUP))
                    after(sp, added[b], n)
                    sp.sem_inc(go_sp)
                    if edge_mlp:
                        after(sp, attr_mm, g - 1 if isinstance(j, int) else j * SLOTS + (u - 1))
                        sp.sem_inc(go_sp)
                        sp.dma_start(attr[u % 2], k.ins["attr"][:, bass.ds(g * (GROUP // 2 * P), GROUP // 2 * P)]
                                     ).then_inc(attr_ready[u % 2], 16)
                    sp.dma_start(k.idx[b][:, :], group_cols(k, g)).then_inc(idx_ready[b], 16)
                    sp.dma_start(k.first[b][:, :], group_first(k, g)).then_inc(idx_ready[b], 16)

            body(0)
            if degrees:
                sp.dma_start(nm3(k.x), dram_nm(k.ins["x"])).then_inc(x_loaded, 16)
            with sp.Fori(1, BODIES) as j:
                body(j)

        @block.gpsimd
        def _(pool):
            def body(j):
                for u in range(SLOTS):
                    b, n = u % RING, uses(j, u, RING)
                    pool.wait_ge(idx_ready[b], n * 32 + 32)
                    after(pool, segmented[b], n)
                    pool.sem_inc(go)
                    for t in range(tiles_of(j, u)):
                        pool.indirect_dma_start(
                            k.gath[b][:, t, 0:D], None, table[0:NP, :],
                            bass.IndirectOffsetOnAxis(ap=k.idx[b][:, t:t + 1], axis=0)
                        ).then_inc(gathered[b], 16)

            body(0)
            with pool.Fori(1, BODIES - 1) as j:
                body(j)
            body(BODIES - 1)
            for u in range(SLOTS - RING, SLOTS):
                pool.wait_ge(gathered[u % RING], landed(BODIES - 1, u))

        @block.vector
        def _(dve):
            def body(j, steps=no_chunk):
                for u in range(SLOTS):
                    b, n = u % RING, uses(j, u, RING)
                    dve.wait_ge(idx_ready[b], n * 32 + 32)
                    dve.tensor_tensor(k.local[b][:, :], k.idx[b][:, GROUP:2 * GROUP],
                                      k.first[b][:, 0:1].to_broadcast([P, GROUP]), ALU.subtract
                                      ).then_inc(local_ready, 1)
                    dve.wait_ge(local_ready, j * SLOTS + u + 1)
                    dve.tensor_tensor(k.oneh[u % 2][:, :, :],
                                      k.iota[:, :].unsqueeze(1).to_broadcast([P, GROUP, WINDOW]),
                                      k.local[b][:, :].unsqueeze(2).to_broadcast([P, GROUP, WINDOW]),
                                      ALU.is_equal).then_inc(onehot_ready[b], 1)
                    if degrees:
                        after(dve, counted[u % 2], uses(j, u, 2))
                        degree_onehots(dve, k, u, b, deg_step, deg_ready,
                                       lambda m: (j * SLOTS + u) * 2 + m, 1)
                    if edge_mlp:
                        dve.wait_ge(gathered[b], landed(j, u))
                        dve.wait_ge(attr_mm, j * SLOTS + u + 1)
                        attr_sum(dve, hid[u % 2], ps_attr, k.gath[b]).then_inc(mlp_sum, 1)
                    if u > 0:
                        add(u - 1, uses(j, u - 1, RING) + 1)
                    elif not isinstance(j, int) or j > 0:
                        add(SLOTS - 1, j * (SLOTS // RING))
                    for c, step in steps(u):
                        work.vector(dve, c, step)

            def add(u, count):
                b = u % RING
                at = dve.value_load(k.first[b][0:1, 0:1], min_val=0, max_val=NP)
                dve.wait_ge(segmented[b], count)
                window = k.acc[0:wide, bass.ds(at, WINDOW)]
                dve.tensor_tensor(window, window, ps_seg[u % 2][0:wide, 0:WINDOW], ALU.add).then_inc(added[b], 1)
                dve.wait_ge(added[b], count)

            dve.memset(k.acc[:, :], 0.0).then_inc(cleared, 1)
            dve.wait_ge(cleared, 1)
            work.vector_start(dve)
            body(0)
            if degrees:
                dve.wait_ge(x_loaded, 16)
            with dve.Fori(0, BODIES - 2) as c:
                body(c + 1, one_chunk(c))
            body(BODIES - 1, two_chunks)
            add(SLOTS - 1, NG // RING)
            for u in range(work.sums_at, SLOTS):
                work.vector(dve, NCH - 1, u)
            if degrees:
                for b in range(2):
                    dve.wait_ge(counted[b], NG // 2 + b)
                finish_degrees(dve, k, ps_deg, done)

        @block.scalar
        def _(act):
            def body(j, steps=no_chunk):
                for u in range(SLOTS):
                    if edge_mlp:
                        act.wait_ge(mlp_sum, j * SLOTS + u + 1)
                        act.activation(msg[u % 2], hid[u % 2], ACT.Relu).then_inc(message[u % 2], 1)
                    for c, step in steps(u):
                        if step == work.sums_at:
                            act.wait_ge(added[RING - 1], uses(j, u, RING))
                        work.scalar(act, c, step)

            work.scalar_start(act)
            if edge_mlp:
                body(0)
            if degrees:
                act.wait_ge(x_loaded, 16)
            with act.Fori(0, BODIES - 2) as c:
                body(c + 1, one_chunk(c))
            body(BODIES - 1, two_chunks)
            act.wait_ge(added[RING - 1], NG // RING)
            for u in range(work.sums_at, SLOTS):
                work.scalar(act, NCH - 1, u)
            work.scalar_end(act)

        @block.tensor
        def _(pe):
            def body(j, steps=no_chunk):
                for u in range(SLOTS):
                    b, n = u % RING, uses(j, u, RING)
                    if edge_mlp:
                        if not (isinstance(j, int) and j * SLOTS + u == NG - 1):
                            pe.wait_ge(mlp_sum, j * SLOTS + u + 1)
                            attr_products(j, u + 1)
                        pe.wait_ge(message[u % 2], uses(j, u, 2) + 1)
                        rows, place = msg[u % 2].rearrange("p (t f) -> p t f", f=D), halves
                    else:
                        pe.wait_ge(gathered[b], landed(j, u))
                        rows, place = k.gath[b], range(GROUP)
                    pe.wait_ge(onehot_ready[b], n + 1)
                    after(pe, added[(u - 2) % RING], n + 1 if u % RING >= 2 else n)
                    for t in range(tiles_of(j, u)):
                        mm = pe.matmul(ps_seg[u % 2][0:wide, 0:WINDOW], rows[:, place[t], 0:wide],
                                       k.oneh[u % 2][:, t, :], start=t == 0, stop=t == tiles_of(j, u) - 1)
                    mm.then_inc(segmented[b], 1)
                    if degrees:
                        pe.wait_ge(deg_ready[u % 2], uses(j, u, 2) + 1)
                        degree_matmuls(pe, k, u, ps_deg).then_inc(counted[u % 2], 1)
                    for c, step in steps(u):
                        work.tensor(pe, c, step)

            def attr_products(j, u):
                pe.wait_ge(attr_ready[u % 2], uses(j, u, 2) * 16 + 16)
                pe.sem_inc(go_pe)
                attr_matmuls(pe, k, ps_attr, attr[u % 2]).then_inc(attr_mm, 1)

            work.tensor_start(pe)
            if degrees:
                degree_zero(pe, k, ps_deg, True)
            if edge_mlp:
                attr_products(0, 0)
            body(0)
            with pe.Fori(0, BODIES - 2) as c:
                body(c + 1, one_chunk(c))
            body(BODIES - 1, two_chunks)
            if degrees:
                degree_zero(pe, k, ps_deg, False).then_inc(counted[1], 1)
            for u in range(work.sums_at, SLOTS):
                work.tensor(pe, NCH - 1, u)


def equality(dve, k, eq, srow, col, low, cnt, sidx, link):
    link(dve.tensor_tensor(eq, srow, col.unsqueeze(2).to_broadcast([P, GROUP, P]), ALU.is_equal))
    link(dve.tensor_tensor(low, eq, k.lower[:, :].unsqueeze(1).to_broadcast([P, GROUP, P]), ALU.mult))
    link(dve.tensor_reduce(cnt[:, 0:GROUP], low, AX.X, ALU.add))
    link(dve.tensor_scalar(cnt[:, GROUP:2 * GROUP], cnt[:, 0:GROUP], 0.5, None, ALU.is_lt))
    link(dve.tensor_scalar(cnt[:, 2 * GROUP:3 * GROUP], col, k.spare[:, 0:1], None, ALU.subtract))
    link(dve.tensor_tensor(cnt[:, 3 * GROUP:4 * GROUP], cnt[:, 2 * GROUP:3 * GROUP],
                           cnt[:, GROUP:2 * GROUP], ALU.mult))
    return dve.tensor_scalar(sidx, cnt[:, 3 * GROUP:4 * GROUP], k.spare[:, 0:1], None, ALU.add)


EQ_STEPS = 6


def general_pass(nc, k, table, by, edge_mlp=False):
    gather_at, scatter_at = (0, GROUP) if by == "dst" else (GROUP, 0)
    row_of = 1 if by == "dst" else 0
    with stage(nc) as (ctx, sem):
        loaded, gathered, step, ready = sem("g_loaded"), sem("g_gathered"), sem("g_step"), sem("g_ready")
        attr_mm, mlp_sum, message = sem("g_attr_mm"), sem("g_mlp_sum"), sem("g_message")
        combined, copied, go = sem("g_combined"), sem("g_copied"), sem("g_go")
        scattered = [sem(f"g_scattered{c}") for c in range(COPIES)]
        go_pe, go_sp = sem("g_pe_go"), sem("g_sp_go")
        ps_c = psum(nc, ctx, "g_ps_c")
        ps_a = psum(nc, ctx, "g_ps_a", 1024)
        wcol = lambda a, n: k.w[:, a:a + n]
        eq = wcol(1024, 1024).rearrange("p (t c) -> p t c", c=P)
        low = wcol(2048, 1024).rearrange("p (t c) -> p t c", c=P)
        attr = wcol(3072, 512)
        hid, msg = wcol(3584, 512), wcol(4096, 512)
        cnt = wcol(4608, 64)
        sidx = wcol(4672, GROUP).bitcast(I32)
        comb = k.gath[1]
        per = (3 if edge_mlp else 2) * 16
        block = ctx.enter_context(nc.Block())
        each = 16 * GROUP // COPIES

        @block.sync
        def _(sp):
            def load(g):
                sp.dma_start(k.idx[0][:, :], group_cols(k, g)).then_inc(loaded, 16)
                sp.dma_start(wcol(0, GROUP * P).bitcast(I32),
                             k.ins["rows_of"][bass.ds(g, 1), row_of, :].to_broadcast([P, GROUP * P])
                             ).then_inc(loaded, 16)
                if edge_mlp:
                    sp.dma_start(attr, k.ins["attr"][:, bass.ds(g * (GROUP // 2 * P), GROUP // 2 * P)]
                                 ).then_inc(loaded, 16)

            load(0)
            with sp.Fori(1, NG) as g:
                for c in range(COPIES):
                    sp.wait_ge(scattered[c], g * each)
                sp.sem_inc(go_sp)
                load(g)
            for c in range(COPIES):
                sp.wait_ge(scattered[c], NG * each)

        @block.gpsimd
        def _(pool):
            with pool.Fori(0, NG) as g:
                pool.wait_ge(loaded, g * per + per)
                pool.sem_inc(go)
                for t in range(GROUP):
                    pool.indirect_dma_start(
                        k.gath[0][:, t, 0:D], None, table[0:NP, :],
                        bass.IndirectOffsetOnAxis(ap=k.idx[0][:, gather_at + t:gather_at + t + 1], axis=0)
                    ).then_inc(gathered, 16)
                pool.wait_ge(ready, g + 1)
                pool.wait_ge(copied, g + 1)
                pool.sem_inc(go)
                for t in range(GROUP):
                    c = t % COPIES
                    if t >= COPIES:
                        pool.wait_ge(scattered[c], g * each + 16 * (t // COPIES))
                        pool.sem_inc(go)
                    pool.indirect_dma_start(
                        k.part[c], bass.IndirectOffsetOnAxis(ap=sidx[:, t:t + 1], axis=0),
                        comb[:, t, 0:D], None, compute_op=ALU.add).then_inc(scattered[c], 16)
            pool.wait_ge(gathered, NG * 16 * GROUP)
            for c in range(COPIES):
                pool.wait_ge(scattered[c], NG * each)

        @block.vector
        def _(dve):
            with dve.Fori(0, NG) as g:
                n = [0]

                def link(ins_):
                    n[0] += 1
                    ins_.then_inc(step, 1)
                    dve.wait_ge(step, g * EQ_STEPS + n[0])

                dve.wait_ge(loaded, g * per + per)
                equality(dve, k, eq, wcol(0, GROUP * P).bitcast(I32).rearrange("p (t c) -> p t c", c=P),
                         k.idx[0][:, scatter_at:scatter_at + GROUP], low, cnt, sidx, link).then_inc(ready, 1)
                assert n[0] == EQ_STEPS
                if edge_mlp:
                    dve.wait_ge(gathered, g * (16 * GROUP) + 16 * GROUP)
                    dve.wait_ge(attr_mm, g + 1)
                    attr_sum(dve, hid, ps_a, k.gath[0]).then_inc(mlp_sum, 1)

        @block.scalar
        def _(act):
            with act.Fori(0, NG) as g:
                if edge_mlp:
                    act.wait_ge(mlp_sum, g + 1)
                    act.activation(msg, hid, ACT.Relu).then_inc(message, 1)
                act.wait_ge(combined, g + 1)
                act.copy(comb[:, :, 0:D], ps_c[:, :].rearrange("p (t f) -> p t f", f=D)).then_inc(copied, 1)

        @block.tensor
        def _(pe):
            with pe.Fori(0, NG) as g:
                if edge_mlp:
                    pe.wait_ge(loaded, g * per + per)
                    pe.sem_inc(go_pe)
                    attr_matmuls(pe, k, ps_a, attr).then_inc(attr_mm, 1)
                    pe.wait_ge(message, g + 1)
                    rows = msg.rearrange("p (t f) -> p t f", f=D)
                    place = halves
                else:
                    pe.wait_ge(gathered, g * (16 * GROUP) + 16 * GROUP)
                    rows, place = k.gath[0], range(GROUP)
                pe.wait_ge(ready, g + 1)
                for t in range(GROUP):
                    mm = pe.matmul(ps_c[:, t * D:(t + 1) * D], eq[:, t, :], rows[:, place[t], 0:D],
                                   start=True, stop=True)
                mm.then_inc(combined, 1)


def reverse_pass(nc, k, table):
    with stage(nc) as (ctx, sem):
        idx_ready = [sem(f"r_idx_ready{b}") for b in range(RING)]
        win_ready = [sem(f"r_win_ready{b}") for b in range(RING)]
        ready = [sem(f"r_ready{b}") for b in range(RING)]
        oh_ready = [sem(f"r_oh_ready{b}") for b in range(RING)]
        mixed, mix_copied, combined, copied, free = (
            sem("r_mixed"), sem("r_mix_copied"), sem("r_combined"), sem("r_copied"), sem("r_free"))
        scattered = [sem(f"r_scattered{c}") for c in range(COPIES)]
        step, go = sem("r_step"), sem("r_go")
        ps_mix = [psum(nc, ctx, f"r_ps_mix{b}", 1024) for b in range(2)]
        ps_c = [psum(nc, ctx, f"r_ps_c{b}") for b in range(2)]
        words, half = GROUP * P, GROUP * P // 2
        area = 3 * half
        onehots = lambda b, n: k.w[:, b * area + n * half:b * area + (n + 1) * half].bitcast(BF16).rearrange(
            "p (t c) -> p t c", c=P)
        eq, low, oh = ([onehots(b, n) for b in range(RING)] for n in range(3))
        srow = [k.y[:, b * words:(b + 1) * words].bitcast(I32) for b in range(RING)]
        mix = [k.h[:, b * words:(b + 1) * words] for b in range(RING)]
        win = [k.h[:, RING * words + b * D:RING * words + (b + 1) * D] for b in range(RING)]
        rest = lambda b, at, n: k.y[:, RING * words + b * 64 + at:RING * words + b * 64 + at + n]
        cnt = [rest(b, 0, 4 * GROUP) for b in range(RING)]
        sidx = [rest(b, 4 * GROUP, GROUP).bitcast(I32) for b in range(RING)]
        comb = k.gath
        total = [16 * (NG if c < LAST_TILES else NG - 1) for c in range(COPIES)]
        assert RING * area <= NT * D and RING * (words + D) <= NT * D
        block = ctx.enter_context(nc.Block())

        @block.sync
        def _(sp):
            def load(b, g, i):
                sp.dma_start(k.idx[b][:, :], group_cols(k, g)).then_inc(idx_ready[b], 16)
                sp.dma_start(k.first[b][:, :], group_first(k, g)).then_inc(idx_ready[b], 16)
                sp.dma_start(srow[b], k.ins["rows_of"][bass.ds(g, 1), 0, :].to_broadcast([P, words])
                             ).then_inc(idx_ready[b], 16)
                sp.wait_ge(idx_ready[b], i * 48 + 48)
                sp.sem_inc(go)
                at = sp.value_load(k.first[b][0:1, 0:1], min_val=0, max_val=NP)
                sp.dma_start(win[b], table[bass.ds(at, WINDOW), :]).then_inc(win_ready[b], 16)

            for b in range(RING):
                load(b, b, 0)
            with sp.Fori(1, NG // RING) as i:
                for b in range(RING):
                    sp.wait_ge(combined, (i - 1) * RING + b + 1)
                    sp.wait_ge(oh_ready[b], i)
                    sp.wait_ge(ready[b], i)
                    sp.sem_inc(go)
                    load(b, i * RING + b, i)
            for c in range(COPIES):
                sp.wait_ge(scattered[c], total[c])

        @block.vector
        def _(dve):
            with dve.Fori(0, NG // RING) as i:
                for b in range(RING):
                    n = [0]

                    def link(ins_):
                        n[0] += 1
                        ins_.then_inc(step, 1)
                        dve.wait_ge(step, (i * RING + b) * (EQ_STEPS + 1) + n[0])

                    dve.wait_ge(idx_ready[b], i * 48 + 48)
                    dve.wait_ge(mixed, i * RING + b + 1)
                    dve.wait_ge(free, i * RING + b + 1)
                    link(dve.tensor_tensor(k.local[b][:, :], k.idx[b][:, GROUP:2 * GROUP],
                                           k.first[b][:, 0:1].to_broadcast([P, GROUP]), ALU.subtract))
                    dve.tensor_tensor(oh[b], k.iota[:, :].unsqueeze(1).to_broadcast([P, GROUP, P]),
                                      k.local[b][:, :].unsqueeze(2).to_broadcast([P, GROUP, P]),
                                      ALU.is_equal).then_inc(oh_ready[b], 1)
                    equality(dve, k, eq[b], srow[b].rearrange("p (t c) -> p t c", c=P),
                             k.idx[b][:, 0:GROUP], low[b], cnt[b], sidx[b], link).then_inc(ready[b], 1)

        @block.tensor
        def _(pe):
            pe.sem_inc(mixed, RING)

            def mix_of(b, i):
                pe.wait_ge(oh_ready[b], i + 1)
                pe.wait_ge(ready[b], i + 1)
                pe.wait_ge(mix_copied, i * RING + b + RING - 1)
                for t in range(GROUP):
                    mm = pe.matmul(ps_mix[b % 2][:, t * P:(t + 1) * P], oh[b][:, t, :], eq[b][:, t, :],
                                   start=True, stop=True)
                mm.then_inc(mixed, 1)

            def rows_of(b, i):
                pe.wait_ge(mix_copied, i * RING + b + RING + 1)
                pe.wait_ge(win_ready[b], i * 16 + 16)
                pe.wait_ge(copied, i * RING + b + RING - 1)
                for t in range(GROUP):
                    mm = pe.matmul(ps_c[b % 2][:, t * D:(t + 1) * D], mix[b][:, t * P:(t + 1) * P], win[b],
                                   start=True, stop=True)
                mm.then_inc(combined, 1)

            with pe.Fori(0, NG // RING) as i:
                for b in range(RING):
                    mix_of(b, i)
                    rows_of(b, i)

        @block.scalar
        def _(act):
            act.sem_inc(mix_copied, RING)
            act.sem_inc(copied, RING)
            with act.Fori(0, NG // RING) as i:
                for b in range(RING):
                    act.wait_ge(mixed, i * RING + b + RING + 1)
                    act.copy(mix[b], ps_mix[b % 2][:, :]).then_inc(mix_copied, 1)
                    act.wait_ge(combined, i * RING + b + 1)
                    act.wait_ge(free, i * RING + b + 1)
                    act.copy(comb[b][:, :, 0:D], ps_c[b % 2][:, :].rearrange("p (t f) -> p t f", f=D)
                             ).then_inc(copied, 1)

        @block.gpsimd
        def _(pool):
            pool.sem_inc(free, RING)

            def scatter(b, i):
                first = isinstance(i, int) and i * RING + b == 0
                pool.wait_ge(ready[b], i + 1)
                pool.wait_ge(copied, i * RING + b + RING + 1)
                last = isinstance(i, int) and i * RING + b == NG - 1
                for t in range(LAST_TILES if last else GROUP):
                    if not first:
                        pool.wait_ge(scattered[t], (i * RING + b) * 16)
                        if t == GROUP - 1:
                            pool.sem_inc(free)
                    pool.sem_inc(go)
                    pool.indirect_dma_start(
                        k.part[t], bass.IndirectOffsetOnAxis(ap=sidx[b][:, t:t + 1], axis=0),
                        comb[b][:, t, 0:D], None, compute_op=ALU.add).then_inc(scattered[t], 16)

            for b in range(RING):
                scatter(b, 0)
            with pool.Fori(1, NG // RING - 1) as i:
                for b in range(RING):
                    scatter(b, i)
            for b in range(RING):
                scatter(b, NG // RING - 1)
            for c in range(COPIES):
                pool.wait_ge(scattered[c], total[c])


def gather_partials(nc, k):
    out = k.y
    with stage(nc) as (ctx, sem):
        loaded, step, zeroed = sem("p_loaded"), sem("p_step"), sem("p_zeroed")
        turned, moved, staged, row_free = sem("p_turned"), sem("p_moved"), sem("p_staged"), sem("p_row_free")
        go = sem("p_go")
        rows = [k.chunk[b][:, :] for b in range(2)]
        ps = [psum(nc, ctx, f"p_ps{b}", 1024, parts=D) for b in range(2)]
        block = ctx.enter_context(nc.Block())

        @block.sync
        def _(sp):
            sp.dma_start(nm3(out), dram_nm(k.part[0])).then_inc(loaded, 16)
            for c in range(1, COPIES):
                if c > 1:
                    sp.wait_ge(step, c - 1)
                sp.dma_start(nm3(k.w), dram_nm(k.part[c])).then_inc(loaded, 16)
                sp.wait_ge(loaded, 16 * (c + 1))
            zero_partials(sp, k, zeroed)
            sp.wait_ge(zeroed, 16 * ZERO_DMAS)

        @block.vector
        def _(dve):
            for c in range(1, COPIES):
                dve.wait_ge(loaded, 16 * (c + 1))
                dve.tensor_tensor(out[:, :], out[:, :], k.w[:, :], ALU.add).then_inc(step, 1)
                dve.wait_ge(step, c)

        @block.gpsimd
        def _(pool):
            pool.wait_ge(step, COPIES - 1)
            with pool.Fori(0, NCH // 2) as i:
                for b in range(2):
                    pool.wait_ge(row_free, 2 * i + b + 1)
                    pool.tensor_copy(rows[b], out[:, bass.ds((2 * i + b) * CW, CW)]).then_inc(staged, 1)

        @block.tensor
        def _(pe):
            with pe.Fori(0, NCH // 2) as i:
                for b in range(2):
                    pe.wait_ge(staged, 2 * i + b + 1)
                    pe.wait_ge(moved, 2 * i + b + 1)
                    pe.sem_inc(go)
                    for j in range(CT):
                        mm = pe.transpose(ps[b][:, j * P:(j + 1) * P], rows[b][:, j * D:(j + 1) * D],
                                          k.ident[:, :])
                    mm.then_inc(turned, 1)

        @block.scalar
        def _(act):
            act.sem_inc(moved, 2)
            act.sem_inc(row_free, 2)
            with act.Fori(0, NCH // 2) as i:
                for b in range(2):
                    act.wait_ge(turned, 2 * i + b + 1)
                    act.sem_inc(row_free)
                    act.copy(k.acc[0:D, bass.ds((2 * i + b) * CF, CF)], ps[b][:, 0:CF]).then_inc(moved, 1)



LAYERS = {
    "mean": dict(source="x", self=("W0_self", "b0"), agg="W0_agg"),
    "sage1": dict(source="x", self=("W1_self", "b1"), agg="W1_agg"),
    "sage2": dict(source="h", self=("W2_self", "b2"), agg="W2_agg", then=(("Wlin", "blin"), ("We_node", "be"))),
    "edge": dict(source="x", self=("Wn_self", "bn"), agg="Wn_agg"),
    "both": dict(source="partials", self=("W3_bwd", "zero"), agg="W3_fwd"),
}
LINKS = {"mean": 22, "sage1": 2, "sage2": 11, "edge": 11, "both": 11 + COPIES - 1}


class NodeWork:

    def __init__(self, nc, k, ctx, sem, layer, counting=False, zeroes=()):
        self.k, self.layer, self.spec = k, layer, LAYERS[layer]
        self.units = 1 + len(self.spec.get("then", ()))
        self.rows_ready, self.turned, self.moved = sem("w_rows_ready"), sem("w_turned"), sem("w_moved")
        self.product, self.consumed, self.step = sem("w_product"), sem("w_consumed"), sem("w_step")
        self.loaded, self.stored, self.go = sem("w_loaded"), sem("w_stored"), sem("w_go")
        self.first_mm, self.first_moved = sem("w_first_mm"), sem("w_first_moved")
        self.var_ready, self.std_ready, self.result = sem("w_var_ready"), sem("w_std_ready"), sem("w_result")
        self.h_ready, self.h_turned = sem("w_h_ready"), sem("w_h_turned")
        self.sums_moved = sem("w_sums_moved")
        self.copied, self.source_free = sem("w_copied"), sem("w_source_free")
        self.ps_turn = psum(nc, ctx, "w_ps_turn", 1024, parts=D)
        self.ps_self, self.ps_agg = psum(nc, ctx, "w_ps_self"), psum(nc, ctx, "w_ps_agg")
        self.xT, self.sT, self.s2T = k.xT[0][0:D, :], k.xT[1], k.sT[0]
        self.rows, self.t, self.y, self.q = k.chunk
        self.n_links = 0
        self.sums_at = 5 if layer == "both" else 4
        self.wide = D + counting
        self.counting = counting
        self.zeroes = zeroes

    def count(self, c, unit=0):
        return c * self.units + unit + 1

    def of(self, buffer, c):
        return buffer[:, bass.ds(c * CW, CW)] if not isinstance(c, int) else buffer[:, c * CW:(c + 1) * CW]

    def of_nodes(self, values, c):
        return over_features(self.part(values, c), CT)

    def part(self, values, c):
        return values[:, bass.ds(c * CT, CT)] if not isinstance(c, int) else values[:, c * CT:(c + 1) * CT]

    def dram(self, table, c):
        part = table[bass.ds(c * CF, CF), :] if not isinstance(c, int) else table[c * CF:(c + 1) * CF, :]
        return part.rearrange("(t p) f -> p t f", p=P)

    def link(self, dve, c, ins):
        self.n_links += 1
        ins.then_inc(self.step, 1)
        dve.wait_ge(self.step, c * LINKS[self.layer] + self.n_links)

    def turn(self, pe, c, unit):
        pe.wait_ge(self.rows_ready, self.count(c, unit))
        pe.sem_inc(self.go)
        for j in range(CT):
            mm = pe.transpose(self.ps_turn[:, j * P:(j + 1) * P], self.rows[:, j * D:(j + 1) * D],
                              self.k.ident[:, :])
        mm.then_inc(self.turned, 1)

    def multiply(self, pe, c, unit, matrix, bias, alone=True):
        k = self.k
        pe.wait_ge(self.consumed, self.count(c, unit))
        pe.matmul(self.ps_self[:, 0:CW].rearrange("p (t f) -> p t f", f=D), k.ones[0:1, :],
                  bias_row(k, bias), start=True, stop=False, skip_group_check=True)
        pe.wait_ge(self.moved, self.count(c, unit))
        pe.sem_inc(self.go)
        for j in range(CT):
            mm = pe.matmul(self.ps_self[:, j * D:(j + 1) * D], self.xT[:, j * P:(j + 1) * P],
                           mat(k, matrix), start=False, stop=self.layer != "edge", skip_group_check=True)
        if alone:
            mm.then_inc(self.product, 1)

    def multiply_sums(self, pe, c, agg):
        k = self.k
        pe.wait_ge(self.sums_moved, c + 1)
        pe.sem_inc(self.go)
        if self.layer == "edge":
            for h in range(2):
                mm = pe.matmul(self.ps_turn[:, h * 512:h * 512 + CF // 2], mat(k, "We_out"),
                               self.sT[0:D, h * (CF // 2):(h + 1) * (CF // 2)], start=True, stop=True)
            mm.then_inc(self.first_mm, 1)
            return
        for j in range(CT):
            mm = pe.matmul(self.ps_agg[:, j * self.wide:(j + 1) * self.wide],
                           self.sT[0:self.wide, j * P:(j + 1) * P],
                           k.agg_count[:, :] if self.counting else mat(k, agg),
                           start=True, stop=True, skip_group_check=True)
        mm.then_inc(self.product, 1)

    def tensor(self, pe, c, slot):
        k, layer = self.k, self.layer
        late = layer == "both"
        if slot == 1 + late:
            self.turn(pe, c, 0)
        if slot == 3 + late:
            self.multiply(pe, c, 0, *self.spec["self"], alone=False)
        if slot == self.sums_at:
            self.multiply_sums(pe, c, self.spec["agg"])
        if layer == "edge" and slot == 5:
            pe.wait_ge(self.first_moved, self.count(c))
            for j in range(CT):
                mm = pe.matmul(self.ps_self[:, j * D:(j + 1) * D], self.s2T[:, j * P:(j + 1) * P],
                               mat(k, "Wn_agg"), start=False, stop=True, skip_group_check=True)
            mm.then_inc(self.product, 1)
        if layer == "mean" and slot == 8:
            pe.wait_ge(self.h_ready, c + 1)
            pe.sem_inc(self.go)
            for j in range(CT):
                mm = pe.transpose(self.ps_turn[:, j * P:(j + 1) * P], self.rows[:, j * D:(j + 1) * D],
                                  k.ident[:, :])
            mm.then_inc(self.h_turned, 1)
        if layer == "sage2":
            for unit, at in ((1, 5), (2, 11)):
                if slot == at:
                    self.turn(pe, c, unit)
                if slot == at + 2:
                    self.multiply(pe, c, unit, *self.spec["then"][unit - 1])

    def move(self, act, c, unit):
        act.wait_ge(self.turned, self.count(c, unit))
        act.wait_ge(self.product, self.count(c, unit))
        act.copy(self.xT[:, :], self.ps_turn[:, 0:CF]).then_inc(self.moved, 1)

    def sqrt(self, act, c, width=CT):
        act.wait_ge(self.var_ready, c + 1)
        act.activation(self.k.stat[1][:, 0:width], self.k.stat[0][:, 0:width], ACT.Sqrt
                       ).then_inc(self.std_ready, 1)

    def store(self, act, c, table, rows):
        act.dma_start(self.dram(table, c), rows.rearrange("p (t f) -> p t f", f=D)).then_inc(self.stored, 16)

    def scalar(self, act, c, slot):
        k, layer = self.k, self.layer
        late = layer == "both"
        if slot == 0:
            if late:
                act.wait_ge(self.source_free, c + 1)
                act.sem_inc(self.go)
                for n in range(COPIES):
                    act.dma_start(k.parts[:, n, :].rearrange("p (t f) -> p t f", f=D),
                                  self.dram(k.part[n], c)).then_inc(self.loaded, 16)
            else:
                if layer == "mean":
                    act.wait_ge(self.source_free, c + 1)
                    act.sem_inc(self.go)
                act.copy(self.rows[:, :], self.of(k.x if self.spec["source"] == "x" else k.h, c)
                         ).then_inc(self.rows_ready, 1)
        if slot == 2 + late:
            self.move(act, c, 0)
        if slot == self.sums_at:
            at = bass.ds(c * CF, CF) if not isinstance(c, int) else slice(c * CF, (c + 1) * CF)
            act.copy(self.sT[0:self.wide, :], self.k.acc[0:self.wide, at]).then_inc(self.sums_moved, 1)
        if layer == "mean" and slot == 6:
            self.sqrt(act, c)
        if layer == "mean" and slot == 9:
            act.wait_ge(self.h_turned, c + 1)
            act.sem_inc(self.go)
            act.copy(k.acc[0:D, bass.ds(c * CF, CF)] if not isinstance(c, int) else
                     k.acc[0:D, c * CF:(c + 1) * CF], self.ps_turn[:, 0:CF])
        zero_at = SLOTS - 2 * len(self.zeroes)
        if slot >= zero_at and slot % 2 == 0 and not (isinstance(c, int) and c == NCH - 1):
            part = k.part[self.zeroes[(slot - zero_at) // 2]]
            if isinstance(c, int) and c == NCH - 2:
                act.dma_start(part[c * CF:NS, :].rearrange("(t p) f -> p t f", p=P),
                              k.zero[:, :].unsqueeze(1).to_broadcast([P, 2 * CT + 1, D])).then_inc(self.stored, 16)
            else:
                act.dma_start(self.dram(part, c), k.zero[:, :].unsqueeze(1).to_broadcast([P, CT, D])
                              ).then_inc(self.stored, 16)
        if self.counting and isinstance(c, int) and c == NCH - 2 and slot == 7:
            act.dma_start(k.tab["x3"][NP:NS, :], k.zero[:, :]).then_inc(self.stored, 16)
        if layer == "sage1" and slot == 5:
            act.wait_ge(self.result, c + 1)
            act.sem_inc(self.go)
            self.store(act, c, k.tab["h1"], self.of(k.h, c))
        if layer == "sage2":
            if slot in (6, 12):
                self.move(act, c, slot // 6)
            if slot == 9:
                self.sqrt(act, c)
            if slot == 14:
                act.wait_ge(self.product, self.count(c, 2) + 1)
                act.wait_ge(self.stored, c * 16 + 16)
                act.copy(self.q[:, :], self.ps_self[:, 0:CW]).then_inc(self.copied, 1)
                act.sem_inc(self.consumed)
            if slot == 15:
                act.wait_ge(self.copied, c + 1)
                act.sem_inc(self.go)
                self.store(act, c, k.tab["pre"], self.q[:, :])
        if layer == "edge":
            if slot == 4:
                act.wait_ge(self.first_mm, self.count(c))
                act.copy(self.s2T[:, :].rearrange("p (a c) -> p a c", a=2),
                         self.ps_turn[:, :].rearrange("p (a c) -> p a c", a=2)[:, :, 0:CF // 2]
                         ).then_inc(self.first_moved, 1)
            if slot == 7:
                self.sqrt(act, c)
            if slot == 9:
                act.wait_ge(self.result, c + 1)
                act.sem_inc(self.go)
                self.store(act, c, k.tab["x3"], self.of(k.x, c))
        if late:
            if slot == 7:
                self.sqrt(act, c)
            if slot == 9:
                act.wait_ge(self.result, c + 1)
                act.sem_inc(self.go)
                if isinstance(c, int) and c == NCH - 1:
                    full = (CT - 1) * P
                    act.dma_start(k.out[c * CF:c * CF + full, :].rearrange("(t p) f -> p t f", p=P),
                                  self.of(k.x, c).rearrange("p (t f) -> p t f", f=D)[:, 0:CT - 1, :]
                                  ).then_inc(self.stored, 16)
                    act.dma_start(k.out[c * CF + full:N, :], k.x[0:LAST, (NT - 1) * D:NT * D]
                                  ).then_inc(self.stored, 16)
                else:
                    self.store(act, c, k.out, self.of(k.x, c))

    def scalar_end(self, act):
        stores = {"mean": self.counting, "both": NCH + 1}.get(self.layer, NCH)
        act.wait_ge(self.stored, 16 + 16 * (stores + len(self.zeroes) * (NCH - 1)))

    def tensor_start(self, pe):
        pe.sem_inc(self.product)

    def scalar_start(self, act):
        act.sem_inc(self.stored, 16)

    def vector_start(self, dve):
        dve.sem_inc(self.consumed)
        dve.sem_inc(self.source_free)
        if self.layer == "mean":
            dve.memset(self.k.sums[:, :], 0.0)
            dve.memset(self.k.h[:, 0:2 * CW], 0.0)
            dve.memset(self.k.is_first[:, :], 1.0)

    def combine(self, dve, c, out, relu):
        k, link = self.k, self.link
        dve.wait_ge(self.product, self.count(c) + 1)
        o3 = lambda t: t.rearrange("p (t f) -> p t f", f=D)
        if self.layer == "edge":
            link(dve, c, dve.tensor_tensor(o3(self.t[:, :]), self.of_nodes(k.deg["dst"], c),
                                           over_tiles(k.be2w[:, :], CT), ALU.mult))
        else:
            products = self.ps_agg[:, 0:CT * self.wide].rearrange("p (t f) -> p t f", f=self.wide)
            if self.counting:
                degree = products[:, :, D:D + 1].rearrange("p t o -> p (t o)")
                dve.tensor_copy(self.part(k.deg["dst"], c), degree)
                link(dve, c, dve.tensor_scalar(k.stat[2][:, 0:CT], degree, 1.0, None, ALU.max))
                link(dve, c, dve.reciprocal(self.part(k.rdeg["dst"], c), k.stat[2][:, 0:CT]))
            link(dve, c, dve.tensor_tensor(o3(self.t[:, :]), products[:, :, 0:D],
                                           self.of_nodes(k.rdeg["dst"], c), ALU.mult))
        if not relu:
            return dve.tensor_tensor(out, self.t[:, :], self.ps_self[:, 0:CW], ALU.add)
        link(dve, c, dve.tensor_tensor(self.t[:, :], self.t[:, :], self.ps_self[:, 0:CW], ALU.add))
        return dve.tensor_scalar(out, self.t[:, :], 0.0, None, ALU.max)

    def norm_begin(self, dve, c):
        k, link, y3 = self.k, self.link, self.y[:, :].rearrange("p (t f) -> p t f", f=D)
        s = k.stat[2]
        link(dve, c, dve.tensor_reduce(s[:, 0:CT], y3, AX.X, ALU.add))
        link(dve, c, dve.tensor_scalar(s[:, 0:CT], s[:, 0:CT], 1.0 / D, None, ALU.mult))
        link(dve, c, dve.tensor_tensor(y3, y3, over_features(s[:, 0:CT], CT), ALU.subtract))
        link(dve, c, dve.tensor_tensor(self.t[:, :], self.y[:, :], self.y[:, :], ALU.mult))
        link(dve, c, dve.tensor_reduce(s[:, 0:CT], self.t[:, :].rearrange("p (t f) -> p t f", f=D),
                                       AX.X, ALU.add))
        dve.tensor_scalar(k.stat[0][:, 0:CT], s[:, 0:CT], 1.0 / D, LN_EPS, ALU.mult, ALU.add
                          ).then_inc(self.var_ready, 1)

    def norm_end(self, dve, c):
        k, y3 = self.k, self.y[:, :].rearrange("p (t f) -> p t f", f=D)
        dve.wait_ge(self.std_ready, c + 1)
        self.link(dve, c, dve.reciprocal(k.stat[3][:, 0:CT], k.stat[1][:, 0:CT]))
        scale = over_features(k.stat[3][:, 0:CT], CT)
        if self.layer == "sage2":
            dve.tensor_tensor(self.rows[:, :].rearrange("p (t f) -> p t f", f=D), y3, scale,
                              ALU.mult).then_inc(self.rows_ready, 1)
        dve.tensor_tensor(self.of(k.x, c).rearrange("p (t f) -> p t f", f=D), y3, scale,
                          ALU.mult).then_inc(self.result, 1)

    def mask_last(self, dve, c, rows):
        last = rows[:, (CT - 1) * D:CT * D]
        self.link(dve, c, dve.tensor_scalar(last, last, self.k.mask[:, 0:1], None, ALU.mult))

    def vector(self, dve, c, slot):
        k, layer, link = self.k, self.layer, self.link
        if slot == 0:
            self.n_links = 0
        if layer == "mean":
            if slot == 4:
                link(dve, c, self.combine(dve, c, self.y[:, :], False))
                dve.sem_inc(self.consumed)
                link(dve, c, dve.tensor_tensor(self.t[:, :], self.y[:, :], self.y[:, :], ALU.mult))
                dve.tensor_reduce(k.stat[0][:, 0:CT], self.t[:, :].rearrange("p (t f) -> p t f", f=D),
                                  AX.X, ALU.add).then_inc(self.var_ready, 1)
            if slot == 7:
                dve.wait_ge(self.std_ready, c + 1)
                link(dve, c, dve.tensor_scalar(k.stat[2][:, 0:CT], k.stat[1][:, 0:CT], L2_EPS, None, ALU.max))
                link(dve, c, dve.reciprocal(k.stat[3][:, 0:CT], k.stat[2][:, 0:CT]))
                link(dve, c, dve.tensor_tensor(
                    self.t[:, :].rearrange("p (t f) -> p t f", f=D),
                    self.y[:, :].rearrange("p (t f) -> p t f", f=D),
                    over_features(k.stat[3][:, 0:CT], CT), ALU.mult))
                link(dve, c, dve.tensor_scalar(self.rows[:, :], self.t[:, :], 0.0, None, ALU.max))
                if isinstance(c, int) and c == NCH - 1:
                    self.mask_last(dve, c, self.rows)
                dve.sem_inc(self.h_ready)
                link(dve, c, dve.tensor_scalar(self.q[:, :], self.rows[:, :], k.is_first[:, 0:1], None, ALU.mult))
                link(dve, c, dve.tensor_tensor(k.base, k.base, self.q[:, :], ALU.add))
                dve.memset(k.is_first[:, :], 0.0)
                link(dve, c, dve.tensor_tensor(self.q[:, :], self.rows[:, :], k.base, ALU.subtract))
                dve.sem_inc(self.source_free)
                if isinstance(c, int) and c == NCH - 1:
                    self.mask_last(dve, c, self.q)
                link(dve, c, dve.tensor_tensor(k.sums[:, :], k.sums[:, :], self.q[:, :], ALU.add))
                link(dve, c, dve.tensor_tensor(self.q[:, :], self.q[:, :], self.q[:, :], ALU.mult))
                link(dve, c, dve.tensor_tensor(k.squares, k.squares, self.q[:, :], ALU.add))
            if slot == 10:
                t3 = self.t[:, :].rearrange("p (t f) -> p t f", f=D)
                link(dve, c, dve.tensor_scalar(self.t[:, :], self.of(k.x, c), 2.0, None, ALU.mult))
                link(dve, c, dve.tensor_tensor(t3, t3, over_tiles(k.beta[:, :], CT), ALU.add))
                link(dve, c, dve.tensor_reduce(k.stat[2][:, 0:CT], t3, AX.X, ALU.add))
                link(dve, c, dve.tensor_scalar(k.stat[2][:, 0:CT], k.stat[2][:, 0:CT], 1.0 / D, None, ALU.mult))
                link(dve, c, dve.tensor_tensor(self.of(k.y, c).rearrange("p (t f) -> p t f", f=D), t3,
                                               over_features(k.stat[2][:, 0:CT], CT), ALU.subtract))
        if layer == "sage1" and slot == 4:
            self.combine(dve, c, self.of(k.h, c), True).then_inc(self.result, 1)
            dve.sem_inc(self.consumed)
        if layer == "sage2":
            if slot == 4:
                self.combine(dve, c, self.rows[:, :], True).then_inc(self.rows_ready, 1)
                dve.sem_inc(self.consumed)
            if slot == 8:
                dve.wait_ge(self.product, self.count(c, 1) + 1)
                link(dve, c, dve.tensor_tensor(self.y[:, :], self.ps_self[:, 0:CW], self.of(k.x, c), ALU.add))
                dve.sem_inc(self.consumed)
                self.norm_begin(dve, c)
            if slot == 10:
                self.norm_end(dve, c)
        if layer == "edge":
            if slot == 6:
                link(dve, c, self.combine(dve, c, self.y[:, :], True))
                dve.sem_inc(self.consumed)
                link(dve, c, dve.tensor_tensor(self.y[:, :], self.y[:, :], self.of(k.x, c), ALU.add))
                self.norm_begin(dve, c)
            if slot == 8:
                self.norm_end(dve, c)
        if layer == "both":
            if slot == 1:
                dve.wait_ge(self.loaded, c * (16 * COPIES) + 16 * COPIES)
                for n in range(1, COPIES):
                    link(dve, c, dve.tensor_tensor(k.parts[:, 0, :], k.parts[:, 0, :], k.parts[:, n, :], ALU.add))
                dve.tensor_tensor(self.rows[:, :].rearrange("p (t f) -> p t f", f=D),
                                  k.parts[:, 0, :].rearrange("p (t f) -> p t f", f=D),
                                  self.of_nodes(k.rdeg["src"], c), ALU.mult).then_inc(self.rows_ready, 1)
                dve.sem_inc(self.source_free)
            if slot == 6:
                link(dve, c, self.combine(dve, c, self.y[:, :], True))
                dve.sem_inc(self.consumed)
                link(dve, c, dve.tensor_tensor(self.y[:, :], self.y[:, :], self.of(k.x, c), ALU.add))
                self.norm_begin(dve, c)
            if slot == 8:
                self.norm_end(dve, c)
        if slot == SLOTS - 1:
            assert self.n_links <= LINKS[layer]
            if self.n_links < LINKS[layer]:
                dve.sem_inc(self.step, LINKS[layer] - self.n_links)


def node_stage(nc, k, layer):
    with stage(nc) as (ctx, sem):
        work = NodeWork(nc, k, ctx, sem, layer)
        block = ctx.enter_context(nc.Block())

        @block.tensor
        def _(pe):
            work.tensor_start(pe)
            with pe.Fori(0, NCH - 1) as c:
                for u in range(SLOTS):
                    work.tensor(pe, c, u)
            for u in range(SLOTS):
                work.tensor(pe, NCH - 1, u)

        @block.scalar
        def _(act):
            work.scalar_start(act)
            with act.Fori(0, NCH - 1) as c:
                for u in range(SLOTS):
                    work.scalar(act, c, u)
            for u in range(SLOTS):
                work.scalar(act, NCH - 1, u)
            work.scalar_end(act)

        @block.vector
        def _(dve):
            work.vector_start(dve)
            with dve.Fori(0, NCH - 1) as c:
                for u in range(SLOTS):
                    work.vector(dve, c, u)
            for u in range(SLOTS):
                work.vector(dve, NCH - 1, u)


def batch_norm_stage(nc, k):
    with stage(nc) as (ctx, sem):
        step, act_done, pe_done, stored = sem("n_step"), sem("n_act"), sem("n_pe"), sem("n_stored")
        staged, product, centred, squared, var_ready, std_ready, result, go = (
            sem("n_staged"), sem("n_product"), sem("n_centred"), sem("n_squared"), sem("n_var_ready"),
            sem("n_std_ready"), sem("n_result"), sem("n_go"))
        summed, inverted = sem("n_summed"), sem("n_inverted")
        ps = psum(nc, ctx, "n_ps")
        ps_rows = [psum(nc, ctx, f"n_ps_rows{b}") for b in range(ROUND)]
        s0, s1, s2 = k.small
        u, mean_of, n_mean, dist = (c[:, :] for c in k.chunk)
        mean, scale, mixer = s0[:, 0:D], s1[:, 0:D], s2[0:D, 0:D]
        shift, var = s2[:, D:2 * D], s0[:, D:2 * D]
        hT = [k.w[0:D + 1, b * CF:(b + 1) * CF] for b in range(ROUND)]
        assert 2 * ROUND == NCH and ROUND * CF <= NT * D and 3 * NT <= CW and ROUND + 1 <= 8
        t3 = lambda t: t.rearrange("p (t f) -> p t f", f=D)
        last = slice((CT - 1) * D, CT * D)
        block = ctx.enter_context(nc.Block())
        marks = {}
        chunk = lambda t, c: t[:, bass.ds(c * CW, CW)] if not isinstance(c, int) else t[:, c * CW:(c + 1) * CW]
        tiles = lambda t, c: t[:, bass.ds(c * CT, CT)] if not isinstance(c, int) else t[:, c * CT:(c + 1) * CT]
        variance, deviation, inverse = (k.chunk[3][:, i * NT:(i + 1) * NT] for i in range(3))
        square = k.h

        @block.vector
        def _(dve):
            n = [0]

            def link(ins_, name=None):
                n[0] += 1
                ins_.then_inc(step, 1)
                dve.wait_ge(step, n[0])
                if name:
                    marks[name] = n[0]

            dve.memset(k.w[D:D + 1, :], 1.0)
            link(dve.tensor_scalar(u, k.sums[:, :], 1.0 / NCH, None, ALU.mult))
            link(dve.tensor_scalar(u[:, last], k.sums[:, last], k.lane_n[:, 1:2], None, ALU.mult))
            link(dve.tensor_tensor(mean_of, k.base, u, ALU.add))
            link(dve.tensor_scalar(n_mean, mean_of, float(NCH), None, ALU.mult))
            link(dve.tensor_scalar(n_mean[:, last], mean_of[:, last], k.lane_n[:, 0:1], None, ALU.mult))
            link(dve.tensor_reduce(s2[:, 0:D], n_mean.rearrange("p (t f) -> p f t", f=D), AX.X, ALU.add), "sums")
            link(dve.tensor_tensor(u, u, k.sums[:, :], ALU.mult))
            link(dve.tensor_tensor(u, k.squares, u, ALU.subtract))
            dve.wait_ge(pe_done, 1)
            link(dve.tensor_scalar(mean, ps[:, 0:D], 1.0 / N, None, ALU.mult))
            link(dve.tensor_tensor(t3(dist), t3(mean_of), over_tiles(mean, CT), ALU.subtract))
            link(dve.tensor_tensor(dist, dist, dist, ALU.mult))
            link(dve.tensor_scalar(n_mean, dist, float(NCH), None, ALU.mult))
            link(dve.tensor_scalar(n_mean[:, last], dist[:, last], k.lane_n[:, 0:1], None, ALU.mult))
            link(dve.tensor_tensor(u, u, n_mean, ALU.add))
            link(dve.tensor_reduce(s2[:, 0:D], u.rearrange("p (t f) -> p f t", f=D), AX.X, ALU.add), "squares")
            dve.wait_ge(pe_done, 2)
            link(dve.tensor_scalar(var, ps[:, D:2 * D], 1.0 / N, BN_EPS, ALU.mult, ALU.add), "var")
            dve.wait_ge(act_done, 1)
            link(dve.reciprocal(scale, s1[:, D:2 * D]))
            link(dve.tensor_tensor(scale, scale, k.gamma[:, :], ALU.mult))
            link(dve.tensor_tensor(mixer, k.ident[0:D, 0:D], scale[0:D, :], ALU.mult), "scales")
            link(dve.tensor_tensor(shift, mean, scale, ALU.mult))
            link(dve.tensor_reduce(k.stat[0][:, 0:1], shift, AX.X, ALU.add))
            link(dve.tensor_scalar(k.stat[0][:, 0:1], k.stat[0][:, 0:1], 1.0 / D, None, ALU.mult))
            link(dve.tensor_scalar(shift, shift, -1.0, k.stat[0][:, 0:1], ALU.mult, ALU.add))
            dve.wait_ge(pe_done, 3)
            dve.tensor_copy(s2[D:D + 1, 0:D], shift[D:D + 1, :])
            link(dve.tensor_copy(mixer, ps[0:D, 2 * D:3 * D]), "mixer")

            def centre(c, b):
                dve.wait_ge(product, c + ROUND + 1)
                dve.tensor_tensor(chunk(k.y, c), ps_rows[b][:, 0:CW], chunk(k.y, c), ALU.add).then_inc(centred, 1)

            def spread(c):
                dve.wait_ge(squared, c + 1)
                dve.tensor_reduce(tiles(variance, c), t3(chunk(square, c)), AX.X, ALU.add).then_inc(summed, 1)
                dve.wait_ge(summed, c + 1)
                dve.tensor_scalar(tiles(variance, c), tiles(variance, c), 1.0 / D, LN_EPS, ALU.mult, ALU.add
                                  ).then_inc(var_ready, 1)

            def divide(c):
                dve.wait_ge(std_ready, c + 1)
                dve.reciprocal(tiles(inverse, c), tiles(deviation, c)).then_inc(inverted, 1)
                dve.wait_ge(inverted, c + 1)
                dve.tensor_tensor(t3(chunk(k.x, c)), t3(chunk(k.y, c)), over_features(tiles(inverse, c), CT),
                                  ALU.mult).then_inc(result, 1)

            with dve.Fori(0, 2) as i:
                for b in range(ROUND + 2):
                    if b < ROUND:
                        centre(i * ROUND + b, b)
                    if 1 <= b <= ROUND:
                        spread(i * ROUND + (b - 1))
                    if b >= 2:
                        divide(i * ROUND + (b - 2))

        @block.scalar
        def _(act):
            act.wait_ge(step, marks["var"])
            act.activation(s1[:, D:2 * D], var, ACT.Sqrt).then_inc(act_done, 1)

            def squares(c):
                act.wait_ge(centred, c + ROUND + 1)
                act.activation(chunk(square, c), chunk(k.y, c), ACT.Square).then_inc(squared, 1)

            def root(c):
                act.wait_ge(var_ready, c + 1)
                act.activation(tiles(deviation, c), tiles(variance, c), ACT.Sqrt).then_inc(std_ready, 1)

            with act.Fori(0, 2) as i:
                for b in range(ROUND + 1):
                    if b < ROUND:
                        squares(i * ROUND + b)
                    if b >= 1:
                        root(i * ROUND + (b - 1))

        @block.gpsimd
        def _(pool):
            with pool.Fori(0, 2) as i:
                for b in range(ROUND):
                    pool.wait_ge(product, i * ROUND + (b + 1))
                    pool.tensor_copy(hT[b][0:D, :], k.acc[0:D, bass.ds((i * ROUND + b) * CF, CF)]).then_inc(staged, 1)

        @block.tensor
        def _(pe):
            pe.wait_ge(step, marks["sums"])
            pe.matmul(ps[:, 0:D], k.ones[:, :], s2[:, 0:D], start=True, stop=True).then_inc(pe_done, 1)
            pe.wait_ge(step, marks["squares"])
            pe.matmul(ps[:, D:2 * D], k.ones[:, :], s2[:, 0:D], start=True, stop=True).then_inc(pe_done, 1)
            pe.wait_ge(step, marks["scales"])
            pe.matmul(ps[0:D, 2 * D:3 * D], mixer, k.centre[:, :], start=True, stop=True).then_inc(pe_done, 1)
            pe.wait_ge(step, marks["mixer"])
            with pe.Fori(0, 2) as i:
                for b in range(ROUND):
                    pe.wait_ge(staged, i * ROUND + (b + 1))
                    pe.wait_ge(centred, i * ROUND + (b + 1))
                    pe.sem_inc(go)
                    for j in range(CT):
                        mm = pe.matmul(ps_rows[b][:, j * D:(j + 1) * D], hT[b][:, j * P:(j + 1) * P],
                                       s2[0:D + 1, 0:D], start=True, stop=True, skip_group_check=True)
                    mm.then_inc(product, 1)

        @block.sync
        def _(sp):
            sp.sem_inc(centred, ROUND)
            sp.sem_inc(product, ROUND)
            with sp.Fori(0, NCH) as c:
                sp.wait_ge(result, c + 1)
                sp.sem_inc(go)
                sp.dma_start(k.tab["x1"][bass.ds(c * CF, CF), :].rearrange("(t p) f -> p t f", p=P),
                             t3(chunk(k.x, c))).then_inc(stored, 16)
            sp.wait_ge(stored, 16 * NCH)


def layer_of(nc, k, fast, table, layer):
    with nc.If(fast):
        fast_pass(nc, k, table, layer)
    with nc.Else():
        if layer == "mean":
            zero_stage(nc, k)
            degree_stage(nc, k)
        general_pass(nc, k, table, "dst", layer == "edge")
        gather_partials(nc, k)
        node_stage(nc, k, layer)


def build(nc, ins, out):
    with ExitStack() as ctx:
        k = alloc(nc, ctx, ins)
        k.out = out
        setup_stage(nc, k)
        fast = nc.values_load(k.flag[0:1, 0:1], min_val=0, max_val=1,
                              skip_runtime_bounds_check_because="it is the result of a comparison")
        layer_of(nc, k, fast, ins["x"], "mean")
        batch_norm_stage(nc, k)
        layer_of(nc, k, fast, k.tab["x1"], "sage1")
        layer_of(nc, k, fast, k.tab["h1"], "sage2")
        layer_of(nc, k, fast, k.tab["pre"], "edge")
        with nc.If(fast):
            reverse_pass(nc, k, k.tab["x3"])
            fast_pass(nc, k, k.tab["x3"], "both")
        with nc.Else():
            general_pass(nc, k, k.tab["x3"], "dst")
            gather_partials(nc, k)
            general_pass(nc, k, k.tab["x3"], "src")
            node_stage(nc, k, "both")


def kernel(x, src, dst, edge_attr_64, L0_gnn_W, L0_gnn_b, L0_gnn_gamma, L0_gnn_beta, L1_gnn_w1_l, L1_gnn_b1,
           L1_gnn_w1_r, L1_gnn_w2_l, L1_gnn_b2, L1_gnn_w2_r, L1_gnn_w_lin, L1_gnn_b_lin, L2_gnn_W1, L2_gnn_b1,
           L2_gnn_W2, L2_gnn_b2, L2_gnn_W3, L2_gnn_b3, L3_gnn_W):
    import concourse.bacc as bacc
    from concourse.bass_utils import run_bass_kernel_spmd

    def padded(a, rows, fill=0):
        return np.concatenate([a, np.full((rows - a.shape[0],) + a.shape[1:], fill, a.dtype)])

    def pieces(a):
        return np.asarray(a)

    src, dst = padded(pieces(src), EP, N), padded(pieces(dst), EP, N)
    s3, d3 = src.reshape(NG, GROUP, P), dst.reshape(NG, GROUP, P)
    attr = padded(pieces(edge_attr_64), EP).reshape(EP // (2 * P), 2, P, D)
    l0, l3, e1, e3 = (pieces(a) for a in (L0_gnn_W, L3_gnn_W, L2_gnn_W1, L2_gnn_W3))
    t = lambda a: pieces(a).T
    mats = {"W0_self": l0[:D], "W0_agg": l0[D:], "W1_agg": t(L1_gnn_w1_l), "W1_self": t(L1_gnn_w1_r),
            "W2_agg": t(L1_gnn_w2_l), "W2_self": t(L1_gnn_w2_r), "Wlin": t(L1_gnn_w_lin),
            "We_node": e1[:D], "We_edge": e1[D:], "We_out": pieces(L2_gnn_W2), "Wn_self": e3[:D],
            "Wn_agg": e3[D:], "W3_fwd": t(l3[:, :D]), "W3_bwd": t(l3[:, D:])}
    rows = {"b0": L0_gnn_b, "b1": L1_gnn_b1, "b2": L1_gnn_b2, "blin": L1_gnn_b_lin, "be": L2_gnn_b1,
            "be2": L2_gnn_b2, "bn": L2_gnn_b3, "gamma": L0_gnn_gamma, "beta": L0_gnn_beta,
            "zero": np.zeros(D, np.float32)}
    arrays = {
        "x": padded(pieces(x), NP),
        "cols": np.concatenate([s3.transpose(0, 2, 1), d3.transpose(0, 2, 1)], axis=2),
        "dst_all": d3.transpose(2, 0, 1).reshape(P, NG * GROUP),
        "first": d3[:, 0, 0].reshape(1, NG),
        "rows_of": np.stack([src.reshape(NG, GROUP * P), dst.reshape(NG, GROUP * P)], axis=1),
        "attr": attr.transpose(1, 3, 0, 2).reshape(P, EP // 2),
        "mats": np.concatenate([mats[m] for m in MATS], axis=1),
        "rows": np.stack([pieces(rows[r]) for r in ROWS])[None],
        "be2_col": pieces(L2_gnn_b2).reshape(D, 1),
    }
    nc = bacc.Bacc("TRN2", target_bir_lowering=False, num_devices=1)
    ins, feed = {}, {}
    for name, a in arrays.items():
        feed[f"in_{name}"] = np.ascontiguousarray(a)
        ins[name] = nc.dram_tensor(f"in_{name}", a.shape, mybir.dt.from_np(a.dtype), kind="ExternalInput").ap()
    out = nc.dram_tensor("out", (N, D), F32, kind="ExternalOutput").ap()
    build(nc, ins, out)
    return run_bass_kernel_spmd(nc, [feed], core_ids=[0]).results[0]["out"]
```
